# Optimizing a Trainium2 kernel written in Bass

```python
import numpy as np
import jax
import jax.numpy as jnp

def _softmax(x, axis=-1):
    return jax.nn.softmax(x, axis=axis)

def _gelu(x):
    return jax.nn.gelu(x, approximate=True)

def _silu(x):
    return jax.nn.silu(x)

def _sigmoid(x):
    return jax.nn.sigmoid(x)

def _layernorm(x, axis=-1, eps=1e-05):
    m = jnp.mean(x, axis=axis, keepdims=True)
    v = jnp.var(x, axis=axis, keepdims=True)
    return (x - m) / jnp.sqrt(v + eps)

def _scatter_add(tgt, idx, src, axis=0):
    return tgt.at[idx].add(src)

def _segment_sum(src, seg, n):
    return jax.ops.segment_sum(src, seg, n)
kernel_name = 'mk_seq_postln_d2_jaxref_r8_6aff57'

def setup_inputs(seed: int=0):
    np.random.seed(seed)
    _w = jnp.asarray

    def _L0_attn_setup():
        import jax, jax.numpy as jnp
        import numpy as np
        NF4 = jnp.array([-1.0, -0.6961928009986877, -0.5250730514526367, -0.39491748809814453, -0.28444138169288635, -0.18477343022823334, -0.09105003625154495, 0.0, 0.07958029955625534, 0.16093020141124725, 0.24611230194568634, 0.33791524171829224, 0.44070982933044434, 0.5626170039176941, 0.7229568362236023, 1.0], dtype=jnp.float32)
        BLOCK = 64

        def _dequant(codes, scales):
            w = NF4[codes]
            O, I = w.shape
            w = w.reshape(O, I // BLOCK, BLOCK) * scales[:, :, None]
            return w.reshape(O, I)

        def _lin_lora(x, W, A, B):
            base = jnp.einsum('bsh,oh->bso', x, W)
            lora = jnp.einsum('bsr,or->bso', jnp.einsum('bsh,rh->bsr', x, A), B)
            return base + lora
        H, I, R, BT, S = (512, 1792, 16, 2, 256)
        key = jax.random.key(seed)
        ks = jax.random.split(key, 12)
        x = jax.random.normal(ks[0], (BT, S, H), jnp.float32)
        codes_attn = jax.random.randint(ks[1], (4, H, H), 0, 16, jnp.int32)
        scales_attn = jax.random.uniform(ks[2], (4, H, H // BLOCK), jnp.float32) * 0.02
        codes_gu = jax.random.randint(ks[3], (2, I, H), 0, 16, jnp.int32)
        scales_gu = jax.random.uniform(ks[4], (2, I, H // BLOCK), jnp.float32) * 0.02
        codes_down = jax.random.randint(ks[5], (H, I), 0, 16, jnp.int32)
        scales_down = jax.random.uniform(ks[6], (H, I // BLOCK), jnp.float32) * 0.02
        lora_A_h = jax.random.normal(ks[7], (6, R, H), jnp.float32) * 0.02
        lora_A_down = jax.random.normal(ks[8], (R, I), jnp.float32) * 0.02
        lora_B_attn = jax.random.normal(ks[9], (4, H, R), jnp.float32) * 0.02
        lora_B_gu = jax.random.normal(ks[10], (2, I, R), jnp.float32) * 0.02
        lora_B_down = jax.random.normal(ks[11], (H, R), jnp.float32) * 0.02
        return dict(x=x, codes_attn=codes_attn, scales_attn=scales_attn, codes_gu=codes_gu, scales_gu=scales_gu, codes_down=codes_down, scales_down=scales_down, lora_A_h=lora_A_h, lora_A_down=lora_A_down, lora_B_attn=lora_B_attn, lora_B_gu=lora_B_gu, lora_B_down=lora_B_down)
    _L0_attn_in = _L0_attn_setup()

    def _L0_ffn_setup():
        import jax, jax.numpy as jnp
        import numpy as np
        NF4 = jnp.array([-1.0, -0.6961928009986877, -0.5250730514526367, -0.39491748809814453, -0.28444138169288635, -0.18477343022823334, -0.09105003625154495, 0.0, 0.07958029955625534, 0.16093020141124725, 0.24611230194568634, 0.33791524171829224, 0.44070982933044434, 0.5626170039176941, 0.7229568362236023, 1.0], dtype=jnp.float32)
        BLOCK = 64
        SCALING = 16.0 / 64.0
        key = jax.random.key(seed)
        k0, k1, k2, k3, k4 = jax.random.split(key, 5)
        B, S, D_in, D_out, r = (4, 256, 512, 512, 64)
        x = jax.random.normal(k0, (B, S, D_in), dtype=jnp.float32)
        codes = jax.random.randint(k1, (D_out, D_in), 0, 16, dtype=jnp.int32)
        absmax = jax.random.uniform(k2, (D_out, D_in // BLOCK), minval=0.01, maxval=1.0, dtype=jnp.float32)
        lora_A = jax.random.normal(k3, (r, D_in), dtype=jnp.float32) * 0.02
        lora_B = jax.random.normal(k4, (D_out, r), dtype=jnp.float32) * 0.02
        return {'x': x, 'codes': codes, 'absmax': absmax, 'lora_A': lora_A, 'lora_B': lora_B}
    _L0_ffn_in = _L0_ffn_setup()

    def _L1_attn_setup():
        import jax, jax.numpy as jnp
        import numpy as np
        H = 512
        D = H // 4
        key = jax.random.key(seed)
        k1, k2, k3, k4, k5 = jax.random.split(key, 5)
        x = jax.random.normal(k1, (4, 512, H), dtype=jnp.float32)
        s_in = 1.0 / np.sqrt(H)
        Wqkv = jax.random.normal(k2, (H, 3 * D), dtype=jnp.float32) * s_in
        bqkv = jax.random.normal(k3, (3 * D,), dtype=jnp.float32) * 0.01
        Wo = jax.random.normal(k4, (D, H), dtype=jnp.float32) * (1.0 / np.sqrt(D))
        bo = jax.random.normal(k5, (H,), dtype=jnp.float32) * 0.01
        return {'x': x, 'Wqkv': Wqkv, 'bqkv': bqkv, 'Wo': Wo, 'bo': bo}
    _L1_attn_in = _L1_attn_setup()

    def _L1_ffn_setup():
        import jax, jax.numpy as jnp
        import numpy as np
        BATCH, SEQ, D = (2, 256, 512)
        K, TOPK, RANK = (64, 16, 16)
        ALPHA = 32.0
        SCALING = ALPHA / RANK
        key = jax.random.key(seed)
        k1, k2, k3, k4 = jax.random.split(key, 4)
        x = jax.random.normal(k1, (BATCH, SEQ, D), dtype=jnp.float32)
        A = jax.random.normal(k2, (K, RANK, D), dtype=jnp.float32) * 0.02
        B = jax.random.normal(k3, (K, D, RANK), dtype=jnp.float32) * 0.02
        Wr = jax.random.normal(k4, (K, D), dtype=jnp.float32) * 0.02
        return {'x': x, 'A': A, 'B': B, 'Wr': Wr}
    _L1_ffn_in = _L1_ffn_setup()
    _d = {'L0_attn_x': _L0_attn_in['x'], 'L0_attn_codes_attn': _L0_attn_in['codes_attn'], 'L0_attn_scales_attn': _L0_attn_in['scales_attn'], 'L0_attn_codes_gu': _L0_attn_in['codes_gu'], 'L0_attn_scales_gu': _L0_attn_in['scales_gu'], 'L0_attn_codes_down': _L0_attn_in['codes_down'], 'L0_attn_scales_down': _L0_attn_in['scales_down'], 'L0_attn_lora_A_h': _L0_attn_in['lora_A_h'], 'L0_attn_lora_A_down': _L0_attn_in['lora_A_down'], 'L0_attn_lora_B_attn': _L0_attn_in['lora_B_attn'], 'L0_attn_lora_B_gu': _L0_attn_in['lora_B_gu'], 'L0_attn_lora_B_down': _L0_attn_in['lora_B_down'], 'L0_ffn_codes': _L0_ffn_in['codes'], 'L0_ffn_absmax': _L0_ffn_in['absmax'], 'L0_ffn_lora_A': _L0_ffn_in['lora_A'], 'L0_ffn_lora_B': _L0_ffn_in['lora_B'], 'L1_attn_Wqkv': _L1_attn_in['Wqkv'], 'L1_attn_bqkv': _L1_attn_in['bqkv'], 'L1_attn_Wo': _L1_attn_in['Wo'], 'L1_attn_bo': _L1_attn_in['bo'], 'L1_ffn_A': _L1_ffn_in['A'], 'L1_ffn_B': _L1_ffn_in['B'], 'L1_ffn_Wr': _L1_ffn_in['Wr']}
    _x0 = _d['L0_attn_x']
    _d['L0_attn_x'] = jax.random.normal(jax.random.fold_in(jax.random.key(seed), 1), (2, 512, 512), dtype=_x0.dtype)
    del _x0
    return _d

def reference(L0_attn_x, L0_attn_codes_attn, L0_attn_scales_attn, L0_attn_codes_gu, L0_attn_scales_gu, L0_attn_codes_down, L0_attn_scales_down, L0_attn_lora_A_h, L0_attn_lora_A_down, L0_attn_lora_B_attn, L0_attn_lora_B_gu, L0_attn_lora_B_down, L0_ffn_codes, L0_ffn_absmax, L0_ffn_lora_A, L0_ffn_lora_B, L1_attn_Wqkv, L1_attn_bqkv, L1_attn_Wo, L1_attn_bo, L1_ffn_A, L1_ffn_B, L1_ffn_Wr):

    def _L0_attn_ref(x, codes_attn, scales_attn, codes_gu, scales_gu, codes_down, scales_down, lora_A_h, lora_A_down, lora_B_attn, lora_B_gu, lora_B_down):
        import jax, jax.numpy as jnp
        import numpy as np
        NF4 = jnp.array([-1.0, -0.6961928009986877, -0.5250730514526367, -0.39491748809814453, -0.28444138169288635, -0.18477343022823334, -0.09105003625154495, 0.0, 0.07958029955625534, 0.16093020141124725, 0.24611230194568634, 0.33791524171829224, 0.44070982933044434, 0.5626170039176941, 0.7229568362236023, 1.0], dtype=jnp.float32)
        BLOCK = 64

        def _dequant(codes, scales):
            w = NF4[codes]
            O, I = w.shape
            w = w.reshape(O, I // BLOCK, BLOCK) * scales[:, :, None]
            return w.reshape(O, I)

        def _lin_lora(x, W, A, B):
            base = jnp.einsum('bsh,oh->bso', x, W)
            lora = jnp.einsum('bsr,or->bso', jnp.einsum('bsh,rh->bsr', x, A), B)
            return base + lora
        q = _lin_lora(x, _dequant(codes_attn[0], scales_attn[0]), lora_A_h[0], lora_B_attn[0])
        k = _lin_lora(x, _dequant(codes_attn[1], scales_attn[1]), lora_A_h[1], lora_B_attn[1])
        v = _lin_lora(x, _dequant(codes_attn[2], scales_attn[2]), lora_A_h[2], lora_B_attn[2])
        attn = (q + k + v) / 3.0
        o = _lin_lora(attn, _dequant(codes_attn[3], scales_attn[3]), lora_A_h[3], lora_B_attn[3])
        x1 = x + o
        g = _lin_lora(x1, _dequant(codes_gu[0], scales_gu[0]), lora_A_h[4], lora_B_gu[0])
        u = _lin_lora(x1, _dequant(codes_gu[1], scales_gu[1]), lora_A_h[5], lora_B_gu[1])
        h = jax.nn.silu(g) * u
        d = _lin_lora(h, _dequant(codes_down, scales_down), lora_A_down, lora_B_down)
        return x1 + d

    def _L0_ffn_ref(x, codes, absmax, lora_A, lora_B):
        import jax, jax.numpy as jnp
        import numpy as np
        NF4 = jnp.array([-1.0, -0.6961928009986877, -0.5250730514526367, -0.39491748809814453, -0.28444138169288635, -0.18477343022823334, -0.09105003625154495, 0.0, 0.07958029955625534, 0.16093020141124725, 0.24611230194568634, 0.33791524171829224, 0.44070982933044434, 0.5626170039176941, 0.7229568362236023, 1.0], dtype=jnp.float32)
        BLOCK = 64
        SCALING = 16.0 / 64.0
        D_out, D_in = codes.shape
        W = (NF4[codes].reshape(D_out, D_in // BLOCK, BLOCK) * absmax[:, :, None]).reshape(D_out, D_in)
        base = jnp.einsum('bsd,od->bso', x, W)
        lora = jnp.einsum('bsr,or->bso', jnp.einsum('bsd,rd->bsr', x, lora_A), lora_B) * SCALING
        return base + lora

    def _L1_attn_ref(x, Wqkv, bqkv, Wo, bo):
        import jax, jax.numpy as jnp
        import numpy as np
        H = 512
        D = H // 4
        B, S, C = x.shape
        d = C // 4
        qkv = jnp.einsum('bsc,cf->bsf', x, Wqkv) + bqkv
        qkv = qkv.reshape(B, S, 3, d)
        q, k, v = (qkv[:, :, 0], qkv[:, :, 1], qkv[:, :, 2])
        scale = 1.0 / jnp.sqrt(jnp.float32(d)).astype(x.dtype)
        attn = jnp.einsum('bqd,bkd->bqk', q, k) * scale
        attn = jax.nn.softmax(attn, axis=-1)
        out = jnp.einsum('bqk,bkd->bqd', attn, v)
        return jnp.einsum('bqd,dc->bqc', out, Wo) + bo

    def _L1_ffn_ref(x, A, B, Wr):
        import jax, jax.numpy as jnp
        import numpy as np
        BATCH, SEQ, D = (2, 256, 512)
        K, TOPK, RANK = (64, 16, 16)
        ALPHA = 32.0
        SCALING = ALPHA / RANK
        prefix = x.shape[:-1]
        xf = x.reshape(-1, x.shape[-1])
        N = xf.shape[0]
        scores = xf @ Wr.T
        top_vals, top_idx = jax.lax.top_k(scores, TOPK)
        gates = jax.nn.softmax(top_vals, axis=-1)
        G = jnp.zeros((N, K), xf.dtype).at[jnp.arange(N)[:, None], top_idx].set(gates)
        h = jnp.einsum('nd,krd->nkr', xf, A)
        out = jnp.einsum('nkr,kdr->nd', h * G[:, :, None], B)
        return (out * SCALING).reshape(*prefix, -1)
    x = L0_attn_x
    x = _layernorm(x + _L0_attn_ref(x, L0_attn_codes_attn, L0_attn_scales_attn, L0_attn_codes_gu, L0_attn_scales_gu, L0_attn_codes_down, L0_attn_scales_down, L0_attn_lora_A_h, L0_attn_lora_A_down, L0_attn_lora_B_attn, L0_attn_lora_B_gu, L0_attn_lora_B_down), axis=-1)
    x = _layernorm(x + _L0_ffn_ref(x, L0_ffn_codes, L0_ffn_absmax, L0_ffn_lora_A, L0_ffn_lora_B), axis=-1)
    x = _layernorm(x + _L1_attn_ref(x, L1_attn_Wqkv, L1_attn_bqkv, L1_attn_Wo, L1_attn_bo), axis=-1)
    x = _layernorm(x + _L1_ffn_ref(x, L1_ffn_A, L1_ffn_B, L1_ffn_Wr), axis=-1)
    return x

_drawn_inputs = setup_inputs


def setup_inputs(seed=0):
    import zlib

    import numpy as np

    out = dict(_drawn_inputs(seed))
    spreads = {}
    factors = {'L0_attn_scales_attn': 8.0,
     'L0_attn_scales_gu': 8.0,
     'L0_attn_scales_down': 8.0,
     'L0_attn_lora_A_h': 8.0,
     'L0_attn_lora_A_down': 8.0,
     'L0_attn_lora_B_attn': 8.0,
     'L0_attn_lora_B_gu': 8.0,
     'L0_attn_lora_B_down': 8.0,
     'L0_ffn_lora_A': 8.0,
     'L0_ffn_lora_B': 8.0,
     'L1_attn_bqkv': 5.074,
     'L1_attn_bo': 5.753,
     'L1_ffn_A': 3.037,
     'L1_ffn_B': 3.03,
     'L1_ffn_Wr': 3.456}
    for name, (base, spread) in spreads.items():
        noise = np.random.default_rng([zlib.crc32(name.encode()), seed]).standard_normal(out[name].shape)
        drawn = base * np.exp(spread * noise) if base else spread * noise
        out[name] = jnp.asarray(drawn.astype(out[name].dtype))
    for name, factor in factors.items():
        out[name] = (out[name] * factor).astype(out[name].dtype)
    return out
```

```python
from contextlib import ExitStack

import concourse.bass as bass
from concourse import mybir

P = 128
H = 512
KT = H // P
TOK = 1024
TT = TOK // P
SEQ = 512
NB = TOK // SEQ
TPB = SEQ // P
FF = 1792
NF = FF // P
QB = 64
RANK = 16
FFN_RANK = 64
HD = 128
EXPERTS, TOPK, ERANK = 64, 16, 16
ER = EXPERTS * ERANK
EPC = H // ERANK
LORA_SCALE = 16.0 / 64.0
EXPERT_SCALE = 32.0 / ERANK
EPS = 1e-5
ATTN_SCALE = float(HD) ** -0.5
TAKEN = -3.0e38

F32 = mybir.dt.float32
F32R = mybir.dt.float32r
I32 = mybir.dt.int32
ALU = mybir.AluOpType
ACT = mybir.ActivationFunctionType
AX_X = mybir.AxisListType.X

NF4 = [-1.0, -0.6961928009986877, -0.5250730514526367, -0.39491748809814453, -0.28444138169288635,
       -0.18477343022823334, -0.09105003625154495, 0.0, 0.07958029955625534, 0.16093020141124725,
       0.24611230194568634, 0.33791524171829224, 0.44070982933044434, 0.5626170039176941,
       0.7229568362236023, 1.0]


def line(sign, a, b):
    slope = sign * (NF4[b] - NF4[a]) / (b - a)
    return slope, sign * NF4[a] - slope * a


UPPER = [line(1, 8, 9), line(1, 10, 11), line(1, 12, 13), line(1, 14, 15)]
LOWER = [line(-1, 6, 5), line(-1, 4, 3), line(-1, 2, 1), (1.5 * (NF4[0] - NF4[1]), -NF4[0])]

GROUPS = [range(0, 4), range(4, 8), range(8, 11), range(11, 14)]


def chunk_list():
    chunks = [("o", k) for k in range(KT)]
    chunks += [(m, k) for k in range(KT) for m in ("q", "k", "v")]
    chunks += [("g", 0), ("u", 0), ("g", 1), ("u", 1), ("d", 0)]
    for f in range(1, NF):
        chunks += [("g", f + 1), ("u", f + 1)] if f + 1 < NF else []
        chunks += [("d", f)]
    return chunks + [("f", k) for k in range(KT)]


CHUNKS = chunk_list()
NJ = len(CHUNKS)
MERGED = [c for c in CHUNKS if c[0] in "ovdf"]
SPLIT = [c for c in CHUNKS if c[0] not in "qk"]
SCALED = [c for c in CHUNKS if c[0] not in "qkv"]
RING_CODES = 3
RING_W = 3
RING_PLANE = 3
RING_H = 5
RING_GU = 2
RING_LN = 4


def vector_order():
    order = []

    def lut(c):
        j = CHUNKS.index(c)
        order.append(("lut", c))
        if j and CHUNKS[j - 1] in SPLIT:
            order.append(("split", CHUNKS[j - 1]))

    for j in range(16):
        lut(CHUNKS[j])
    lut(("g", 0))
    order.extend(("m1", i) for i in range(2))
    order.extend(("xsplit", i) for i in range(2 * KT))
    order.extend(("m1", i) for i in range(2, KT))
    lut(("u", 0))
    order.extend(("x1", n) for n in range(2))
    lut(("g", 1))
    order.extend(("x1", n) for n in range(2, 4))
    lut(("u", 1))
    order.append(("bprep", 0))
    order.extend(("x1", n) for n in range(4, 8))
    order.extend(("p", b) for b in range(NB))
    for f in range(NF):
        luts = [("g", f + 1), ("u", f + 1)] if 1 <= f < NF - 1 else []
        due = [gi for gi in range(len(GROUPS) - 1) if GROUPS[gi][-1] + 1 == f - 1]
        downs = [("down", due[0], t) for t in range(TT)] if due else []
        for c in luts:
            order.extend(downs[:3])
            del downs[:3]
            lut(c)
        order.extend(downs)
        if f < NF - 1:
            order.append(("unit", 2 * f))
            lut(("d", f))
        else:
            lut(("d", f))
            order.append(("unit", 2 * f))
        order.append(("unit", 2 * f + 1))
    for k in range(KT):
        lut(("f", k))
    order.append(("split", CHUNKS[-1]))
    return order


def tensor_order():
    order = []
    for f in range(NF):
        order.append(("lora", ("d", f)))
        order += [("unit", 2 * f), ("unit", 2 * f + 1)]
        for gi in range(len(GROUPS) - 1):
            if GROUPS[gi][-1] + 1 == f:
                order += [("down", gi, t) for t in range(TT)]
    return order


def tail_order():
    order = []
    gi = len(GROUPS) - 1
    for r in range(TT + 6):
        if r < TT:
            order += [("down", gi, t) for t in range(2 * r, min(2 * r + 2, TT))]
            order.append(("stat", 0, r))
        if 0 <= r - 1 < TT:
            order.append(("norm", 0, r - 1))
        if 0 <= r - 2 < TT:
            order.append(("turn", 0, r - 2))
        if 0 <= r - 3 < TT:
            order.append(("ffn", r - 3))
            order.append(("stat", 1, r - 3))
        if 0 <= r - 4 < TT:
            order.append(("norm", 1, r - 4))
        if 0 <= r - 5 < TT:
            order.append(("turn", 1, r - 5))
    for b in range(NB):
        order += [("qkv", b), ("vturn", b)]
        order += [("s", b, 0), ("s", b, 1), ("pturn", b, 0), ("s", b, 2), ("pturn", b, 1), ("s", b, 3),
                  ("pturn", b, 2), ("pturn", b, 3), ("ot", b)]
        order += [("wo", TPB * b + i) for i in range(TPB)]
    for r in range(TT + 5):
        if r < TT:
            order.append(("stat", 2, r))
        if 0 <= r - 1 < TT:
            order.append(("norm", 2, r - 1))
        if 0 <= r - 2 < TT:
            order += [("turn", 2, r - 2), ("score", r - 2), ("h", r - 2)]
        if 0 <= r - 3 < TT:
            order += [("hturn", r - 3), ("mix", r - 3), ("stat", 3, r - 3)]
        if 0 <= r - 4 < TT:
            order.append(("norm", 3, r - 4))
    return order


def build(nc, codes, scales, scales_qkv, eye, xT, loA_o, loB_o, loA_qkv, loB_qkv, loA_gu, loB_gu,
          loA_d, loB_d, loA_f, loB_f, w_qkv, b_qkv, w_o, b_o, ex_A, ex_B, w_r, out):
    with ExitStack() as ctx:
        bn6 = ctx.enter_context(nc.sbuf_tensor("bn6", [P, RING_LN, 6], F32))
        mv = ctx.enter_context(nc.sbuf_tensor("mv", [P, RING_LN, 2], F32))
        veps = ctx.enter_context(nc.sbuf_tensor("veps", [P, RING_LN], F32))
        rstd = ctx.enter_context(nc.sbuf_tensor("rstd", [P, RING_LN], F32))
        neg_half = ctx.enter_context(nc.sbuf_tensor("neg_half", [P, 1], F32))
        base = (nc.sbuf_base + 63) // 64 * 64

        def at(name, kb, shape, dt=F32):
            return nc.alloc_sbuf_tensor_at(name, shape, dt, offset=base + int(kb * 1024))

        def sem(name):
            return ctx.enter_context(nc.semaphore(name))

        code = at("code", 0, [P, RING_CODES, 512], I32)
        scale = at("scale", 6, [P, RING_CODES, 512])
        half = at("half", 12, [P, 2, 512])
        halves = at("halves", 16, [P, 2, 2, 512])
        wf = at("wf", 24, [P, RING_W, 512])
        act_f = at("act_f", 30, [P, 2, 512])
        xs = at("xs", 34, [P, KT, TOK])
        x_hi = at("x_hi", 50, [P, KT, TOK], F32R)
        x_lo = at("x_lo", 66, [P, KT, TOK], F32R)
        m1_hi = at("m1_hi", 82, [P, KT, H], F32R)
        m1_lo = at("m1_lo", 90, [P, KT, H], F32R)
        h_hi = at("h_hi", 50, [P, RING_H, TOK], F32R)
        h_lo = at("h_lo", 70, [P, RING_H, TOK], F32R)
        rows = at("rows", 98, [P, TT, H])
        bgu_raw = at("bgu_raw", 98, [P, 2, FF])
        a4_raw = at("a4_raw", 112, [P, KT, P])
        wq_hi = at("wq_hi", 114, [P, KT, H], F32R)
        wq_lo = at("wq_lo", 122, [P, KT, H], F32R)
        wo_hi = at("wo_hi", 130, [P, KT, H], F32R)
        wo_lo = at("wo_lo", 138, [P, KT, H], F32R)
        wd_hi = at("wd_hi", 114, [P, RING_H, H], F32R)
        wd_lo = at("wd_lo", 124, [P, RING_H, H], F32R)
        bg4 = at("bg4", 134, [P, FF], F32R)
        p4 = at("p4", 141, [P, TOK], F32R)
        a4_hi = at("a4_hi", 205, [P, KT, P], F32R)
        x1_hi = at("x1_hi", 146, [P, KT, TOK], F32R)
        x1_lo = at("x1_lo", 162, [P, KT, TOK], F32R)
        gu_hi = at("gu_hi", 178, [P, RING_GU, 2, KT, P], F32R)
        gu_lo = at("gu_lo", 186, [P, RING_GU, 2, KT, P], F32R)
        la_o = at("la_o", 182, [RANK, 512])
        lb_o = at("lb_o", 184, [RANK, 512])
        la_qkv = at("la_qkv", 190, [3 * RANK, 512])
        lb_qkv = at("lb_qkv", 192, [3 * RANK, 512])
        bu4 = at("bu4", 194, [P, FF], F32R)
        la_d = at("la_d", 201, [P, 512])
        lb_d = at("lb_d", 203, [P, 512])
        a4_lo = at("a4_lo", 132, [P, KT, P], F32R)
        ident = at("ident", 207, [P, P])
        la_f = at("la_f", 141, [FFN_RANK, 512])
        lb_f = at("lb_f", 143, [FFN_RANK, 512])
        wff_hi = at("wff_hi", 146, [P, KT, H], F32R)
        wff_lo = at("wff_lo", 154, [P, KT, H], F32R)
        xa_hi = at("xa_hi", 0, [P, KT, TOK], F32R)
        xa_lo = at("xa_lo", 16, [P, KT, TOK], F32R)
        xb_hi = at("xb_hi", 50, [P, KT, TOK], F32R)
        xb_lo = at("xb_lo", 66, [P, KT, TOK], F32R)
        ea_raw = at("ea_raw", 34, [P, KT, ER])
        eb_raw = at("eb_raw", 34, [P, ER // P, H])
        ea_hi = at("ea_hi", 162, [P, KT, ER], F32R)
        ea_lo = at("ea_lo", 178, [P, KT, ER], F32R)
        eb_hi = at("eb_hi", 114, [P, ER // P, H], F32R)
        eb_lo = at("eb_lo", 130, [P, ER // P, H], F32R)
        wqkv_raw = at("wqkv_raw", 194, [P, KT, 3 * HD])
        wout_raw = at("wout_raw", 200, [P, H])
        br_qkv = at("br_qkv", 202, [P, 3])
        wqkv_hi = at("wqkv_hi", 82, [P, KT, 3 * HD], F32R)
        wqkv_lo = at("wqkv_lo", 88, [P, KT, 3 * HD], F32R)
        wout_hi = at("wout_hi", 94, [P, H], F32R)
        wout_lo = at("wout_lo", 96, [P, H], F32R)
        bo_rows = at("bo_rows", 32, [P, H])
        wr = at("wr", 203, [P, KT, EXPERTS])
        q_hi = at("q_hi", 0, [P, SEQ], F32R)
        q_lo = at("q_lo", 2, [P, SEQ], F32R)
        k_hi = at("k_hi", 4, [P, SEQ], F32R)
        k_lo = at("k_lo", 6, [P, SEQ], F32R)
        vT = at("vT", 8, [P, SEQ])
        v_hi = at("v_hi", 10, [P, TPB, HD], F32R)
        v_lo = at("v_lo", 12, [P, TPB, HD], F32R)
        oT_hi = at("oT_hi", 14, [P, SEQ], F32R)
        oT_lo = at("oT_lo", 16, [P, SEQ], F32R)
        prob = at("prob", 18, [P, 2, SEQ])
        pT_hi = at("pT_hi", 146, [P, TPB, SEQ], F32R)
        pT_lo = at("pT_lo", 154, [P, TPB, SEQ], F32R)
        hg = at("hg", 0, [P, 2, ER])
        hgT_hi = at("hgT_hi", 8, [P, 2, ER // P, P], F32R)
        hgT_lo = at("hgT_lo", 16, [P, 2, ER // P, P], F32R)
        left1 = at("left1", 24, [P, 2, EXPERTS])
        left2 = at("left2", 24.5, [P, 2, EXPERTS])
        gexp = at("gexp", 25, [P, 2, EXPERTS])
        gate = at("gate", 25.5, [P, 2, EXPERTS])
        sc_qkv = at("sc_qkv", 205, [P, 12, H // QB])
        rmax = at("rmax", 22, [P, TT])
        nmax = at("nmax", 22.25, [P, TT])
        rsum = at("rsum", 22.5, [P, TT])
        rinv = at("rinv", 22.75, [P, TT])
        top8 = at("top8", 26, [P, 2, 2, 8])
        gmax = at("gmax", 26.25, [P, 2])
        gsum = at("gsum", 26.5, [P, 2])
        ginv = at("ginv", 26.75, [P, 2])

        bank = [ctx.enter_context(nc.psum_tensor(f"bank{i}", [P, 512], F32)) for i in range(8)]
        plane = bank[0:RING_PLANE]
        lora_ps = bank[3]
        mm_ps = bank[4:8]
        turn_ps = bank[0:2]
        rows_ps = bank[4:6]
        qkv_ps = [bank[6], bank[7], bank[2]]
        s_ps = bank[6:8]
        oT_ps = bank[3]
        score_ps = bank[2:4]
        hid_ps = bank[6:8]

        codes_in = [sem(f"codes_in{i}") for i in range(RING_CODES)]
        scale_in = [sem(f"scale_in{i}") for i in range(RING_CODES)]
        sqkv_in = sem("sqkv_in")
        x_in = sem("x_in")
        eye_in = sem("eye_in")
        lora_in = sem("lora_in")
        lorad_in = sem("lorad_in")
        loraf_in = sem("loraf_in")
        bgu_in = sem("bgu_in")
        a4_in = sem("a4_in")
        plane_ready = sem("plane_ready")
        lut_step = sem("lut_step")
        diff_done = sem("diff_done")
        mult_done = sem("mult_done")
        weight_ready = sem("weight_ready")
        lora_ready = sem("lora_ready")
        lora_added = sem("lora_added")
        eye_mid = sem("eye_mid")
        hi_done = sem("hi_done")
        lo_done = sem("lo_done")
        xhi_done = sem("xhi_done")
        xlo_done = sem("xlo_done")
        m1_ready = sem("m1_ready")
        m1_third = sem("m1_third")
        m1_f = sem("m1_f")
        m1hi_done = sem("m1hi_done")
        m1lo_done = sem("m1lo_done")
        x1_ready = sem("x1_ready")
        x1hi_done = sem("x1hi_done")
        x1lo_done = sem("x1lo_done")
        xs_done = sem("xs_done")
        bprep_hi = sem("bprep_hi")
        bprep_done = sem("bprep_done")
        p_ready = sem("p_ready")
        phi_done = sem("phi_done")
        plo_done = sem("plo_done")
        gate_ready = sem("gate_ready")
        unit_ready = sem("unit_ready")
        silu_done = sem("silu_done")
        h_done = sem("h_done")
        hhi_done = sem("hhi_done")
        hlo_done = sem("hlo_done")
        down_ready = sem("down_ready")
        down_added = sem("down_added")
        neg_half_set = sem("neg_half_set")
        bn_step = sem("bn_step")
        var_ready = sem("var_ready")
        rstd_ready = sem("rstd_ready")
        norm_done = sem("norm_done")
        turn_ready = sem("turn_ready")
        turnhi_done = sem("turnhi_done")
        turnlo_done = sem("turnlo_done")
        ffn_ready = sem("ffn_ready")
        attn_in = sem("attn_in")
        bo_in = sem("bo_in")
        ea_in = sem("ea_in")
        eb_in = sem("eb_in")
        whi_done = sem("whi_done")
        wlo_done = sem("wlo_done")
        bo_added = sem("bo_added")
        qkv_ready = sem("qkv_ready")
        qkvhi_done = sem("qkvhi_done")
        qklo_done = sem("qklo_done")
        s_ready = sem("s_ready")
        max_done = sem("max_done")
        nmax_done = sem("nmax_done")
        exp_done = sem("exp_done")
        rinv_done = sem("rinv_done")
        oT_ready = sem("oT_ready")
        oThi_done = sem("oThi_done")
        oTlo_done = sem("oTlo_done")
        wo_ready = sem("wo_ready")
        res_done = sem("res_done")
        score_ready = sem("score_ready")
        top_step = sem("top_step")
        gexp_done = sem("gexp_done")
        gate_done = sem("gate_done")
        gsum_done = sem("gsum_done")
        ginv_done = sem("ginv_done")
        hid_ready = sem("hid_ready")
        hg_done = sem("hg_done")
        mix_ready = sem("mix_ready")
        out_done = sem("out_done")

        V, T = vector_order(), tensor_order()
        TAIL = tail_order()

        def split_no(c):
            return SPLIT.index(c) + 1

        def group_of(f):
            return next(i for i, g in enumerate(GROUPS) if f in g)

        def down_bank(gi, t):
            return mm_ps[t % 4] if gi < len(GROUPS) - 1 else mm_ps[2 + t % 2]

        def slot_free_down(f):
            return TT * (group_of(f - RING_H) + 1)

        turn_no = {}
        n = 0
        for x in TAIL:
            if x[0] in ("turn", "vturn", "pturn", "hturn"):
                turn_no[x] = n
                n += 2 if x[0] == "hturn" else 1
        rows_no = {x: i for i, x in enumerate(x for x in TAIL if x[0] in ("ffn", "wo", "mix"))}
        norm_no = {x[1:]: i for i, x in enumerate(x for x in TAIL if x[0] == "norm")}
        stat_no = {x[1:]: i for i, x in enumerate(x for x in TAIL if x[0] == "stat")}

        def rows_free(i):
            x = next(x for x, m in rows_no.items() if m == i - 2)
            if x[0] == "ffn":
                return norm_done, norm_no[(1, x[1])] + 1
            if x[0] == "wo":
                return res_done, x[1] + 1
            return res_done, TT + x[1] + 1

        def dest(c):
            kind, k = c
            if kind == "o":
                return wo_hi[:, k, :], wo_lo[:, k, :]
            if kind == "v":
                return wq_hi[:, k, :], wq_lo[:, k, :]
            if kind in "gu":
                g = "gu".index(kind)
                return gu_hi[:, k % RING_GU, g, :, :], gu_lo[:, k % RING_GU, g, :, :]
            if kind == "d":
                return wd_hi[:, k % RING_H, :], wd_lo[:, k % RING_H, :]
            return wff_hi[:, k, :], wff_lo[:, k, :]

        def shaped(c, w):
            return w.rearrange("p (k o) -> p k o", k=KT) if c[0] in "gu" else w

        def late_weights():
            pieces = []
            for k in range(KT):
                for h in range(ER // 512):
                    cut = slice(h * 512, (h + 1) * 512)
                    pieces.append((ea_raw[:, k, cut], ea_hi[:, k, cut], ea_lo[:, k, cut], ea_in, 16))
            for k in range(KT):
                pieces.append((wqkv_raw[:, k, :], wqkv_hi[:, k, :], wqkv_lo[:, k, :], attn_in, 64))
            pieces.append((wout_raw[:, :], wout_hi[:, :], wout_lo[:, :], attn_in, 64))
            for m in range(ER // P):
                pieces.append((eb_raw[:, m, :], eb_hi[:, m, :], eb_lo[:, m, :], eb_in, 16))
            return pieces

        N_EA, N_ATTN = KT * (ER // 512), KT + 1

        late_at = {None: range(N_EA), ("turn", 0, 3): range(N_EA, N_EA + N_ATTN),
                   ("turn", 1, 2): range(N_EA + N_ATTN, len(late_weights()))}

        block = ctx.enter_context(nc.Block())

        @block.sync
        def _(sp):
            for j, c in enumerate(CHUNKS):
                s = j % RING_CODES
                if j >= RING_CODES:
                    sp.wait_ge(lut_step, 6 * (j - RING_CODES + 1))
                sp.dma_start(code[:, s, :], codes[j]).then_inc(codes_in[s], 16)
                if c in SCALED:
                    i = SCALED.index(c)
                    if i >= RING_CODES:
                        before = CHUNKS.index(SCALED[i - RING_CODES])
                        sp.wait_ge(weight_ready, before + 1)
                    src = scales[i].unsqueeze(1).to_broadcast([2, QB, 512])
                    for g in range(2):
                        sp.dma_start(scale[g * QB:(g + 1) * QB, i % RING_CODES, :],
                                     src[g]).then_inc(scale_in[i % RING_CODES], 16)
            sp.wait_ge(unit_ready, 2 * NF)
            sp.dma_start(la_f[:, :], loA_f).then_inc(loraf_in, 16)
            sp.dma_start(lb_f[:, :], loB_f).then_inc(loraf_in, 16)
            sp.wait_ge(down_ready, TT)
            sp.dma_start(ea_raw[:, :, :], ex_A).then_inc(ea_in, 16)
            sp.wait_ge(lora_ready, MERGED.index(("d", NF - 1)) + 1)
            sp.dma_start(wqkv_raw[:, :, :], w_qkv).then_inc(attn_in, 16)
            sp.dma_start(wout_raw[:, :], w_o).then_inc(attn_in, 16)
            sp.dma_start(br_qkv[:, :], b_qkv).then_inc(attn_in, 16)
            sp.dma_start(wr[:, :, :], w_r).then_inc(attn_in, 16)
            sp.wait_ge(hhi_done, 2 * NF)
            sp.wait_ge(hlo_done, 2 * NF)
            sp.dma_start(bo_rows[:, :], b_o.to_broadcast([P, H])).then_inc(bo_in, 16)
            sp.wait_ge(whi_done, N_EA)
            sp.wait_ge(wlo_done, N_EA)
            sp.dma_start(eb_raw[:, :, :], ex_B).then_inc(eb_in, 16)
            for t in range(TT):
                sp.wait_ge(norm_done, norm_no[(3, t)] + 1)
                sp.dma_start(out[t * P:(t + 1) * P, :], rows[:, t, :]).then_inc(out_done, 16)
            sp.wait_ge(out_done, 16 * TT)

        @block.gpsimd
        def _(pool):
            pool.memset(neg_half[:, :], -0.5).then_inc(neg_half_set, 1)
            mults = 0
            for item in V:
                kind = item[0]
                if kind == "lut":
                    c = item[1]
                    j = CHUNKS.index(c)
                    w = wf[:, j % RING_W, :]
                    pool.wait_ge(lut_step, 6 * (j + 1))
                    if j >= RING_W:
                        before = [x for x in CHUNKS[:j - RING_W + 1] if x in SPLIT]
                        if before:
                            pool.wait_ge(lo_done, split_no(before[-1]))
                        pool.wait_ge(weight_ready, j)
                    pool.tensor_tensor(w, halves[:, j % 2, 0, :], halves[:, j % 2, 1, :],
                                       ALU.subtract).then_inc(diff_done, 1)
                    pool.wait_ge(diff_done, j + 1)
                    done = mult_done if c[0] in "kv" else weight_ready
                    mults += c[0] in "kv"
                    if c in SCALED:
                        i = SCALED.index(c)
                        pool.wait_ge(scale_in[i % RING_CODES], 32 * (i // RING_CODES + 1))
                        pool.tensor_tensor(w, w, scale[:, i % RING_CODES, :], ALU.mult).then_inc(done, 1)
                    else:
                        pool.wait_ge(sqkv_in, 16)
                        wv = w.rearrange("p (b e) -> p b e", e=QB)
                        sv = sc_qkv[:, "qkv".index(c[0]) * KT + c[1], :].unsqueeze(2)
                        pool.tensor_tensor(wv, wv, sv.to_broadcast([P, H // QB, QB]), ALU.mult)\
                            .then_inc(done, 1)
                    if c[0] in "kv":
                        pool.wait_ge(mult_done, mults)
                        pool.wait_ge(weight_ready, j)
                        pool.tensor_tensor(w, w, wf[:, (j - 1) % RING_W, :], ALU.add)\
                            .then_inc(weight_ready, 1)
                elif kind == "split":
                    c = item[1]
                    hi, lo = dest(c)
                    pool.wait_ge(hi_done, split_no(c))
                    w = wf[:, CHUNKS.index(c) % RING_W, :]
                    pool.tensor_tensor(lo, shaped(c, w), hi.bitcast(F32), ALU.subtract).then_inc(lo_done, 1)
            def late(item):
                for n in late_at.get(item, ()):
                    raw, hi, lo, _, _ = late_weights()[n]
                    pool.wait_ge(whi_done, n + 1)
                    pool.tensor_tensor(lo, raw, hi.bitcast(F32), ALU.subtract).then_inc(wlo_done, 1)

            late(None)
            for item in TAIL:
                if item[0] == "stat":
                    i = stat_no[item[1:]]
                    pool.wait_ge(neg_half_set, 1)
                    pool.wait_ge(var_ready, i + 1)
                    s = i % RING_LN
                    if i >= RING_LN:
                        pool.wait_ge(norm_done, i - RING_LN + 1)
                    pool.tensor_tensor(rstd[:, s:s + 1], veps[:, s:s + 1], neg_half[:, :], ALU.pow)\
                        .then_inc(rstd_ready, 1)
                elif item[0] == "turn" and item[1] == 1:
                    t = item[2]
                    pool.wait_ge(bo_in, 16)
                    pool.wait_ge(turn_ready, turn_no[item] + 1)
                    pool.tensor_tensor(rows[:, t, :], rows[:, t, :], bo_rows[:, :], ALU.add)\
                        .then_inc(bo_added, 1)
                late(item)

        @block.scalar
        def _(act):
            act.dma_start(sc_qkv[:, :, :], scales_qkv).then_inc(sqkv_in, 16)
            act.dma_start(ident[:, :], eye).then_inc(eye_in, 16)
            act.dma_start(la_o[:, :], loA_o).then_inc(lora_in, 16)
            act.dma_start(lb_o[:, :], loB_o).then_inc(lora_in, 16)
            act.dma_start(la_qkv[:, :], loA_qkv).then_inc(lora_in, 16)
            act.dma_start(lb_qkv[:, :], loB_qkv).then_inc(lora_in, 16)
            act.dma_start(xs[:, :, :], xT).then_inc(x_in, 16)
            act.dma_start(la_d[:, :], loA_d).then_inc(lorad_in, 16)
            act.dma_start(lb_d[:, :], loB_d).then_inc(lorad_in, 16)
            act.dma_start(bgu_raw[:, :, :], loB_gu).then_inc(bgu_in, 16)
            act.dma_start(a4_raw[:, :, :], loA_gu).then_inc(a4_in, 16)

            def copy(dst, src, done):
                nc.scalar.activation(dst, src, ACT.Copy).then_inc(done, 1)

            for item in V:
                kind = item[0]
                if kind == "lut":
                    c = item[1]
                    j = CHUNKS.index(c)
                    src = code[:, j % RING_CODES, :]
                    act.wait_ge(codes_in[j % RING_CODES], 16 * (j // RING_CODES + 1))
                    steps = [(h[2][0], h[2][1] - h[3][1], ACT.Identity) for h in (UPPER, LOWER)]
                    steps += [(h[0][0], h[0][1], ACT.Relu) for h in (UPPER, LOWER)]
                    steps += [(h[1][0], h[1][1], ACT.Identity) for h in (UPPER, LOWER)]
                    for i, (slope, start, func) in enumerate(steps):
                        m = 6 * j + i
                        if m >= RING_PLANE:
                            act.wait_ge(lut_step, m - RING_PLANE + 1)
                        nc.scalar.activation(plane[m % RING_PLANE][:, :], src, func, bias=float(start),
                                             scale=float(slope)).then_inc(plane_ready, 1)
                elif kind == "split":
                    c = item[1]
                    j = CHUNKS.index(c)
                    hi, _ = dest(c)
                    act.wait_ge(weight_ready, j + 1)
                    if c in MERGED:
                        act.wait_ge(lora_added, MERGED.index(c) + 1)
                    if c[0] in "gu" and c[1] == 1:
                        act.wait_ge(lora_ready, 2 * KT)
                    if c[0] in "gu" and c[1] >= RING_GU:
                        act.wait_ge(unit_ready, 2 * (c[1] - RING_GU) + 2)
                    if c[0] == "d" and c[1] == 0:
                        act.wait_ge(m1_ready, KT)
                    if c[0] == "d" and c[1] == RING_H - 1:
                        act.wait_ge(p_ready, NB)
                    if c[0] == "d" and c[1] >= RING_H:
                        act.wait_ge(down_ready, slot_free_down(c[1]))
                    if c[0] == "f":
                        act.wait_ge(unit_ready, 2 * NF)
                    copy(hi, shaped(c, wf[:, j % RING_W, :]), hi_done)
                elif kind == "xsplit":
                    k, b = item[1] // NB, item[1] % NB
                    act.wait_ge(x_in, 16)
                    copy(x_hi[:, k, b * SEQ:(b + 1) * SEQ], xs[:, k, b * SEQ:(b + 1) * SEQ], xhi_done)
                elif kind == "m1":
                    act.wait_ge(m1_f, item[1] + 1)
                    copy(m1_hi[:, item[1], :], act_f[:, item[1] % 2, :], m1hi_done)
                elif kind == "x1":
                    n = item[1]
                    b, o = n // KT, n % KT
                    act.wait_ge(x1_ready, n + 1)
                    copy(x1_hi[:, o, b * SEQ:(b + 1) * SEQ], mm_ps[n % 4][:, :], x1hi_done)
                elif kind == "bprep":
                    act.wait_ge(bgu_in, 16)
                    act.wait_ge(a4_in, 16)
                    act.wait_ge(m1_ready, KT)
                    copy(bg4[:, :], bgu_raw[:, 0, :], bprep_hi)
                    copy(bu4[:, :], bgu_raw[:, 1, :], bprep_hi)
                    copy(a4_hi[:, :, :], a4_raw[:, :, :], bprep_hi)
                elif kind == "p":
                    b = item[1]
                    act.wait_ge(p_ready, b + 1)
                    copy(p4[:, b * SEQ:(b + 1) * SEQ], mm_ps[b][:, :], phi_done)
                elif kind == "unit":
                    n = item[1]
                    f, b = n // NB, n % NB
                    act.wait_ge(gate_ready, n + 1)
                    if n >= 2:
                        act.wait_ge(hlo_done, n - 1)
                    nc.scalar.activation(act_f[:, n % 2, :], mm_ps[2 * (n % 2)][:, :], ACT.Silu)\
                        .then_inc(silu_done, 1)
                    act.wait_ge(h_done, n + 1)
                    if f >= RING_H:
                        act.wait_ge(down_ready, slot_free_down(f))
                    copy(h_hi[:, f % RING_H, b * SEQ:(b + 1) * SEQ], act_f[:, n % 2, :], hhi_done)
            def late(item):
                for n in late_at.get(item, ()):
                    raw, hi, lo, arrived, count = late_weights()[n]
                    act.wait_ge(arrived, count)
                    act.wait_ge(unit_ready, 2 * NF)
                    if item:
                        act.wait_ge(down_ready, TT * len(GROUPS))
                    copy(hi, raw, whi_done)

            late(None)
            for item in TAIL:
                kind = item[0]
                if kind == "turn":
                    L, t = item[1:]
                    i = turn_no[item]
                    hi = xa_hi if L == 0 else xb_hi
                    act.wait_ge(turn_ready, i + 1)
                    if L == 0:
                        act.wait_ge(lo_done, len(SPLIT))
                    if L == 1:
                        act.wait_ge(down_ready, TT * len(GROUPS))
                    if L == 2:
                        act.wait_ge(qkv_ready, 3 * NB)
                    copy(hi[:, :, t * P:(t + 1) * P],
                         turn_ps[i % 2][:, :].rearrange("p (k c) -> p k c", k=KT), turnhi_done)
                    late(item)
                elif kind == "qkv":
                    b = item[1]
                    act.wait_ge(attn_in, 64)
                    act.wait_ge(ffn_ready, TT)
                    if b:
                        act.wait_ge(s_ready, TPB * b)
                        act.wait_ge(turn_ready, turn_no[("vturn", b - 1)] + 1)
                    for m, dst in enumerate((q_hi, k_hi, vT)):
                        act.wait_ge(qkv_ready, 3 * b + m + 1)
                        nc.scalar.activation(dst[:, :], qkv_ps[m][:, :], ACT.Identity,
                                             bias=br_qkv[:, m:m + 1]).then_inc(qkvhi_done, 1)
                elif kind == "vturn":
                    b, i = item[1], turn_no[item]
                    act.wait_ge(turn_ready, i + 1)
                    if b:
                        act.wait_ge(oT_ready, b)
                    copy(v_hi[:, :, :], turn_ps[i % 2][:, :].rearrange("p (k c) -> p k c", k=TPB), turnhi_done)
                elif kind == "s":
                    b, q = item[1:]
                    n = TPB * b + q
                    act.wait_ge(nmax_done, n + 1)
                    if n >= 2:
                        act.wait_ge(turn_ready, turn_no[("pturn", (n - 2) // TPB, (n - 2) % TPB)] + 1)
                    nc.scalar.activation(prob[:, n % 2, :], s_ps[n % 2][:, :], ACT.Exp, scale=ATTN_SCALE,
                                         bias=nmax[:, n:n + 1], accum_out=rsum[:, n:n + 1]).then_inc(exp_done, 1)
                elif kind == "pturn":
                    b, q = item[1:]
                    i = turn_no[item]
                    act.wait_ge(turn_ready, i + 1)
                    act.wait_ge(ffn_ready, TT)
                    if b:
                        act.wait_ge(oT_ready, b)
                    copy(pT_hi[:, :, q * P:(q + 1) * P],
                         turn_ps[i % 2][:, :].rearrange("p (k c) -> p k c", k=TPB), turnhi_done)
                elif kind == "ot":
                    b = item[1]
                    act.wait_ge(oT_ready, b + 1)
                    if b:
                        act.wait_ge(wo_ready, TPB * b)
                    copy(oT_hi[:, :], oT_ps[:, :], oThi_done)
                elif kind == "score":
                    t = item[1]
                    act.wait_ge(top_step, 5 * t + 3)
                    if t >= 2:
                        act.wait_ge(gate_done, t - 1)
                    nc.scalar.activation(gexp[:, t % 2, :], score_ps[t % 2][:, 0:EXPERTS], ACT.Exp,
                                         bias=gmax[:, t % 2:t % 2 + 1]).then_inc(gexp_done, 1)
                elif kind == "hturn":
                    t, i = item[1], turn_no[item]
                    for c in range(2):
                        act.wait_ge(turn_ready, i + c + 1)
                        if t >= 2 and c == 0:
                            act.wait_ge(mix_ready, t - 1)
                        copy(hgT_hi[:, t % 2, c * 4:(c + 1) * 4, :],
                             turn_ps[(i + c) % 2][:, :].rearrange("p (k c) -> p k c", k=4), turnhi_done)

        @block.tensor
        def _(pe):
            def product(ps, terms, start=True, stop=True):
                last = None
                for i, (ah, al, bh, bl) in enumerate(terms):
                    for n, (a, b) in enumerate(((ah, bh), (ah, bl), (al, bh))):
                        last = nc.tensor.matmul(ps, a, b, start=start and i == 0 and n == 0,
                                                stop=stop and i == len(terms) - 1 and n == 2)
                return last

            def lora(c):
                i = MERGED.index(c)
                if i:
                    pe.wait_ge(lora_added, i)
                kind, k = c
                if kind == "o":
                    a, b = la_o[:, k * P:(k + 1) * P], lb_o[:, :]
                elif kind == "v":
                    a, b = lb_qkv[:, k * P:(k + 1) * P], la_qkv[:, :]
                elif kind == "d":
                    pe.wait_ge(lorad_in, 32)
                    r = slice(32 * (k // 4), 32 * (k // 4) + RANK)
                    a, b = la_d[r, (k % 4) * P:(k % 4 + 1) * P], lb_d[r, :]
                else:
                    pe.wait_ge(loraf_in, 32)
                    a, b = la_f[:, k * P:(k + 1) * P], lb_f[:, :]
                nc.tensor.matmul(lora_ps[:, :], a, b, start=True, stop=True).then_inc(lora_ready, 1)

            pe.wait_ge(lora_in, 64)
            for c in MERGED[:2 * KT]:
                lora(c)
            pe.wait_ge(hi_done, split_no(("v", KT - 1)))
            pe.wait_ge(lo_done, split_no(("v", KT - 1)))
            for i in range(KT):
                cut = slice(i * P, (i + 1) * P)
                product(mm_ps[i][:, :], [(wq_hi[:, k, cut], wq_lo[:, k, cut], wo_hi[:, k, :], wo_lo[:, k, :])
                                         for k in range(KT)]).then_inc(m1_ready, 1)
            pe.wait_ge(m1hi_done, KT)
            pe.wait_ge(m1lo_done, KT)
            pe.wait_ge(xhi_done, 2 * KT)
            pe.wait_ge(xlo_done, 2 * KT)
            for n in range(NB * KT):
                b, o = n // KT, n % KT
                if n >= 4:
                    pe.wait_ge(x1hi_done, n - 3)
                    pe.wait_ge(xs_done, n - 3)
                cut, tk = slice(o * P, (o + 1) * P), slice(b * SEQ, (b + 1) * SEQ)
                product(mm_ps[n % 4][:, :], [(m1_hi[:, k, cut], m1_lo[:, k, cut], x_hi[:, k, tk], x_lo[:, k, tk])
                                             for k in range(KT)]).then_inc(x1_ready, 1)
            pe.wait_ge(bprep_done, 5)
            for b in range(NB):
                pe.wait_ge(x1hi_done, NB * KT)
                pe.wait_ge(x1lo_done, NB * KT)
                pe.wait_ge(xs_done, NB * KT)
                tk = slice(b * SEQ, (b + 1) * SEQ)
                product(mm_ps[b][:, :], [(a4_hi[:, k, :], a4_lo[:, k, :], x1_hi[:, k, tk], x1_lo[:, k, tk])
                                         for k in range(KT)]).then_inc(p_ready, 1)

            def unit(n):
                f, b = n // NB, n % NB
                tk = slice(b * SEQ, (b + 1) * SEQ)
                if n < 2:
                    pe.wait_ge(phi_done, NB)
                    pe.wait_ge(plo_done, NB)
                else:
                    pe.wait_ge(h_done, n - 1)
                downs = sum(1 for x in T[:T.index(("unit", n))] if x[0] == "down")
                if downs:
                    pe.wait_ge(down_added, downs)
                s = f % RING_GU
                for g, b4, done in ((0, bg4, gate_ready), (1, bu4, unit_ready)):
                    pe.wait_ge(hi_done, split_no(("gu"[g], f)))
                    pe.wait_ge(lo_done, split_no(("gu"[g], f)))
                    ps = mm_ps[2 * (n % 2) + g][:, :]
                    product(ps, [(gu_hi[:, s, g, k, :], gu_lo[:, s, g, k, :], x1_hi[:, k, tk], x1_lo[:, k, tk])
                                 for k in range(KT)], stop=False)
                    nc.tensor.matmul(ps, b4[:, f * P:(f + 1) * P], p4[:, tk], start=False, stop=True)\
                        .then_inc(done, 1)

            def down(gi, t):
                n = gi * TT + t
                last_f = GROUPS[gi][-1]
                deep = 4 if gi < len(GROUPS) - 1 else 2
                if t < deep:
                    pe.wait_ge(h_done, min(2 * (last_f + 2), 2 * NF))
                else:
                    pe.wait_ge(down_added, n - deep + 1)
                pe.wait_ge(hhi_done, 2 * last_f + 2)
                pe.wait_ge(hlo_done, 2 * last_f + 2)
                pe.wait_ge(hi_done, split_no(("d", last_f)))
                pe.wait_ge(lo_done, split_no(("d", last_f)))
                tk = slice(t * P, (t + 1) * P)
                ps = down_bank(gi, t)
                last = product(ps[:, :], [(h_hi[:, f % RING_H, tk], h_lo[:, f % RING_H, tk],
                                           wd_hi[:, f % RING_H, :], wd_lo[:, f % RING_H, :])
                                          for f in GROUPS[gi]], stop=gi > 0)
                if gi == 0:
                    pe.wait_ge(eye_in, 16)
                    for k in range(KT):
                        last = nc.tensor.matmul(ps[:, k * P:(k + 1) * P], xs[:, k, tk], ident[:, :],
                                                start=False, stop=k == KT - 1)
                last.then_inc(down_ready, 1)

            for item in T:
                if item[0] == "lora":
                    lora(item[1])
                elif item[0] == "unit":
                    unit(item[1])
                else:
                    down(item[1], item[2])
            for k in range(KT):
                lora(("f", k))

            def turn(ps, src):
                for k in range(4):
                    last = nc.tensor.transpose(ps[:, k * P:(k + 1) * P], src[:, k * P:(k + 1) * P], ident[:, :])
                return last

            def turn_free(i):
                if i >= 2:
                    pe.wait_ge(turnlo_done, i - 1)
                else:
                    pe.wait_ge(lut_step, 6 * NJ)

            def rows_wait(i):
                if i < 2:
                    pe.wait_ge(h_done, 2 * NF)
                    pe.wait_ge(down_added, TT * (len(GROUPS) - 1))
                else:
                    s, v = rows_free(i)
                    pe.wait_ge(s, v)

            for item in TAIL:
                kind = item[0]
                if kind == "down":
                    down(item[1], item[2])
                elif kind == "turn":
                    L, t = item[1:]
                    i = turn_no[item]
                    turn_free(i)
                    pe.wait_ge(norm_done, norm_no[(L, t)] + 1)
                    turn(turn_ps[i % 2], rows[:, t, :]).then_inc(turn_ready, 1)
                elif kind == "ffn":
                    t = item[1]
                    rows_wait(rows_no[item])
                    pe.wait_ge(turnlo_done, turn_no[("turn", 0, t)] + 1)
                    pe.wait_ge(turnhi_done, turn_no[("turn", 0, t)] + 1)
                    pe.wait_ge(hi_done, len(SPLIT))
                    pe.wait_ge(lo_done, len(SPLIT))
                    tk = slice(t * P, (t + 1) * P)
                    product(rows_ps[rows_no[item] % 2][:, :],
                            [(xa_hi[:, k, tk], xa_lo[:, k, tk], wff_hi[:, k, :], wff_lo[:, k, :])
                             for k in range(KT)]).then_inc(ffn_ready, 1)
                elif kind == "qkv":
                    b = item[1]
                    pe.wait_ge(turnlo_done, turn_no[("turn", 1, TPB * b + TPB - 1)] + 1)
                    pe.wait_ge(wlo_done, N_EA + N_ATTN)
                    pe.wait_ge(down_added, TT * len(GROUPS))
                    pe.wait_ge(lut_step, 6 * NJ)
                    if b:
                        pe.wait_ge(exp_done, TPB * b)
                        pe.wait_ge(qkvhi_done, 3 * b)
                    tk = slice(b * SEQ, (b + 1) * SEQ)
                    for m in range(3):
                        cut = slice(m * HD, (m + 1) * HD)
                        product(qkv_ps[m][:, :], [(wqkv_hi[:, k, cut], wqkv_lo[:, k, cut],
                                                   xb_hi[:, k, tk], xb_lo[:, k, tk])
                                                  for k in range(KT)]).then_inc(qkv_ready, 1)
                elif kind == "vturn":
                    b, i = item[1], turn_no[item]
                    turn_free(i)
                    pe.wait_ge(qkvhi_done, 3 * b + 3)
                    turn(turn_ps[i % 2], vT).then_inc(turn_ready, 1)
                elif kind == "s":
                    b, q = item[1:]
                    n = TPB * b + q
                    pe.wait_ge(qkvhi_done, 3 * b + 2)
                    pe.wait_ge(qklo_done, 2 * b + 2)
                    if n >= 2:
                        pe.wait_ge(exp_done, n - 1)
                    cut = slice(q * P, (q + 1) * P)
                    product(s_ps[n % 2][:, :], [(q_hi[:, cut], q_lo[:, cut], k_hi[:, :], k_lo[:, :])])\
                        .then_inc(s_ready, 1)
                elif kind == "pturn":
                    b, q = item[1:]
                    n, i = TPB * b + q, turn_no[item]
                    turn_free(i)
                    pe.wait_ge(exp_done, n + 1)
                    turn(turn_ps[i % 2], prob[:, n % 2, :]).then_inc(turn_ready, 1)
                elif kind == "ot":
                    b = item[1]
                    i = turn_no[("pturn", b, TPB - 1)]
                    pe.wait_ge(turnhi_done, i + 1)
                    pe.wait_ge(turnlo_done, i + 1)
                    pe.wait_ge(lora_added, len(MERGED))
                    if b:
                        pe.wait_ge(oTlo_done, b)
                    product(oT_ps[:, :], [(v_hi[:, k, :], v_lo[:, k, :], pT_hi[:, k, :], pT_lo[:, k, :])
                                          for k in range(TPB)]).then_inc(oT_ready, 1)
                elif kind == "wo":
                    t = item[1]
                    b = t // TPB
                    rows_wait(rows_no[item])
                    pe.wait_ge(oThi_done, b + 1)
                    pe.wait_ge(oTlo_done, b + 1)
                    cut = slice((t % TPB) * P, (t % TPB + 1) * P)
                    product(rows_ps[rows_no[item] % 2][:, :],
                            [(oT_hi[:, cut], oT_lo[:, cut], wout_hi[:, :], wout_lo[:, :])]).then_inc(wo_ready, 1)
                elif kind == "score":
                    t = item[1]
                    i = turn_no[("turn", 2, t)]
                    pe.wait_ge(turnhi_done, i + 1)
                    pe.wait_ge(turnlo_done, i + 1)
                    pe.wait_ge(attn_in, 64)
                    if t < 2:
                        pe.wait_ge(oTlo_done, NB)
                        pe.wait_ge(qkvhi_done, 3 * NB)
                    else:
                        pe.wait_ge(gate_done, t - 1)
                    tk = slice(t * P, (t + 1) * P)
                    for n, (part, k) in enumerate((part, k) for part in (xb_hi, xb_lo) for k in range(KT)):
                        last = nc.tensor.matmul(score_ps[t % 2][:, 0:EXPERTS], part[:, k, tk].bitcast(F32),
                                                wr[:, k, :], start=n == 0, stop=n == 2 * KT - 1)
                    last.then_inc(score_ready, 1)
                elif kind == "h":
                    t = item[1]
                    tk = slice(t * P, (t + 1) * P)
                    pe.wait_ge(exp_done, TT)
                    for c in range(2):
                        if t:
                            pe.wait_ge(hg_done, 2 * (t - 1) + c + 1)
                        cut = slice(c * 512, (c + 1) * 512)
                        product(hid_ps[c][:, :], [(xb_hi[:, k, tk], xb_lo[:, k, tk], ea_hi[:, k, cut], ea_lo[:, k, cut])
                                                  for k in range(KT)]).then_inc(hid_ready, 1)
                elif kind == "hturn":
                    t, i = item[1], turn_no[item]
                    for c in range(2):
                        turn_free(i + c)
                        pe.wait_ge(hg_done, 2 * t + c + 1)
                        turn(turn_ps[(i + c) % 2], hg[:, t % 2, c * 512:(c + 1) * 512]).then_inc(turn_ready, 1)
                elif kind == "mix":
                    t = item[1]
                    i = turn_no[("hturn", t)]
                    rows_wait(rows_no[item])
                    pe.wait_ge(turnhi_done, i + 2)
                    pe.wait_ge(turnlo_done, i + 2)
                    pe.wait_ge(wlo_done, len(late_weights()))
                    product(rows_ps[rows_no[item] % 2][:, :],
                            [(hgT_hi[:, t % 2, m, :], hgT_lo[:, t % 2, m, :], eb_hi[:, m, :], eb_lo[:, m, :])
                             for m in range(ER // P)]).then_inc(mix_ready, 1)

        @block.vector
        def _(dve):
            eye_mids = 0
            bn_steps = 0

            def low(dst, src, hi, done):
                nc.vector.tensor_tensor(dst, src, hi.bitcast(F32), ALU.subtract).then_inc(done, 1)

            for item in V:
                kind = item[0]
                if kind == "lut":
                    c = item[1]
                    j = CHUNKS.index(c)
                    src = code[:, j % RING_CODES, :]
                    dve.wait_ge(codes_in[j % RING_CODES], 16 * (j // RING_CODES + 1))
                    for i in range(6):
                        m, side = 6 * j + i, i % 2
                        lines = (UPPER, LOWER)[side]
                        ps, acc = plane[m % RING_PLANE][:, :], half[:, side, :]
                        dve.wait_ge(plane_ready, m + 1)
                        if m >= 2:
                            dve.wait_ge(lut_step, m - 1)
                        if i < 2:
                            ins = nc.vector.scalar_tensor_tensor(acc, src, float(lines[3][0]), ps, ALU.mult, ALU.max)
                        elif i < 4:
                            ins = nc.vector.scalar_tensor_tensor(acc, acc, float(lines[3][1]), ps, ALU.add, ALU.max)
                        else:
                            if j >= 2:
                                dve.wait_ge(diff_done, j - 1)
                            ins = nc.vector.tensor_tensor(halves[:, j % 2, side, :], acc, ps, ALU.max)
                        ins.then_inc(lut_step, 1)
                elif kind == "split" and item[1] in MERGED:
                    c = item[1]
                    j, i = CHUNKS.index(c), MERGED.index(c)
                    w = wf[:, j % RING_W, :]
                    dve.wait_ge(weight_ready, j + 1)
                    dve.wait_ge(lora_ready, i + 1)
                    if c[0] != "f":
                        nc.vector.tensor_tensor(w, lora_ps[:, :], w, ALU.add).then_inc(lora_added, 1)
                    else:
                        eye_mids += 1
                        nc.vector.scalar_tensor_tensor(w, lora_ps[:, :], LORA_SCALE, w, ALU.mult, ALU.add)\
                            .then_inc(eye_mid, 1)
                        dve.wait_ge(eye_mid, eye_mids)
                        d = w[:, c[1] * P:(c[1] + 1) * P]
                        nc.vector.tensor_tensor(d, d, ident[:, :], ALU.add).then_inc(lora_added, 1)
                elif kind == "xsplit":
                    k, b = item[1] // NB, item[1] % NB
                    tk = slice(b * SEQ, (b + 1) * SEQ)
                    dve.wait_ge(xhi_done, item[1] + 1)
                    low(x_lo[:, k, tk], xs[:, k, tk], x_hi[:, k, tk], xlo_done)
                elif kind == "m1":
                    i = item[1]
                    dve.wait_ge(m1_ready, i + 1)
                    dve.wait_ge(eye_in, 16)
                    if i >= 2:
                        dve.wait_ge(m1lo_done, i - 1)
                    f = act_f[:, i % 2, :]
                    nc.vector.tensor_scalar(f, mm_ps[i][:, :], 1.0 / 3.0, None, ALU.mult).then_inc(m1_third, 1)
                    dve.wait_ge(m1_third, i + 1)
                    d = f[:, i * P:(i + 1) * P]
                    nc.vector.tensor_tensor(d, d, ident[:, :], ALU.add).then_inc(m1_f, 1)
                    dve.wait_ge(m1hi_done, i + 1)
                    low(m1_lo[:, i, :], f, m1_hi[:, i, :], m1lo_done)
                elif kind == "x1":
                    n = item[1]
                    b, o = n // KT, n % KT
                    tk = slice(b * SEQ, (b + 1) * SEQ)
                    dve.wait_ge(x1hi_done, n + 1)
                    dve.wait_ge(xlo_done, 2 * KT)
                    low(x1_lo[:, o, tk], mm_ps[n % 4][:, :], x1_hi[:, o, tk], x1lo_done)
                    nc.vector.tensor_tensor(xs[:, o, tk], mm_ps[n % 4][:, :], xs[:, o, tk], ALU.add)\
                        .then_inc(xs_done, 1)
                elif kind == "bprep":
                    dve.wait_ge(bprep_hi, 3)
                    for g, b4 in enumerate((bg4, bu4)):
                        for r in (32, 96):
                            low(b4[r:r + 32, :], bgu_raw[r:r + 32, g, :], b4[r:r + 32, :], bprep_done)
                    low(a4_lo[:, :, :], a4_raw[:, :, :], a4_hi[:, :, :], bprep_done)
                elif kind == "p":
                    b = item[1]
                    tk = slice(b * SEQ, (b + 1) * SEQ)
                    dve.wait_ge(phi_done, b + 1)
                    low(p4[64:128, tk], mm_ps[b][64:128, :], p4[64:128, tk], plo_done)
                elif kind == "unit":
                    n = item[1]
                    f, b = n // NB, n % NB
                    tk = slice(b * SEQ, (b + 1) * SEQ)
                    a = act_f[:, n % 2, :]
                    dve.wait_ge(silu_done, n + 1)
                    dve.wait_ge(unit_ready, n + 1)
                    nc.vector.tensor_tensor(a, a, mm_ps[2 * (n % 2) + 1][:, :], ALU.mult).then_inc(h_done, 1)
                    dve.wait_ge(hhi_done, n + 1)
                    low(h_lo[:, f % RING_H, tk], a, h_hi[:, f % RING_H, tk], hlo_done)
                elif kind == "down":
                    gi, t = item[1:]
                    n = gi * TT + t
                    dve.wait_ge(down_ready, n + 1)
                    if gi == 0:
                        dve.wait_ge(bprep_done, 5)
                        nc.vector.tensor_copy(rows[:, t, :], down_bank(gi, t)[:, :]).then_inc(down_added, 1)
                    else:
                        dve.wait_ge(down_added, (gi - 1) * TT + t + 1)
                        nc.vector.tensor_tensor(rows[:, t, :], down_bank(gi, t)[:, :], rows[:, t, :], ALU.add)\
                            .then_inc(down_added, 1)

            for item in TAIL:
                kind = item[0]
                if kind == "down":
                    gi, t = item[1:]
                    n = gi * TT + t
                    dve.wait_ge(down_ready, n + 1)
                    dve.wait_ge(down_added, (gi - 1) * TT + t + 1)
                    nc.vector.tensor_tensor(rows[:, t, :], down_bank(gi, t)[:, :], rows[:, t, :], ALU.add)\
                        .then_inc(down_added, 1)
                elif kind == "stat":
                    L, t = item[1:]
                    i = stat_no[(L, t)]
                    s = i % RING_LN
                    src = rows[:, t, :]
                    if L == 0:
                        dve.wait_ge(down_added, TT * (len(GROUPS) - 1) + t + 1)
                    elif L == 1:
                        dve.wait_ge(ffn_ready, t + 1)
                        src = rows_ps[rows_no[("ffn", t)] % 2][:, :]
                    elif L == 2:
                        dve.wait_ge(res_done, t + 1)
                    else:
                        dve.wait_ge(mix_ready, t + 1)
                        nc.vector.scalar_tensor_tensor(src, rows_ps[rows_no[("mix", t)] % 2][:, :], EXPERT_SCALE,
                                                       src, ALU.mult, ALU.add).then_inc(res_done, 1)
                        dve.wait_ge(res_done, TT + t + 1)
                    nc.vector.bn_stats(bn6[:, s, :], src).then_inc(bn_step, 1)
                    dve.wait_ge(bn_step, 2 * i + 1)
                    if i >= RING_LN:
                        dve.wait_ge(norm_done, i - RING_LN + 1)
                    nc.vector.bn_aggr(mv[:, s, :], bn6[:, s, :]).then_inc(bn_step, 1)
                    dve.wait_ge(bn_step, 2 * i + 2)
                    if i >= RING_LN:
                        dve.wait_ge(rstd_ready, i - RING_LN + 1)
                    nc.vector.tensor_scalar(veps[:, s:s + 1], mv[:, s, 1:2], EPS, None, ALU.add)\
                        .then_inc(var_ready, 1)
                elif kind == "norm":
                    L, t = item[1:]
                    i = norm_no[(L, t)]
                    s = stat_no[(L, t)] % RING_LN
                    src = rows_ps[rows_no[("ffn", t)] % 2][:, :] if L == 1 else rows[:, t, :]
                    dve.wait_ge(rstd_ready, stat_no[(L, t)] + 1)
                    if L == 1:
                        dve.wait_ge(turn_ready, turn_no[("turn", 0, t)] + 1)
                    if L == 3:
                        dve.wait_ge(res_done, TT + t + 1)
                    nc.vector.tensor_scalar(rows[:, t, :], src, mv[:, s, 0:1], rstd[:, s:s + 1],
                                            ALU.subtract, ALU.mult).then_inc(norm_done, 1)
                elif kind == "turn":
                    L, t = item[1:]
                    i = turn_no[item]
                    hi, lo = (xa_hi, xa_lo) if L == 0 else (xb_hi, xb_lo)
                    dve.wait_ge(turnhi_done, i + 1)
                    tk = slice(t * P, (t + 1) * P)
                    low(lo[:, :, tk], turn_ps[i % 2][:, :].rearrange("p (k c) -> p k c", k=KT), hi[:, :, tk],
                        turnlo_done)
                elif kind == "qkv":
                    b = item[1]
                    for m, (hi, lo) in enumerate(((q_hi, q_lo), (k_hi, k_lo))):
                        dve.wait_ge(qkvhi_done, 3 * b + m + 1)
                        nc.vector.scalar_tensor_tensor(lo[:, :], qkv_ps[m][:, :], br_qkv[:, m:m + 1],
                                                       hi[:, :].bitcast(F32), ALU.add, ALU.subtract)\
                            .then_inc(qklo_done, 1)
                elif kind == "vturn":
                    i = turn_no[item]
                    dve.wait_ge(turnhi_done, i + 1)
                    low(v_lo[:, :, :], turn_ps[i % 2][:, :].rearrange("p (k c) -> p k c", k=TPB), v_hi[:, :, :],
                        turnlo_done)
                elif kind == "s":
                    b, q = item[1:]
                    n = TPB * b + q
                    dve.wait_ge(s_ready, n + 1)
                    nc.vector.reduce_max(rmax[:, n:n + 1], s_ps[n % 2][:, :], AX_X).then_inc(max_done, 1)
                    dve.wait_ge(max_done, n + 1)
                    nc.vector.tensor_scalar(nmax[:, n:n + 1], rmax[:, n:n + 1], -ATTN_SCALE, None, ALU.mult)\
                        .then_inc(nmax_done, 1)
                elif kind == "pturn":
                    b, q = item[1:]
                    n, i = TPB * b + q, turn_no[item]
                    dve.wait_ge(exp_done, n + 1)
                    nc.vector.reciprocal(rinv[:, n:n + 1], rsum[:, n:n + 1]).then_inc(rinv_done, 1)
                    dve.wait_ge(turnhi_done, i + 1)
                    cut = slice(q * P, (q + 1) * P)
                    low(pT_lo[:, :, cut], turn_ps[i % 2][:, :].rearrange("p (k c) -> p k c", k=TPB),
                        pT_hi[:, :, cut], turnlo_done)
                elif kind == "ot":
                    dve.wait_ge(oThi_done, item[1] + 1)
                    low(oT_lo[:, :], oT_ps[:, :], oT_hi[:, :], oTlo_done)
                elif kind == "wo":
                    t = item[1]
                    dve.wait_ge(wo_ready, t + 1)
                    dve.wait_ge(rinv_done, t + 1)
                    dve.wait_ge(bo_added, t + 1)
                    nc.vector.scalar_tensor_tensor(rows[:, t, :], rows_ps[rows_no[item] % 2][:, :],
                                                   rinv[:, t:t + 1], rows[:, t, :], ALU.mult, ALU.add)\
                        .then_inc(res_done, 1)
                elif kind == "score":
                    t = item[1]
                    s, sc = t % 2, score_ps[t % 2][:, 0:EXPERTS]
                    dve.wait_ge(score_ready, t + 1)
                    nc.vector.max(top8[:, s, 0, :], sc).then_inc(top_step, 1)
                    dve.wait_ge(top_step, 5 * t + 1)
                    if t >= 2:
                        dve.wait_ge(gexp_done, t - 1)
                    nc.vector.tensor_scalar(gmax[:, s:s + 1], top8[:, s, 0, 0:1], -1.0, None, ALU.mult)\
                        .then_inc(top_step, 1)
                    nc.vector.match_replace(left1[:, s, :], top8[:, s, 0, :], sc, TAKEN).then_inc(top_step, 1)
                    dve.wait_ge(top_step, 5 * t + 3)
                    nc.vector.max(top8[:, s, 1, :], left1[:, s, :]).then_inc(top_step, 1)
                    dve.wait_ge(top_step, 5 * t + 4)
                    nc.vector.match_replace(left2[:, s, :], top8[:, s, 1, :], left1[:, s, :], TAKEN)\
                        .then_inc(top_step, 1)
                    dve.wait_ge(top_step, 5 * t + 5)
                    dve.wait_ge(gexp_done, t + 1)
                    nc.vector.scalar_tensor_tensor(gate[:, s, :], left2[:, s, :], TAKEN, gexp[:, s, :],
                                                   ALU.is_equal, ALU.mult, accum_out=gsum[:, s:s + 1])\
                        .then_inc(gsum_done, 1)
                    dve.wait_ge(gsum_done, t + 1)
                    nc.vector.reciprocal(ginv[:, s:s + 1], gsum[:, s:s + 1]).then_inc(ginv_done, 1)
                    dve.wait_ge(ginv_done, t + 1)
                    nc.vector.tensor_scalar(gate[:, s, :], gate[:, s, :], ginv[:, s:s + 1], None, ALU.mult)\
                        .then_inc(gate_done, 1)
                elif kind == "h":
                    t = item[1]
                    dve.wait_ge(gate_done, t + 1)
                    if t >= 2:
                        dve.wait_ge(turn_ready, turn_no[("hturn", t - 2)] + 2)
                    for c in range(2):
                        dve.wait_ge(hid_ready, 2 * t + c + 1)
                        g = gate[:, t % 2, c * EPC:(c + 1) * EPC].unsqueeze(2).to_broadcast([P, EPC, ERANK])
                        nc.vector.tensor_tensor(
                            hg[:, t % 2, c * 512:(c + 1) * 512].rearrange("p (e r) -> p e r", r=ERANK),
                            hid_ps[c][:, :].rearrange("p (e r) -> p e r", r=ERANK), g, ALU.mult)\
                            .then_inc(hg_done, 1)
                elif kind == "hturn":
                    t, i = item[1], turn_no[item]
                    for c in range(2):
                        dve.wait_ge(turnhi_done, i + c + 1)
                        low(hgT_lo[:, t % 2, c * 4:(c + 1) * 4, :],
                            turn_ps[(i + c) % 2][:, :].rearrange("p (k c) -> p k c", k=4),
                            hgT_hi[:, t % 2, c * 4:(c + 1) * 4, :], turnlo_done)


def laid_out(a):
    import numpy as np

    def cat(parts):
        return np.ascontiguousarray(np.stack(parts))

    ca, cg, cd, cf = (np.asarray(a[n]) for n in ("L0_attn_codes_attn", "L0_attn_codes_gu", "L0_attn_codes_down",
                                                 "L0_ffn_codes"))
    sa, sg, sd, sf = (np.asarray(a[n]) for n in ("L0_attn_scales_attn", "L0_attn_scales_gu",
                                                 "L0_attn_scales_down", "L0_ffn_absmax"))
    codes, scales = [], []
    for kind, k in CHUNKS:
        cut, blk = slice(k * P, (k + 1) * P), slice(2 * k, 2 * k + 2)
        if kind == "o":
            codes.append(ca[3].T[cut])
            scales.append(sa[3].T[blk])
        elif kind in "qkv":
            codes.append(ca["qkv".index(kind)][cut])
        elif kind in "gu":
            g = "gu".index(kind)
            codes.append(cg[g][cut].reshape(P, KT, P).transpose(2, 1, 0).reshape(P, H))
            scales.append(sg[g][cut].reshape(P, KT, 2).transpose(2, 1, 0).reshape(2, H))
        elif kind == "d":
            codes.append(cd.T[cut])
            scales.append(sd.T[blk])
        else:
            codes.append(cf.T[cut])
            scales.append(sf.T[blk])

    def tiles(m):
        return np.ascontiguousarray(m.reshape(-1, P, m.shape[1]).transpose(1, 0, 2))

    x = np.asarray(a["L0_attn_x"]).reshape(TOK, H)
    Ah, Ad = np.asarray(a["L0_attn_lora_A_h"]), np.asarray(a["L0_attn_lora_A_down"])
    Ba, Bg, Bd = (np.asarray(a[n]) for n in ("L0_attn_lora_B_attn", "L0_attn_lora_B_gu", "L0_attn_lora_B_down"))
    zero = np.zeros((RANK, FF), np.float32)
    la_d = np.zeros((P, 512), np.float32)
    lb_d = np.zeros((P, 512), np.float32)
    for g in range(4):
        part = Ad[:, g * 512:(g + 1) * 512]
        la_d[32 * g:32 * g + RANK, :part.shape[1]] = part
        lb_d[32 * g:32 * g + RANK] = Bd.T
    A4 = np.tile(np.concatenate([Ah[4], Ah[5]]), (4, 1))
    B4 = [np.tile(np.concatenate(rows), (4, 1)) for rows in ((Bg[0].T, zero), (zero, Bg[1].T))]
    eA, eB = np.asarray(a["L1_ffn_A"]), np.asarray(a["L1_ffn_B"])
    named = dict(
        codes=cat(codes), scales=cat(scales),
        scales_qkv=np.ascontiguousarray(sa[:3].reshape(3 * KT, P, H // QB).transpose(1, 0, 2)),
        eye=np.eye(P, dtype=np.float32), xT=tiles(x.T),
        loA_o=Ah[3], loB_o=Ba[3].T, loA_qkv=Ah[:3].reshape(3 * RANK, H),
        loB_qkv=Ba[:3].transpose(0, 2, 1).reshape(3 * RANK, H),
        loA_gu=tiles(A4.T), loB_gu=np.stack(B4, 1), loA_d=la_d, loB_d=lb_d,
        loA_f=np.asarray(a["L0_ffn_lora_A"]), loB_f=np.asarray(a["L0_ffn_lora_B"]).T,
        w_qkv=tiles(np.asarray(a["L1_attn_Wqkv"])),
        b_qkv=np.asarray(a["L1_attn_bqkv"]).reshape(3, HD).T,
        w_o=np.asarray(a["L1_attn_Wo"]), b_o=np.asarray(a["L1_attn_bo"]).reshape(1, H),
        ex_A=tiles(eA.reshape(ER, H).T),
        ex_B=tiles(eB.transpose(0, 2, 1).reshape(ER, H)),
        w_r=tiles(np.asarray(a["L1_ffn_Wr"]).T),
    )
    return {k: np.ascontiguousarray(v) for k, v in named.items()}


def kernel(**inputs):
    import concourse.bacc as bacc
    from concourse.bass_utils import run_bass_kernel_spmd

    arrays = laid_out(inputs)
    nc = bacc.Bacc("TRN2", target_bir_lowering=False, num_devices=1)
    args = {k: nc.dram_tensor(k, v.shape, mybir.dt.from_np(v.dtype), kind="ExternalInput").ap()
            for k, v in arrays.items()}
    out = nc.dram_tensor("out", (TOK, H), F32, kind="ExternalOutput").ap()
    build(nc, out=out, **args)
    result = run_bass_kernel_spmd(nc, [arrays], core_ids=[0])
    return result.results[0]["out"].reshape(NB, SEQ, H)
```

```python
from contextlib import ExitStack

import concourse.bass as bass
from concourse import mybir

P = 128
H = 512
KT = H // P
TOK = 1024
TT = TOK // P
SEQ = 512
NB = TOK // SEQ
TPB = SEQ // P
FF = 1792
NF = FF // P
QB = 64
RANK = 16
FFN_RANK = 64
HD = 128
EXPERTS, TOPK, ERANK = 64, 16, 16
ER = EXPERTS * ERANK
EPC = H // ERANK
LORA_SCALE = 16.0 / 64.0
EXPERT_SCALE = 32.0 / ERANK
EPS = 1e-5
ATTN_SCALE = float(HD) ** -0.5
TAKEN = -3.0e38

F32 = mybir.dt.float32
F32R = mybir.dt.float32r
I32 = mybir.dt.int32
ALU = mybir.AluOpType
ACT = mybir.ActivationFunctionType
AX_X = mybir.AxisListType.X

NF4 = [-1.0, -0.6961928009986877, -0.5250730514526367, -0.39491748809814453, -0.28444138169288635,
       -0.18477343022823334, -0.09105003625154495, 0.0, 0.07958029955625534, 0.16093020141124725,
       0.24611230194568634, 0.33791524171829224, 0.44070982933044434, 0.5626170039176941,
       0.7229568362236023, 1.0]


def line(sign, a, b):
    slope = sign * (NF4[b] - NF4[a]) / (b - a)
    return slope, sign * NF4[a] - slope * a


UPPER = [line(1, 8, 9), line(1, 10, 11), line(1, 12, 13), line(1, 14, 15)]
LOWER = [line(-1, 6, 5), line(-1, 4, 3), line(-1, 2, 1), (1.5 * (NF4[0] - NF4[1]), -NF4[0])]

GROUPS = [range(f, f + 2) for f in range(0, NF, 2)]
FFN_AT = {5 + 2 * k: k for k in range(KT)}


def chunk_list():
    chunks = [("o", k) for k in range(KT)]
    chunks += [(m, k) for k in range(KT) for m in ("q", "k", "v")]
    chunks += [("g", 0), ("u", 0), ("g", 1), ("u", 1), ("d", 0)]
    for f in range(1, NF):
        chunks += [("g", f + 1), ("u", f + 1)] if f + 1 < NF else []
        chunks += [("d", f)]
        chunks += [("f", FFN_AT[f])] if f in FFN_AT else []
    return chunks


CHUNKS = chunk_list()
NJ = len(CHUNKS)
MERGED = [c for c in CHUNKS if c[0] in "ovdf"]
SPLIT = [c for c in CHUNKS if c[0] not in "qk"]
SCALED = [c for c in CHUNKS if c[0] not in "qkv"]
RING_CODES = 3
RING_W = 3
RING_PLANE = 3
RING_H = 5
RING_GU = 2
RING_LN = 4


def vector_order():
    order = []

    def lut(c):
        j = CHUNKS.index(c)
        order.append(("lut", c))
        if j and CHUNKS[j - 1] in SPLIT:
            order.append(("split", CHUNKS[j - 1]))

    for j in range(16):
        lut(CHUNKS[j])
    order.extend(("xsplit", i) for i in range(KT))
    lut(("g", 0))
    order.extend(("m1", i) for i in range(KT))
    order.extend(("xsplit", i) for i in range(KT, 2 * KT))
    lut(("u", 0))
    order.extend(("x1", n) for n in range(3))
    order.append(("bprep", 0))
    lut(("g", 1))
    order.extend(("x1", n) for n in range(3, 6))
    lut(("u", 1))
    order.extend(("x1", n) for n in range(6, 8))
    order.extend(("p", b) for b in range(NB))
    for f in range(NF):
        downs = downs_beside(f)
        ahead = [("g", f + 1), ("u", f + 1)] if 1 <= f < NF - 1 else [None, None]
        for b, c in enumerate(ahead):
            if c:
                lut(c)
            elif f == NF - 1 and b == 0:
                lut(("d", f))
            order.append(("silu", 2 * f + b))
            order.extend(downs[2 * b:2 * b + 1])
            if b and f < NF - 1:
                lut(("d", f))
            if b and f in FFN_AT:
                lut(("f", FFN_AT[f]))
            order.append(("h", 2 * f + b))
            order.extend(downs[2 * b + 1:2 * b + 2])
    order.append(("split", CHUNKS[-1]))
    return order


def downs_beside(f):
    g = f // 2 - 1
    return [("down", g, t) for t in range(4 * (f % 2), 4 * (f % 2) + 4)] if g >= 0 else []


def tensor_order():
    order = []
    for f in range(NF):
        downs = downs_beside(f)
        for b in range(NB):
            order.append(("gate", 2 * f + b))
            order.extend(downs[2 * b:2 * b + 1])
            order.append(("up", 2 * f + b))
            order.extend(downs[2 * b + 1:2 * b + 2])
            if b == 0:
                order.append(("lora", ("d", f)))
            elif f in FFN_AT:
                order.append(("lora", ("f", FFN_AT[f])))
    return order


def tail_order():
    order = []
    gi = len(GROUPS) - 1
    for r in range(TT + 7):
        if 0 <= r - 2 < TT:
            order.append(("turn", 0, r - 2))
        if 0 <= r - 6 < TT:
            order.append(("turn", 1, r - 6))
        if 0 <= r - 1 < TT:
            order.append(("norm", 0, r - 1))
        if 0 <= r - 5 < TT:
            order.append(("norm", 1, r - 5))
        if 0 <= r - 3 < TT:
            order.append(("ffn", r - 3))
        if r < TT:
            order += [("down", gi, t) for t in range(2 * r, min(2 * r + 2, TT))]
            order.append(("stat", 0, r))
        if 0 <= r - 4 < TT:
            order.append(("stat", 1, r - 4))
    order += [("qkv", 0, m) for m in range(3)]
    order += [("vturn", 0), ("s", 0, 0), ("s", 0, 1), ("qkv", 1, 0), ("pturn", 0, 0), ("s", 0, 2), ("qkv", 1, 1),
              ("pturn", 0, 1), ("s", 0, 3), ("qkv", 1, 2), ("pturn", 0, 2), ("vturn", 1), ("pturn", 0, 3),
              ("s", 1, 0), ("ot", 0), ("s", 1, 1), ("pturn", 1, 0), ("wo", 0), ("s", 1, 2), ("pturn", 1, 1),
              ("wo", 1), ("wo", 2), ("s", 1, 3), ("pturn", 1, 2), ("wo", 3), ("pturn", 1, 3)]
    for r in range(TT + 6):
        if r == 1:
            order += [("ot", 1)]
        if 1 <= r <= TPB:
            order.append(("wo", TPB + r - 1))
        if 0 <= r - 2 < TT:
            order.append(("turn", 2, r - 2))
        if 0 <= r - 4 < TT:
            order.append(("hturn", r - 4))
        if 0 <= r - 3 < TT:
            order.append(("score", r - 3))
        if 0 <= r - 5 < TT:
            order.append(("stat", 3, r - 5))
        if r < TT:
            order.append(("stat", 2, r))
        if 0 <= r - 1 < TT:
            order.append(("norm", 2, r - 1))
        if 0 <= r - 5 < TT:
            order.append(("norm", 3, r - 5))
        if 0 <= r - 3 < TT:
            order.append(("h", r - 3))
        if 0 <= r - 4 < TT:
            order.append(("mix", r - 4))
    return order


def build(nc, codes, scales, scales_qkv, eye, xT, loA_o, loB_o, loA_qkv, loB_qkv, loA_gu, loB_gu,
          loA_d, loB_d, loA_f, loB_f, w_qkv, b_qkv, w_o, b_o, ex_A, ex_B, w_r, out):
    with ExitStack() as ctx:
        bn6 = ctx.enter_context(nc.sbuf_tensor("bn6", [P, RING_LN, 6], F32))
        mv = ctx.enter_context(nc.sbuf_tensor("mv", [P, RING_LN, 2], F32))
        veps = ctx.enter_context(nc.sbuf_tensor("veps", [P, RING_LN], F32))
        rstd = ctx.enter_context(nc.sbuf_tensor("rstd", [P, RING_LN], F32))
        nbias = ctx.enter_context(nc.sbuf_tensor("nbias", [P, RING_LN], F32))
        neg_half = ctx.enter_context(nc.sbuf_tensor("neg_half", [P, 1], F32))
        low_rows = ctx.enter_context(nc.sbuf_tensor("low_rows", [P, 1], F32))
        base = (nc.sbuf_base + 63) // 64 * 64

        def at(name, kb, shape, dt=F32):
            return nc.alloc_sbuf_tensor_at(name, shape, dt, offset=base + int(kb * 1024))

        def sem(name):
            return ctx.enter_context(nc.semaphore(name))

        code = at("code", 0, [P, RING_CODES, 512], I32)
        scale = at("scale", 6, [P, RING_CODES, 512])
        half = at("half", 12, [P, 2, 512])
        halves = at("halves", 16, [P, 2, 2, 512])
        wf = at("wf", 24, [P, RING_W, 512])
        act_f = at("act_f", 30, [P, 2, 512])
        xs = at("xs", 34, [P, KT, TOK])
        x_hi = at("x_hi", 50, [P, KT, TOK], F32R)
        x_lo = at("x_lo", 66, [P, KT, TOK], F32R)
        m1_hi = at("m1_hi", 82, [P, KT, H], F32R)
        m1_lo = at("m1_lo", 90, [P, KT, H], F32R)
        h_hi = at("h_hi", 50, [P, RING_H, TOK], F32R)
        h_lo = at("h_lo", 70, [P, RING_H, TOK], F32R)
        rows = at("rows", 98, [P, TT, H])
        bgu_raw = at("bgu_raw", 98, [P, 2, FF])
        a4_raw = at("a4_raw", 112, [P, KT, P])
        wq_hi = at("wq_hi", 146, [P, KT, H], F32R)
        wq_lo = at("wq_lo", 154, [P, KT, H], F32R)
        wo_hi = at("wo_hi", 162, [P, KT, H], F32R)
        wo_lo = at("wo_lo", 170, [P, KT, H], F32R)
        wd_hi = at("wd_hi", 114, [P, RING_H, H], F32R)
        wd_lo = at("wd_lo", 124, [P, RING_H, H], F32R)
        bg4 = at("bg4", 134, [P, FF], F32R)
        p4 = at("p4", 141, [P, TOK], F32R)
        a4_hi = at("a4_hi", 205, [P, KT, P], F32R)
        x1_hi = at("x1_hi", 146, [P, KT, TOK], F32R)
        x1_lo = at("x1_lo", 162, [P, KT, TOK], F32R)
        gu_hi = at("gu_hi", 178, [P, RING_GU, 2, KT, P], F32R)
        gu_lo = at("gu_lo", 186, [P, RING_GU, 2, KT, P], F32R)
        la_o = at("la_o", 182, [RANK, 512])
        lb_o = at("lb_o", 184, [RANK, 512])
        la_qkv = at("la_qkv", 190, [3 * RANK, 512])
        lb_qkv = at("lb_qkv", 192, [3 * RANK, 512])
        bu4 = at("bu4", 194, [P, FF], F32R)
        la_d = at("la_d", 201, [P, 512])
        lb_d = at("lb_d", 203, [P, 512])
        a4_lo = at("a4_lo", 132, [P, KT, P], F32R)
        ident = at("ident", 207, [P, P])
        la_f = at("la_f", 90, [FFN_RANK, 512])
        lb_f = at("lb_f", 92, [FFN_RANK, 512])
        wff_hi = at("wff_hi", 34, [P, KT, H], F32R)
        wff_lo = at("wff_lo", 42, [P, KT, H], F32R)
        xa_hi = at("xa_hi", 0, [P, KT, TOK], F32R)
        xa_lo = at("xa_lo", 16, [P, KT, TOK], F32R)
        xb_hi = at("xb_hi", 50, [P, KT, TOK], F32R)
        xb_lo = at("xb_lo", 66, [P, KT, TOK], F32R)
        ea_raw = at("ea_raw", 178, [P, KT, ER])
        eb_raw = at("eb_raw", 130, [P, ER // P, H])
        ea_hi = at("ea_hi", 162, [P, KT, ER], F32R)
        ea_lo = at("ea_lo", 178, [P, KT, ER], F32R)
        eb_hi = at("eb_hi", 114, [P, ER // P, H], F32R)
        eb_lo = at("eb_lo", 130, [P, ER // P, H], F32R)
        wqkv_raw = at("wqkv_raw", 194, [P, KT, 3 * HD])
        wout_raw = at("wout_raw", 200, [P, H])
        br_qkv = at("br_qkv", 202, [P, 3])
        wqkv_hi = at("wqkv_hi", 82, [P, KT, 3 * HD], F32R)
        wqkv_lo = at("wqkv_lo", 88, [P, KT, 3 * HD], F32R)
        wout_hi = at("wout_hi", 94, [P, H], F32R)
        wout_lo = at("wout_lo", 96, [P, H], F32R)
        bo_rows = at("bo_rows", 32, [P, H])
        wr = at("wr", 203, [P, KT, EXPERTS])
        q_hi = at("q_hi", 0, [P, NB, SEQ], F32R)
        q_lo = at("q_lo", 4, [P, NB, SEQ], F32R)
        k_hi = at("k_hi", 8, [P, NB, SEQ], F32R)
        k_lo = at("k_lo", 12, [P, NB, SEQ], F32R)
        vT = at("vT", 16, [P, SEQ])
        v_hi = at("v_hi", 24, [P, NB, TPB, HD], F32R)
        v_lo = at("v_lo", 28, [P, NB, TPB, HD], F32R)
        oT_hi = at("oT_hi", 146, [P, NB, SEQ], F32R)
        oT_lo = at("oT_lo", 150, [P, NB, SEQ], F32R)
        prob = at("prob", 18, [P, 2, SEQ])
        pT_hi = at("pT_hi", 34, [P, TPB, SEQ], F32R)
        pT_lo = at("pT_lo", 42, [P, TPB, SEQ], F32R)
        hg = at("hg", 0, [P, 2, ER])
        hgT_hi = at("hgT_hi", 8, [P, 2, ER // P, P], F32R)
        hgT_lo = at("hgT_lo", 16, [P, 2, ER // P, P], F32R)
        left1 = at("left1", 24, [P, 2, EXPERTS])
        left2 = at("left2", 24.5, [P, 2, EXPERTS])
        gexp = at("gexp", 25, [P, 2, EXPERTS])
        gate = at("gate", 25.5, [P, 2, EXPERTS])
        sc_qkv = at("sc_qkv", 205, [P, 12, H // QB])
        rmax = at("rmax", 22, [P, TT])
        nmax = at("nmax", 22.25, [P, TT])
        rsum = at("rsum", 22.5, [P, TT])
        rinv = at("rinv", 22.75, [P, TT])
        top8 = at("top8", 26, [P, 2, 2, 8])
        gmax = at("gmax", 26.25, [P, 2])
        gsum = at("gsum", 26.5, [P, 2])
        ginv = at("ginv", 26.75, [P, 2])

        bank = [ctx.enter_context(nc.psum_tensor(f"bank{i}", [P, 512], F32)) for i in range(8)]
        plane = bank[0:RING_PLANE]
        lora_ps = bank[3]
        mm_ps = bank[4:8]
        unit_ps = bank[4:7]
        turn_ps = bank[0:2]
        rows_ps = [bank[4], bank[5], bank[2]]
        qkv_ps = bank[3:6]
        s_ps = bank[6:8]
        oT_ps = bank[3]
        score_ps = bank[3]
        hid_ps = bank[6:8]

        codes_in = [sem(f"codes_in{i}") for i in range(RING_CODES)]
        scale_in = [sem(f"scale_in{i}") for i in range(RING_CODES)]
        sqkv_in = sem("sqkv_in")
        x_in = sem("x_in")
        eye_in = sem("eye_in")
        lora_in = sem("lora_in")
        lorad_in = sem("lorad_in")
        loraf_in = sem("loraf_in")
        bgu_in = sem("bgu_in")
        a4_in = sem("a4_in")
        plane_ready = sem("plane_ready")
        lut_step = sem("lut_step")
        diff_done = sem("diff_done")
        mult_done = sem("mult_done")
        weight_ready = sem("weight_ready")
        lora_ready = sem("lora_ready")
        lora_added = sem("lora_added")
        eye_mid = sem("eye_mid")
        hi_done = sem("hi_done")
        lo_done = sem("lo_done")
        xhi_done = sem("xhi_done")
        xlo_done = sem("xlo_done")
        m1_ready = sem("m1_ready")
        m1_third = sem("m1_third")
        m1_f = sem("m1_f")
        m1hi_done = sem("m1hi_done")
        m1lo_done = sem("m1lo_done")
        x1_ready = sem("x1_ready")
        x1hi_done = sem("x1hi_done")
        x1lo_done = sem("x1lo_done")
        xs_done = sem("xs_done")
        bprep_hi = sem("bprep_hi")
        bprep_done = sem("bprep_done")
        p_ready = sem("p_ready")
        phi_done = sem("phi_done")
        plo_done = sem("plo_done")
        gate_ready = sem("gate_ready")
        unit_ready = sem("unit_ready")
        silu_done = sem("silu_done")
        h_done = sem("h_done")
        hhi_done = sem("hhi_done")
        hlo_done = sem("hlo_done")
        down_ready = sem("down_ready")
        down_added = sem("down_added")
        neg_half_set = sem("neg_half_set")
        low_rows_set = sem("low_rows_set")
        bn_step = sem("bn_step")
        var_ready = sem("var_ready")
        rstd_ready = sem("rstd_ready")
        nbias_ready = sem("nbias_ready")
        norm_done = sem("norm_done")
        turn_ready = sem("turn_ready")
        turnhi_done = sem("turnhi_done")
        turnlo_done = sem("turnlo_done")
        ffn_ready = sem("ffn_ready")
        attn_in = sem("attn_in")
        bo_in = sem("bo_in")
        ea_in = sem("ea_in")
        eb_in = sem("eb_in")
        whi_done = sem("whi_done")
        wlo_done = sem("wlo_done")
        bo_added = sem("bo_added")
        qkv_ready = sem("qkv_ready")
        qkvhi_done = sem("qkvhi_done")
        qklo_done = sem("qklo_done")
        s_ready = sem("s_ready")
        max_done = sem("max_done")
        nmax_done = sem("nmax_done")
        exp_done = sem("exp_done")
        rinv_done = sem("rinv_done")
        oT_ready = sem("oT_ready")
        oThi_done = sem("oThi_done")
        oTlo_done = sem("oTlo_done")
        wo_ready = sem("wo_ready")
        res_done = sem("res_done")
        score_ready = sem("score_ready")
        top_step = sem("top_step")
        gexp_done = sem("gexp_done")
        gate_done = sem("gate_done")
        gsum_done = sem("gsum_done")
        ginv_done = sem("ginv_done")
        hid_ready = sem("hid_ready")
        hg_done = sem("hg_done")
        mix_ready = sem("mix_ready")
        out_done = sem("out_done")

        V, T = vector_order(), tensor_order()
        TAIL = tail_order()

        def split_no(c):
            return SPLIT.index(c) + 1

        def group_of(f):
            return next(i for i, g in enumerate(GROUPS) if f in g)

        def down_bank(gi, t):
            return bank[7] if gi < len(GROUPS) - 1 else bank[7 - t % 2]

        def slot_free_down(f):
            return TT * (group_of(f - RING_H) + 1)

        turn_no = {}
        n = 0
        for x in TAIL:
            if x[0] in ("turn", "vturn", "pturn", "hturn"):
                turn_no[x] = n
                n += 2 if x[0] == "hturn" else 1
        rows_no = {x: i for i, x in enumerate(x for x in TAIL if x[0] in ("ffn", "wo", "mix"))}
        norm_no = {x[1:]: i for i, x in enumerate(x for x in TAIL if x[0] == "norm")}
        stat_no = {x[1:]: i for i, x in enumerate(x for x in TAIL if x[0] == "stat")}

        def slot_normed(i):
            return norm_no[next(x for x, m in stat_no.items() if m == i - RING_LN)] + 1

        def rows_free(i):
            x = next(x for x, m in rows_no.items() if m == i - 3)
            if x[0] == "ffn":
                return norm_done, norm_no[(1, x[1])] + 1
            if x[0] == "wo":
                return res_done, x[1] + 1
            return res_done, TT + x[1] + 1

        def dest(c):
            kind, k = c
            if kind == "o":
                return wo_hi[:, k, :], wo_lo[:, k, :]
            if kind == "v":
                return wq_hi[:, k, :], wq_lo[:, k, :]
            if kind in "gu":
                g = "gu".index(kind)
                return gu_hi[:, k % RING_GU, g, :, :], gu_lo[:, k % RING_GU, g, :, :]
            if kind == "d":
                return wd_hi[:, k % RING_H, :], wd_lo[:, k % RING_H, :]
            return wff_hi[:, k, :], wff_lo[:, k, :]

        def shaped(c, w):
            return w.rearrange("p (k o) -> p k o", k=KT) if c[0] in "gu" else w

        def late_weights():
            pieces = []
            for k in range(KT):
                pieces.append((wqkv_raw[:, k, :], wqkv_hi[:, k, :], wqkv_lo[:, k, :], attn_in, 64))
            pieces.append((wout_raw[:, :], wout_hi[:, :], wout_lo[:, :], attn_in, 64))
            for k in range(KT):
                for h in range(ER // 512):
                    cut = slice(h * 512, (h + 1) * 512)
                    pieces.append((ea_raw[:, k, cut], ea_hi[:, k, cut], ea_lo[:, k, cut], ea_in, 16))
            for m in range(ER // P):
                pieces.append((eb_raw[:, m, :], eb_hi[:, m, :], eb_lo[:, m, :], eb_in, 16))
            return pieces

        N_EA, N_ATTN = KT * (ER // 512), KT + 1
        late_at = {x: n for n, x in enumerate(
            x for x in TAIL if x[0] in ("s", "pturn") or x[0] == "stat" and x[1] == 1) if n < len(late_weights())}

        block = ctx.enter_context(nc.Block())

        @block.sync
        def _(sp):
            for j, c in enumerate(CHUNKS):
                s = j % RING_CODES
                if c == ("o", 3):
                    sp.dma_start(xs[:, :, :], xT).then_inc(x_in, 16)
                if c == ("k", 1):
                    sp.dma_start(bgu_raw[:, :, :], loB_gu).then_inc(bgu_in, 16)
                    sp.dma_start(a4_raw[:, :, :], loA_gu).then_inc(a4_in, 16)
                if c == ("k", 2):
                    sp.dma_start(la_d[:, :], loA_d).then_inc(lorad_in, 16)
                    sp.dma_start(lb_d[:, :], loB_d).then_inc(lorad_in, 16)
                if c == ("g", 3):
                    sp.wait_ge(x1_ready, NB * KT)
                    sp.dma_start(la_f[:, :], loA_f).then_inc(loraf_in, 16)
                    sp.dma_start(lb_f[:, :], loB_f).then_inc(loraf_in, 16)
                if j >= RING_CODES:
                    sp.wait_ge(lut_step, 6 * (j - RING_CODES + 1))
                sp.dma_start(code[:, s, :], codes[j]).then_inc(codes_in[s], 16)
                if c in SCALED:
                    i = SCALED.index(c)
                    if i >= RING_CODES:
                        before = CHUNKS.index(SCALED[i - RING_CODES])
                        sp.wait_ge(weight_ready, before + 1)
                    src = scales[i].unsqueeze(1).to_broadcast([2, QB, 512])
                    for g in range(2):
                        sp.dma_start(scale[g * QB:(g + 1) * QB, i % RING_CODES, :],
                                     src[g]).then_inc(scale_in[i % RING_CODES], 16)
            sp.wait_ge(unit_ready, 2 * NF)
            sp.wait_ge(lora_ready, len(MERGED))
            sp.dma_start(wqkv_raw[:, :, :], w_qkv).then_inc(attn_in, 16)
            sp.dma_start(wout_raw[:, :], w_o).then_inc(attn_in, 16)
            sp.dma_start(br_qkv[:, :], b_qkv).then_inc(attn_in, 16)
            sp.dma_start(wr[:, :, :], w_r).then_inc(attn_in, 16)
            sp.dma_start(ea_raw[:, :, :], ex_A).then_inc(ea_in, 16)
            sp.wait_ge(hhi_done, 2 * NF)
            sp.wait_ge(hlo_done, 2 * NF)
            sp.dma_start(bo_rows[:, :], b_o.to_broadcast([P, H])).then_inc(bo_in, 16)
            sp.wait_ge(down_ready, TT * len(GROUPS))
            sp.dma_start(eb_raw[:, :, :], ex_B).then_inc(eb_in, 16)
            for t in range(TT):
                sp.wait_ge(norm_done, norm_no[(3, t)] + 1)
                sp.dma_start(out[t * P:(t + 1) * P, :], rows[:, t, :]).then_inc(out_done, 16)
            sp.wait_ge(out_done, 16 * TT)

        @block.gpsimd
        def _(pool):
            pool.memset(neg_half[:, :], -0.5).then_inc(neg_half_set, 1)
            mults = 0
            for item in V:
                kind = item[0]
                if kind == "lut":
                    c = item[1]
                    j = CHUNKS.index(c)
                    w = wf[:, j % RING_W, :]
                    pool.wait_ge(lut_step, 6 * (j + 1))
                    if j >= RING_W:
                        before = [x for x in CHUNKS[:j - RING_W + 1] if x in SPLIT]
                        if before:
                            pool.wait_ge(lo_done, split_no(before[-1]))
                        pool.wait_ge(weight_ready, j)
                    pool.tensor_tensor(w, halves[:, j % 2, 0, :], halves[:, j % 2, 1, :],
                                       ALU.subtract).then_inc(diff_done, 1)
                    pool.wait_ge(diff_done, j + 1)
                    done = mult_done if c[0] in "kv" else weight_ready
                    mults += c[0] in "kv"
                    if c in SCALED:
                        i = SCALED.index(c)
                        pool.wait_ge(scale_in[i % RING_CODES], 32 * (i // RING_CODES + 1))
                        pool.tensor_tensor(w, w, scale[:, i % RING_CODES, :], ALU.mult).then_inc(done, 1)
                    else:
                        pool.wait_ge(sqkv_in, 16)
                        wv = w.rearrange("p (b e) -> p b e", e=QB)
                        sv = sc_qkv[:, "qkv".index(c[0]) * KT + c[1], :].unsqueeze(2)
                        pool.tensor_tensor(wv, wv, sv.to_broadcast([P, H // QB, QB]), ALU.mult)\
                            .then_inc(done, 1)
                    if c[0] in "kv":
                        pool.wait_ge(mult_done, mults)
                        pool.wait_ge(weight_ready, j)
                        pool.tensor_tensor(w, w, wf[:, (j - 1) % RING_W, :], ALU.add)\
                            .then_inc(weight_ready, 1)
                elif kind == "split":
                    c = item[1]
                    hi, lo = dest(c)
                    pool.wait_ge(hi_done, split_no(c))
                    w = wf[:, CHUNKS.index(c) % RING_W, :]
                    pool.tensor_tensor(lo, shaped(c, w), hi.bitcast(F32), ALU.subtract).then_inc(lo_done, 1)
                elif kind == "h":
                    n = item[1]
                    f, b = n // NB, n % NB
                    hs = slice(b * SEQ, (b + 1) * SEQ)
                    pool.wait_ge(hhi_done, n + 1)
                    pool.tensor_tensor(h_lo[:, f % RING_H, hs], act_f[:, n % 2, :],
                                       h_hi[:, f % RING_H, hs].bitcast(F32), ALU.subtract).then_inc(hlo_done, 1)
            def late(item):
                if item in late_at:
                    raw, hi, lo, _, _ = late_weights()[late_at[item]]
                    pool.wait_ge(whi_done, late_at[item] + 1)
                    pool.tensor_tensor(lo, raw, hi.bitcast(F32), ALU.subtract).then_inc(wlo_done, 1)

            for item in TAIL:
                if item[0] == "stat":
                    i = stat_no[item[1:]]
                    pool.wait_ge(neg_half_set, 1)
                    pool.wait_ge(var_ready, i + 1)
                    s = i % RING_LN
                    if i >= RING_LN:
                        pool.wait_ge(norm_done, slot_normed(i))
                    pool.tensor_tensor(rstd[:, s:s + 1], veps[:, s:s + 1], neg_half[:, :], ALU.pow)\
                        .then_inc(rstd_ready, 1)
                    pool.wait_ge(rstd_ready, i + 1)
                    pool.tensor_scalar(nbias[:, s:s + 1], mv[:, s, 0:1], rstd[:, s:s + 1], -1.0, ALU.mult, ALU.mult)\
                        .then_inc(nbias_ready, 1)
                elif item[0] == "s":
                    t = TPB * item[1] + item[2]
                    pool.wait_ge(bo_in, 16)
                    pool.wait_ge(turn_ready, turn_no[("turn", 1, t)] + 1)
                    pool.tensor_tensor(rows[:, t, :], rows[:, t, :], bo_rows[:, :], ALU.add)\
                        .then_inc(bo_added, 1)
                late(item)

        @block.scalar
        def _(act):
            act.dma_start(sc_qkv[:, :, :], scales_qkv).then_inc(sqkv_in, 16)
            act.dma_start(ident[:, :], eye).then_inc(eye_in, 16)
            act.dma_start(la_o[:, :], loA_o).then_inc(lora_in, 16)
            act.dma_start(lb_o[:, :], loB_o).then_inc(lora_in, 16)
            act.dma_start(la_qkv[:, :], loA_qkv).then_inc(lora_in, 16)
            act.dma_start(lb_qkv[:, :], loB_qkv).then_inc(lora_in, 16)

            def copy(dst, src, done):
                nc.scalar.activation(dst, src, ACT.Copy).then_inc(done, 1)

            for item in V:
                kind = item[0]
                if kind == "lut":
                    c = item[1]
                    j = CHUNKS.index(c)
                    src = code[:, j % RING_CODES, :]
                    act.wait_ge(codes_in[j % RING_CODES], 16 * (j // RING_CODES + 1))
                    steps = [(h[2][0], h[2][1] - h[3][1], ACT.Identity) for h in (UPPER, LOWER)]
                    steps += [(h[0][0], h[0][1], ACT.Relu) for h in (UPPER, LOWER)]
                    steps += [(h[1][0], h[1][1], ACT.Identity) for h in (UPPER, LOWER)]
                    for i, (slope, start, func) in enumerate(steps):
                        m = 6 * j + i
                        if m >= RING_PLANE:
                            act.wait_ge(lut_step, m - RING_PLANE + 1)
                        nc.scalar.activation(plane[m % RING_PLANE][:, :], src, func, bias=float(start),
                                             scale=float(slope)).then_inc(plane_ready, 1)
                elif kind == "split":
                    c = item[1]
                    j = CHUNKS.index(c)
                    hi, _ = dest(c)
                    act.wait_ge(weight_ready, j + 1)
                    if c in MERGED:
                        act.wait_ge(lora_added, MERGED.index(c) + 1)
                    if c[0] in "gu" and c[1] == 1:
                        act.wait_ge(lora_ready, 2 * KT)
                    if c[0] in "gu" and c[1] >= RING_GU:
                        act.wait_ge(unit_ready, 2 * (c[1] - RING_GU) + 2)
                    if c[0] == "d" and c[1] == 0:
                        act.wait_ge(m1_ready, KT)
                    if c[0] == "d" and c[1] == RING_H - 1:
                        act.wait_ge(p_ready, NB)
                    if c[0] == "d" and c[1] >= RING_H:
                        act.wait_ge(down_ready, slot_free_down(c[1]))
                    if c[0] == "f":
                        act.wait_ge(down_ready, TT)
                    copy(hi, shaped(c, wf[:, j % RING_W, :]), hi_done)
                elif kind == "xsplit":
                    k, b = item[1] // NB, item[1] % NB
                    act.wait_ge(x_in, 16)
                    copy(x_hi[:, k, b * SEQ:(b + 1) * SEQ], xs[:, k, b * SEQ:(b + 1) * SEQ], xhi_done)
                elif kind == "m1":
                    act.wait_ge(m1_ready, KT)
                    nc.scalar.activation(m1_hi[:, item[1], :], mm_ps[item[1]][:, :], ACT.Copy, scale=1.0 / 3.0)\
                        .then_inc(m1hi_done, 1)
                elif kind == "x1":
                    n = item[1]
                    b, o = n // KT, n % KT
                    act.wait_ge(x1_ready, n + 1)
                    copy(x1_hi[:, o, b * SEQ:(b + 1) * SEQ], mm_ps[n % 4][:, :], x1hi_done)
                elif kind == "bprep":
                    act.wait_ge(bgu_in, 16)
                    act.wait_ge(a4_in, 16)
                    act.wait_ge(weight_ready, 16)
                    copy(bg4[:, :], bgu_raw[:, 0, :], bprep_hi)
                    copy(bu4[:, :], bgu_raw[:, 1, :], bprep_hi)
                    copy(a4_hi[:, :, :], a4_raw[:, :, :], bprep_hi)
                elif kind == "p":
                    b = item[1]
                    act.wait_ge(p_ready, b + 1)
                    copy(p4[:, b * SEQ:(b + 1) * SEQ], mm_ps[b][:, :], phi_done)
                elif kind == "silu":
                    n = item[1]
                    act.wait_ge(gate_ready, n + 1)
                    if n >= 2:
                        act.wait_ge(hlo_done, n - 1)
                    nc.scalar.activation(act_f[:, n % 2, :], unit_ps[2 * n % 3][:, :], ACT.Silu)\
                        .then_inc(silu_done, 1)
                elif kind == "h":
                    n = item[1]
                    f, b = n // NB, n % NB
                    act.wait_ge(h_done, n + 1)
                    if f >= RING_H:
                        act.wait_ge(down_ready, slot_free_down(f))
                    copy(h_hi[:, f % RING_H, b * SEQ:(b + 1) * SEQ], act_f[:, n % 2, :], hhi_done)

            def late(item):
                if item in late_at:
                    raw, hi, lo, arrived, count = late_weights()[late_at[item]]
                    act.wait_ge(arrived, count)
                    act.wait_ge(unit_ready, 2 * NF)
                    act.wait_ge(down_ready, TT * len(GROUPS))
                    copy(hi, raw, whi_done)

            for item in TAIL:
                kind = item[0]
                if kind == "norm":
                    L, t = item[1:]
                    s = stat_no[(L, t)] % RING_LN
                    src = rows_ps[rows_no[("ffn", t)] % 3][:, :] if L == 1 else rows[:, t, :]
                    act.wait_ge(nbias_ready, stat_no[(L, t)] + 1)
                    if L == 0:
                        act.wait_ge(down_added, TT * (len(GROUPS) - 1) + t + 1)
                    if L == 1:
                        act.wait_ge(turn_ready, turn_no[("turn", 0, t)] + 1)
                    if L >= 2:
                        act.wait_ge(res_done, TT * (L - 2) + t + 1)
                    nc.scalar.activation(rows[:, t, :], src, ACT.Identity, bias=nbias[:, s:s + 1],
                                         scale=rstd[:, s:s + 1]).then_inc(norm_done, 1)
                elif kind == "turn":
                    L, t = item[1:]
                    i = turn_no[item]
                    hi = xa_hi if L == 0 else xb_hi
                    act.wait_ge(turn_ready, i + 1)
                    if L == 0:
                        act.wait_ge(lo_done, len(SPLIT))
                    if L == 1:
                        act.wait_ge(down_ready, TT * len(GROUPS))
                    if L == 2:
                        act.wait_ge(qkv_ready, 3 * NB)
                    copy(hi[:, :, t * P:(t + 1) * P],
                         turn_ps[i % 2][:, :].rearrange("p (k c) -> p k c", k=KT), turnhi_done)
                elif kind == "qkv":
                    b, m = item[1:]
                    act.wait_ge(attn_in, 64)
                    act.wait_ge(ffn_ready, TT)
                    if b and m == 2:
                        act.wait_ge(turn_ready, turn_no[("vturn", b - 1)] + 1)
                    dst = (q_hi[:, b, :], k_hi[:, b, :], vT[:, :])[m]
                    act.wait_ge(qkv_ready, 3 * b + m + 1)
                    nc.scalar.activation(dst, qkv_ps[m][:, :], ACT.Identity,
                                         bias=br_qkv[:, m:m + 1]).then_inc(qkvhi_done, 1)
                elif kind == "vturn":
                    b, i = item[1], turn_no[item]
                    act.wait_ge(turn_ready, i + 1)
                    copy(v_hi[:, b, :, :], turn_ps[i % 2][:, :].rearrange("p (k c) -> p k c", k=TPB), turnhi_done)
                elif kind == "s":
                    b, q = item[1:]
                    n = TPB * b + q
                    act.wait_ge(nmax_done, n + 1)
                    if n >= 2:
                        act.wait_ge(turn_ready, turn_no[("pturn", (n - 2) // TPB, (n - 2) % TPB)] + 1)
                    nc.scalar.activation(prob[:, n % 2, :], s_ps[n % 2][:, :], ACT.Exp, scale=ATTN_SCALE,
                                         bias=nmax[:, n:n + 1], accum_out=rsum[:, n:n + 1]).then_inc(exp_done, 1)
                elif kind == "pturn":
                    b, q = item[1:]
                    i = turn_no[item]
                    act.wait_ge(turn_ready, i + 1)
                    act.wait_ge(ffn_ready, TT)
                    if b:
                        act.wait_ge(oT_ready, b)
                    copy(pT_hi[:, :, q * P:(q + 1) * P],
                         turn_ps[i % 2][:, :].rearrange("p (k c) -> p k c", k=TPB), turnhi_done)
                elif kind == "ot":
                    b = item[1]
                    act.wait_ge(oT_ready, b + 1)
                    copy(oT_hi[:, b, :], oT_ps[:, :], oThi_done)
                elif kind == "score":
                    t = item[1]
                    act.wait_ge(top_step, 5 * t + 3)
                    if t >= 2:
                        act.wait_ge(gate_done, t - 1)
                    nc.scalar.activation(gexp[:, t % 2, :], score_ps[:, 0:EXPERTS], ACT.Exp,
                                         bias=gmax[:, t % 2:t % 2 + 1]).then_inc(gexp_done, 1)
                elif kind == "hturn":
                    t, i = item[1], turn_no[item]
                    for c in range(2):
                        act.wait_ge(turn_ready, i + c + 1)
                        if t >= 2 and c == 0:
                            act.wait_ge(mix_ready, t - 1)
                        copy(hgT_hi[:, t % 2, c * 4:(c + 1) * 4, :],
                             turn_ps[(i + c) % 2][:, :].rearrange("p (k c) -> p k c", k=4), turnhi_done)
                late(item)

        @block.tensor
        def _(pe):
            def product(ps, terms, start=True, stop=True):
                last = None
                for i, (ah, al, bh, bl) in enumerate(terms):
                    for n, (a, b) in enumerate(((ah, bh), (ah, bl), (al, bh))):
                        last = nc.tensor.matmul(ps, a, b, start=start and i == 0 and n == 0,
                                                stop=stop and i == len(terms) - 1 and n == 2)
                return last

            def lora(c):
                i = MERGED.index(c)
                if i:
                    pe.wait_ge(lora_added, i)
                kind, k = c
                if kind == "o":
                    a, b = la_o[:, k * P:(k + 1) * P], lb_o[:, :]
                elif kind == "v":
                    a, b = lb_qkv[:, k * P:(k + 1) * P], la_qkv[:, :]
                elif kind == "d":
                    pe.wait_ge(lorad_in, 32)
                    r = slice(32 * (k // 4), 32 * (k // 4) + RANK)
                    a, b = la_d[r, (k % 4) * P:(k % 4 + 1) * P], lb_d[r, :]
                else:
                    pe.wait_ge(loraf_in, 32)
                    a, b = la_f[:, k * P:(k + 1) * P], lb_f[:, :]
                nc.tensor.matmul(lora_ps[:, :], a, b, start=True, stop=True).then_inc(lora_ready, 1)

            pe.wait_ge(lora_in, 64)
            for c in MERGED[:KT + 1]:
                lora(c)
            pe.wait_ge(eye_in, 16)
            for k in range(KT):
                pe.wait_ge(hi_done, split_no(("v", k)))
                pe.wait_ge(lo_done, split_no(("v", k)))
                for i in range(KT):
                    cut = slice(i * P, (i + 1) * P)
                    last = product(mm_ps[i][:, :], [(wq_hi[:, k, cut], wq_lo[:, k, cut],
                                                     wo_hi[:, k, :], wo_lo[:, k, :])],
                                   start=k == 0, stop=k == KT - 1)
                    if k == 0:
                        for _ in range(3):
                            nc.tensor.matmul(mm_ps[i][:, cut], ident[:, :], ident[:, :], start=False, stop=False)
                    if k == KT - 1:
                        last.then_inc(m1_ready, 1)
                if k < KT - 1:
                    lora(("v", k + 1))
            pe.wait_ge(m1hi_done, KT)
            pe.wait_ge(m1lo_done, KT)
            pe.wait_ge(xhi_done, 2 * KT)
            pe.wait_ge(xlo_done, 2 * KT)
            for n in range(NB * KT):
                b, o = n // KT, n % KT
                if n >= 4:
                    pe.wait_ge(x1hi_done, n - 3)
                    pe.wait_ge(xs_done, n - 3)
                cut, tk = slice(o * P, (o + 1) * P), slice(b * SEQ, (b + 1) * SEQ)
                product(mm_ps[n % 4][:, :], [(m1_hi[:, k, cut], m1_lo[:, k, cut], x_hi[:, k, tk], x_lo[:, k, tk])
                                             for k in range(KT)]).then_inc(x1_ready, 1)
            pe.wait_ge(bprep_done, 3)
            for b in range(NB):
                pe.wait_ge(x1hi_done, NB * KT)
                pe.wait_ge(x1lo_done, NB * KT)
                pe.wait_ge(xs_done, NB * KT)
                tk = slice(b * SEQ, (b + 1) * SEQ)
                product(mm_ps[b][:, :], [(a4_hi[:, k, :], a4_lo[:, k, :], x1_hi[:, k, tk], x1_lo[:, k, tk])
                                         for k in range(KT)]).then_inc(p_ready, 1)

            def unit(n, g):
                f, b = n // NB, n % NB
                m = 2 * n + g
                tk = slice(b * SEQ, (b + 1) * SEQ)
                if m < 3:
                    pe.wait_ge(phi_done, NB)
                    pe.wait_ge(plo_done, NB)
                elif g == 0:
                    pe.wait_ge(h_done, n - 1)
                else:
                    pe.wait_ge(silu_done, n)
                pe.wait_ge(hi_done, split_no(("gu"[g], f)))
                pe.wait_ge(lo_done, split_no(("gu"[g], f)))
                s, ps = f % RING_GU, unit_ps[m % 3][:, :]
                product(ps, [(gu_hi[:, s, g, k, :], gu_lo[:, s, g, k, :], x1_hi[:, k, tk], x1_lo[:, k, tk])
                             for k in range(KT)], stop=False)
                nc.tensor.matmul(ps, (bg4, bu4)[g][:, f * P:(f + 1) * P], p4[:, tk], start=False, stop=True)\
                    .then_inc((gate_ready, unit_ready)[g], 1)

            def down(gi, t):
                n = gi * TT + t
                last_f = GROUPS[gi][-1]
                if gi == len(GROUPS) - 1 and t == 1:
                    pe.wait_ge(h_done, 2 * NF)
                elif gi == len(GROUPS) - 1 and t > 1:
                    pe.wait_ge(down_added, n - 1)
                elif n:
                    pe.wait_ge(down_added, n)
                pe.wait_ge(hhi_done, 2 * last_f + 2)
                pe.wait_ge(hlo_done, 2 * last_f + 2)
                pe.wait_ge(hi_done, split_no(("d", last_f)))
                pe.wait_ge(lo_done, split_no(("d", last_f)))
                tk = slice(t * P, (t + 1) * P)
                ps = down_bank(gi, t)
                last = product(ps[:, :], [(h_hi[:, f % RING_H, tk], h_lo[:, f % RING_H, tk],
                                           wd_hi[:, f % RING_H, :], wd_lo[:, f % RING_H, :])
                                          for f in GROUPS[gi]], stop=gi > 0)
                if gi == 0:
                    pe.wait_ge(eye_in, 16)
                    for k in range(KT):
                        last = nc.tensor.matmul(ps[:, k * P:(k + 1) * P], xs[:, k, tk], ident[:, :],
                                                start=False, stop=k == KT - 1)
                last.then_inc(down_ready, 1)

            for item in T:
                if item[0] == "lora":
                    lora(item[1])
                elif item[0] == "down":
                    down(item[1], item[2])
                else:
                    unit(item[1], item[0] == "up")

            def turn(ps, src):
                for k in range(4):
                    last = nc.tensor.transpose(ps[:, k * P:(k + 1) * P], src[:, k * P:(k + 1) * P], ident[:, :])
                return last

            def turn_free(i):
                if i >= 2:
                    pe.wait_ge(turnlo_done, i - 1)
                else:
                    pe.wait_ge(lut_step, 6 * NJ)

            def rows_wait(i):
                if i < 3:
                    pe.wait_ge(lut_step, 6 * NJ)
                    pe.wait_ge(h_done, 2 * NF)
                    pe.wait_ge(down_added, TT * (len(GROUPS) - 1))
                else:
                    s, v = rows_free(i)
                    pe.wait_ge(s, v)

            for item in TAIL:
                kind = item[0]
                if kind == "down":
                    down(item[1], item[2])
                elif kind == "turn":
                    L, t = item[1:]
                    i = turn_no[item]
                    turn_free(i)
                    pe.wait_ge(norm_done, norm_no[(L, t)] + 1)
                    turn(turn_ps[i % 2], rows[:, t, :]).then_inc(turn_ready, 1)
                elif kind == "ffn":
                    t = item[1]
                    rows_wait(rows_no[item])
                    pe.wait_ge(turnlo_done, turn_no[("turn", 0, t)] + 1)
                    pe.wait_ge(turnhi_done, turn_no[("turn", 0, t)] + 1)
                    pe.wait_ge(hi_done, len(SPLIT))
                    pe.wait_ge(lo_done, len(SPLIT))
                    tk = slice(t * P, (t + 1) * P)
                    product(rows_ps[rows_no[item] % 3][:, :],
                            [(xa_hi[:, k, tk], xa_lo[:, k, tk], wff_hi[:, k, :], wff_lo[:, k, :])
                             for k in range(KT)]).then_inc(ffn_ready, 1)
                elif kind == "qkv":
                    b, m = item[1:]
                    pe.wait_ge(turnlo_done, turn_no[("turn", 1, TPB * b + TPB - 1)] + 1)
                    pe.wait_ge(wlo_done, N_ATTN)
                    pe.wait_ge(norm_done, norm_no[(1, TT - 1)] + 1)
                    pe.wait_ge(lora_added, len(MERGED))
                    if b:
                        pe.wait_ge(qkvhi_done, 3 * (b - 1) + m + 1)
                        pe.wait_ge(qklo_done, min(2 * (b - 1) + m + 1, 2 * b))
                    tk = slice(b * SEQ, (b + 1) * SEQ)
                    cut = slice(m * HD, (m + 1) * HD)
                    product(qkv_ps[m][:, :], [(wqkv_hi[:, k, cut], wqkv_lo[:, k, cut],
                                               xb_hi[:, k, tk], xb_lo[:, k, tk])
                                              for k in range(KT)]).then_inc(qkv_ready, 1)
                elif kind == "vturn":
                    b, i = item[1], turn_no[item]
                    turn_free(i)
                    pe.wait_ge(qkvhi_done, 3 * b + 3)
                    turn(turn_ps[i % 2], vT).then_inc(turn_ready, 1)
                elif kind == "s":
                    b, q = item[1:]
                    n = TPB * b + q
                    pe.wait_ge(qkvhi_done, 3 * b + 2)
                    pe.wait_ge(qklo_done, 2 * b + 2)
                    pe.wait_ge(down_added, TT * len(GROUPS))
                    if n >= 2:
                        pe.wait_ge(exp_done, n - 1)
                    cut = slice(q * P, (q + 1) * P)
                    product(s_ps[n % 2][:, :], [(q_hi[:, b, cut], q_lo[:, b, cut], k_hi[:, b, :], k_lo[:, b, :])])\
                        .then_inc(s_ready, 1)
                elif kind == "pturn":
                    b, q = item[1:]
                    n, i = TPB * b + q, turn_no[item]
                    turn_free(i)
                    pe.wait_ge(exp_done, n + 1)
                    turn(turn_ps[i % 2], prob[:, n % 2, :]).then_inc(turn_ready, 1)
                elif kind == "ot":
                    b = item[1]
                    i = turn_no[("pturn", b, TPB - 1)]
                    pe.wait_ge(turnhi_done, i + 1)
                    pe.wait_ge(turnlo_done, i + 1)
                    pe.wait_ge(qkvhi_done, 3 * NB)
                    pe.wait_ge(qklo_done, 2 * NB)
                    if b:
                        pe.wait_ge(oTlo_done, b)
                    product(oT_ps[:, :], [(v_hi[:, b, k, :], v_lo[:, b, k, :], pT_hi[:, k, :], pT_lo[:, k, :])
                                          for k in range(TPB)]).then_inc(oT_ready, 1)
                elif kind == "wo":
                    t = item[1]
                    b = t // TPB
                    rows_wait(rows_no[item])
                    pe.wait_ge(oThi_done, b + 1)
                    pe.wait_ge(oTlo_done, b + 1)
                    cut = slice((t % TPB) * P, (t % TPB + 1) * P)
                    product(rows_ps[rows_no[item] % 3][:, :],
                            [(oT_hi[:, b, cut], oT_lo[:, b, cut], wout_hi[:, :], wout_lo[:, :])]).then_inc(wo_ready, 1)
                elif kind == "score":
                    t = item[1]
                    i = turn_no[("turn", 2, t)]
                    pe.wait_ge(turnhi_done, i + 1)
                    pe.wait_ge(turnlo_done, i + 1)
                    pe.wait_ge(attn_in, 64)
                    pe.wait_ge(oTlo_done, NB)
                    if t:
                        pe.wait_ge(gate_done, t)
                    tk = slice(t * P, (t + 1) * P)
                    for n, (part, k) in enumerate((part, k) for part in (xb_hi, xb_lo) for k in range(KT)):
                        last = nc.tensor.matmul(score_ps[:, 0:EXPERTS], part[:, k, tk].bitcast(F32),
                                                wr[:, k, :], start=n == 0, stop=n == 2 * KT - 1)
                    last.then_inc(score_ready, 1)
                elif kind == "h":
                    t = item[1]
                    tk = slice(t * P, (t + 1) * P)
                    pe.wait_ge(exp_done, TT)
                    pe.wait_ge(wlo_done, N_ATTN + N_EA)
                    for c in range(2):
                        if t:
                            pe.wait_ge(hg_done, 2 * (t - 1) + c + 1)
                        cut = slice(c * 512, (c + 1) * 512)
                        product(hid_ps[c][:, :], [(xb_hi[:, k, tk], xb_lo[:, k, tk], ea_hi[:, k, cut], ea_lo[:, k, cut])
                                                  for k in range(KT)]).then_inc(hid_ready, 1)
                elif kind == "hturn":
                    t, i = item[1], turn_no[item]
                    for c in range(2):
                        turn_free(i + c)
                        pe.wait_ge(hg_done, 2 * t + c + 1)
                        turn(turn_ps[(i + c) % 2], hg[:, t % 2, c * 512:(c + 1) * 512]).then_inc(turn_ready, 1)
                elif kind == "mix":
                    t = item[1]
                    i = turn_no[("hturn", t)]
                    rows_wait(rows_no[item])
                    pe.wait_ge(turnhi_done, i + 2)
                    pe.wait_ge(turnlo_done, i + 2)
                    pe.wait_ge(wlo_done, len(late_weights()))
                    product(rows_ps[rows_no[item] % 3][:, :],
                            [(hgT_hi[:, t % 2, m, :], hgT_lo[:, t % 2, m, :], eb_hi[:, m, :], eb_lo[:, m, :])
                             for m in range(ER // P)]).then_inc(mix_ready, 1)

        @block.vector
        def _(dve):
            eye_mids = 0
            for g in range(4):
                dve.memset(low_rows[32 * g:32 * g + 32, :], -float(g % 2)).then_inc(low_rows_set, 1)

            def low(dst, src, hi, done):
                nc.vector.tensor_tensor(dst, src, hi.bitcast(F32), ALU.subtract).then_inc(done, 1)

            for item in V:
                kind = item[0]
                if kind == "lut":
                    c = item[1]
                    j = CHUNKS.index(c)
                    src = code[:, j % RING_CODES, :]
                    dve.wait_ge(codes_in[j % RING_CODES], 16 * (j // RING_CODES + 1))
                    for i in range(6):
                        m, side = 6 * j + i, i % 2
                        lines = (UPPER, LOWER)[side]
                        ps, acc = plane[m % RING_PLANE][:, :], half[:, side, :]
                        dve.wait_ge(plane_ready, m + 1)
                        if m >= 2:
                            dve.wait_ge(lut_step, m - 1)
                        if i < 2:
                            ins = nc.vector.scalar_tensor_tensor(acc, src, float(lines[3][0]), ps, ALU.mult, ALU.max)
                        elif i < 4:
                            ins = nc.vector.scalar_tensor_tensor(acc, acc, float(lines[3][1]), ps, ALU.add, ALU.max)
                        else:
                            if j >= 2:
                                dve.wait_ge(diff_done, j - 1)
                            ins = nc.vector.tensor_tensor(halves[:, j % 2, side, :], acc, ps, ALU.max)
                        ins.then_inc(lut_step, 1)
                elif kind == "split" and item[1] in MERGED:
                    c = item[1]
                    j, i = CHUNKS.index(c), MERGED.index(c)
                    w = wf[:, j % RING_W, :]
                    dve.wait_ge(weight_ready, j + 1)
                    dve.wait_ge(lora_ready, i + 1)
                    if c[0] != "f":
                        nc.vector.tensor_tensor(w, lora_ps[:, :], w, ALU.add).then_inc(lora_added, 1)
                    else:
                        eye_mids += 1
                        nc.vector.scalar_tensor_tensor(w, lora_ps[:, :], LORA_SCALE, w, ALU.mult, ALU.add)\
                            .then_inc(eye_mid, 1)
                        dve.wait_ge(eye_mid, eye_mids)
                        d = w[:, c[1] * P:(c[1] + 1) * P]
                        nc.vector.tensor_tensor(d, d, ident[:, :], ALU.add).then_inc(lora_added, 1)
                elif kind == "xsplit":
                    k, b = item[1] // NB, item[1] % NB
                    tk = slice(b * SEQ, (b + 1) * SEQ)
                    dve.wait_ge(xhi_done, item[1] + 1)
                    low(x_lo[:, k, tk], xs[:, k, tk], x_hi[:, k, tk], xlo_done)
                elif kind == "m1":
                    i = item[1]
                    dve.wait_ge(m1hi_done, i + 1)
                    nc.vector.scalar_tensor_tensor(m1_lo[:, i, :], mm_ps[i][:, :], 1.0 / 3.0,
                                                   m1_hi[:, i, :].bitcast(F32), ALU.mult, ALU.subtract)\
                        .then_inc(m1lo_done, 1)
                elif kind == "x1":
                    n = item[1]
                    b, o = n // KT, n % KT
                    tk = slice(b * SEQ, (b + 1) * SEQ)
                    dve.wait_ge(x1hi_done, n + 1)
                    dve.wait_ge(xlo_done, 2 * KT)
                    low(x1_lo[:, o, tk], mm_ps[n % 4][:, :], x1_hi[:, o, tk], x1lo_done)
                    nc.vector.tensor_tensor(xs[:, o, tk], mm_ps[n % 4][:, :], xs[:, o, tk], ALU.add)\
                        .then_inc(xs_done, 1)
                elif kind == "bprep":
                    dve.wait_ge(bprep_hi, 3)
                    dve.wait_ge(low_rows_set, 4)
                    for g, b4 in enumerate((bg4, bu4)):
                        nc.vector.scalar_tensor_tensor(b4[:, :], b4[:, :].bitcast(F32), low_rows[:, :],
                                                       bgu_raw[:, g, :], ALU.mult, ALU.add)\
                            .then_inc(bprep_done, 1)
                    low(a4_lo[:, :, :], a4_raw[:, :, :], a4_hi[:, :, :], bprep_done)
                elif kind == "p":
                    b = item[1]
                    tk = slice(b * SEQ, (b + 1) * SEQ)
                    dve.wait_ge(phi_done, b + 1)
                    low(p4[64:128, tk], mm_ps[b][64:128, :], p4[64:128, tk], plo_done)
                elif kind == "h":
                    n = item[1]
                    a = act_f[:, n % 2, :]
                    dve.wait_ge(silu_done, n + 1)
                    dve.wait_ge(unit_ready, n + 1)
                    nc.vector.tensor_tensor(a, a, unit_ps[(2 * n + 1) % 3][:, :], ALU.mult).then_inc(h_done, 1)
                elif kind == "down":
                    gi, t = item[1:]
                    n = gi * TT + t
                    dve.wait_ge(down_ready, n + 1)
                    if gi == 0:
                        dve.wait_ge(bprep_done, 3)
                        nc.vector.tensor_copy(rows[:, t, :], down_bank(gi, t)[:, :]).then_inc(down_added, 1)
                    else:
                        dve.wait_ge(down_added, (gi - 1) * TT + t + 1)
                        nc.vector.tensor_tensor(rows[:, t, :], down_bank(gi, t)[:, :], rows[:, t, :], ALU.add)\
                            .then_inc(down_added, 1)

            for item in TAIL:
                kind = item[0]
                if kind == "down":
                    gi, t = item[1:]
                    n = gi * TT + t
                    dve.wait_ge(down_ready, n + 1)
                    dve.wait_ge(down_added, (gi - 1) * TT + t + 1)
                    nc.vector.tensor_tensor(rows[:, t, :], down_bank(gi, t)[:, :], rows[:, t, :], ALU.add)\
                        .then_inc(down_added, 1)
                elif kind == "stat":
                    L, t = item[1:]
                    i = stat_no[(L, t)]
                    s = i % RING_LN
                    src = rows[:, t, :]
                    if L == 0:
                        dve.wait_ge(down_added, TT * (len(GROUPS) - 1) + t + 1)
                    elif L == 1:
                        dve.wait_ge(ffn_ready, t + 1)
                        src = rows_ps[rows_no[("ffn", t)] % 3][:, :]
                    elif L == 2:
                        dve.wait_ge(res_done, t + 1)
                    else:
                        dve.wait_ge(mix_ready, t + 1)
                        nc.vector.scalar_tensor_tensor(src, rows_ps[rows_no[("mix", t)] % 3][:, :], EXPERT_SCALE,
                                                       src, ALU.mult, ALU.add).then_inc(res_done, 1)
                        dve.wait_ge(res_done, TT + t + 1)
                    nc.vector.bn_stats(bn6[:, s, :], src).then_inc(bn_step, 1)
                    dve.wait_ge(bn_step, 2 * i + 1)
                    if i >= RING_LN:
                        dve.wait_ge(norm_done, slot_normed(i))
                    nc.vector.bn_aggr(mv[:, s, :], bn6[:, s, :]).then_inc(bn_step, 1)
                    dve.wait_ge(bn_step, 2 * i + 2)
                    if i >= RING_LN:
                        dve.wait_ge(rstd_ready, i - RING_LN + 1)
                    nc.vector.tensor_scalar(veps[:, s:s + 1], mv[:, s, 1:2], EPS, None, ALU.add)\
                        .then_inc(var_ready, 1)
                elif kind == "turn":
                    L, t = item[1:]
                    i = turn_no[item]
                    hi, lo = (xa_hi, xa_lo) if L == 0 else (xb_hi, xb_lo)
                    dve.wait_ge(turnhi_done, i + 1)
                    tk = slice(t * P, (t + 1) * P)
                    low(lo[:, :, tk], turn_ps[i % 2][:, :].rearrange("p (k c) -> p k c", k=KT), hi[:, :, tk],
                        turnlo_done)
                elif kind == "qkv":
                    b, m = item[1:]
                    if m < 2:
                        hi, lo = ((q_hi, q_lo), (k_hi, k_lo))[m]
                        dve.wait_ge(qkvhi_done, 3 * b + m + 1)
                        nc.vector.scalar_tensor_tensor(lo[:, b, :], qkv_ps[m][:, :], br_qkv[:, m:m + 1],
                                                       hi[:, b, :].bitcast(F32), ALU.add, ALU.subtract)\
                            .then_inc(qklo_done, 1)
                elif kind == "vturn":
                    b, i = item[1], turn_no[item]
                    dve.wait_ge(turnhi_done, i + 1)
                    low(v_lo[:, b, :, :], turn_ps[i % 2][:, :].rearrange("p (k c) -> p k c", k=TPB),
                        v_hi[:, b, :, :], turnlo_done)
                elif kind == "s":
                    b, q = item[1:]
                    n = TPB * b + q
                    dve.wait_ge(s_ready, n + 1)
                    nc.vector.reduce_max(rmax[:, n:n + 1], s_ps[n % 2][:, :], AX_X).then_inc(max_done, 1)
                    dve.wait_ge(max_done, n + 1)
                    nc.vector.tensor_scalar(nmax[:, n:n + 1], rmax[:, n:n + 1], -ATTN_SCALE, None, ALU.mult)\
                        .then_inc(nmax_done, 1)
                elif kind == "pturn":
                    b, q = item[1:]
                    n, i = TPB * b + q, turn_no[item]
                    dve.wait_ge(exp_done, n + 1)
                    nc.vector.reciprocal(rinv[:, n:n + 1], rsum[:, n:n + 1]).then_inc(rinv_done, 1)
                    dve.wait_ge(turnhi_done, i + 1)
                    cut = slice(q * P, (q + 1) * P)
                    low(pT_lo[:, :, cut], turn_ps[i % 2][:, :].rearrange("p (k c) -> p k c", k=TPB),
                        pT_hi[:, :, cut], turnlo_done)
                elif kind == "ot":
                    b = item[1]
                    dve.wait_ge(oThi_done, b + 1)
                    low(oT_lo[:, b, :], oT_ps[:, :], oT_hi[:, b, :], oTlo_done)
                elif kind == "wo":
                    t = item[1]
                    dve.wait_ge(wo_ready, t + 1)
                    dve.wait_ge(rinv_done, t + 1)
                    dve.wait_ge(bo_added, t + 1)
                    nc.vector.scalar_tensor_tensor(rows[:, t, :], rows_ps[rows_no[item] % 3][:, :],
                                                   rinv[:, t:t + 1], rows[:, t, :], ALU.mult, ALU.add)\
                        .then_inc(res_done, 1)
                elif kind == "score":
                    t = item[1]
                    s, sc = t % 2, score_ps[:, 0:EXPERTS]
                    dve.wait_ge(score_ready, t + 1)
                    nc.vector.max(top8[:, s, 0, :], sc).then_inc(top_step, 1)
                    dve.wait_ge(top_step, 5 * t + 1)
                    if t >= 2:
                        dve.wait_ge(gexp_done, t - 1)
                    nc.vector.tensor_scalar(gmax[:, s:s + 1], top8[:, s, 0, 0:1], -1.0, None, ALU.mult)\
                        .then_inc(top_step, 1)
                    nc.vector.match_replace(left1[:, s, :], top8[:, s, 0, :], sc, TAKEN).then_inc(top_step, 1)
                    dve.wait_ge(top_step, 5 * t + 3)
                    nc.vector.max(top8[:, s, 1, :], left1[:, s, :]).then_inc(top_step, 1)
                    dve.wait_ge(top_step, 5 * t + 4)
                    nc.vector.match_replace(left2[:, s, :], top8[:, s, 1, :], left1[:, s, :], TAKEN)\
                        .then_inc(top_step, 1)
                    dve.wait_ge(top_step, 5 * t + 5)
                    dve.wait_ge(gexp_done, t + 1)
                    nc.vector.scalar_tensor_tensor(gate[:, s, :], left2[:, s, :], TAKEN, gexp[:, s, :],
                                                   ALU.is_equal, ALU.mult, accum_out=gsum[:, s:s + 1])\
                        .then_inc(gsum_done, 1)
                    dve.wait_ge(gsum_done, t + 1)
                    nc.vector.reciprocal(ginv[:, s:s + 1], gsum[:, s:s + 1]).then_inc(ginv_done, 1)
                    dve.wait_ge(ginv_done, t + 1)
                    nc.vector.tensor_scalar(gate[:, s, :], gate[:, s, :], ginv[:, s:s + 1], None, ALU.mult)\
                        .then_inc(gate_done, 1)
                elif kind == "h":
                    t = item[1]
                    dve.wait_ge(gate_done, t + 1)
                    if t >= 2:
                        dve.wait_ge(turn_ready, turn_no[("hturn", t - 2)] + 2)
                    for c in range(2):
                        dve.wait_ge(hid_ready, 2 * t + c + 1)
                        g = gate[:, t % 2, c * EPC:(c + 1) * EPC].unsqueeze(2).to_broadcast([P, EPC, ERANK])
                        nc.vector.tensor_tensor(
                            hg[:, t % 2, c * 512:(c + 1) * 512].rearrange("p (e r) -> p e r", r=ERANK),
                            hid_ps[c][:, :].rearrange("p (e r) -> p e r", r=ERANK), g, ALU.mult)\
                            .then_inc(hg_done, 1)
                elif kind == "hturn":
                    t, i = item[1], turn_no[item]
                    for c in range(2):
                        dve.wait_ge(turnhi_done, i + c + 1)
                        low(hgT_lo[:, t % 2, c * 4:(c + 1) * 4, :],
                            turn_ps[(i + c) % 2][:, :].rearrange("p (k c) -> p k c", k=4),
                            hgT_hi[:, t % 2, c * 4:(c + 1) * 4, :], turnlo_done)


def laid_out(a):
    import numpy as np

    def cat(parts):
        return np.ascontiguousarray(np.stack(parts))

    ca, cg, cd, cf = (np.asarray(a[n]) for n in ("L0_attn_codes_attn", "L0_attn_codes_gu", "L0_attn_codes_down",
                                                 "L0_ffn_codes"))
    sa, sg, sd, sf = (np.asarray(a[n]) for n in ("L0_attn_scales_attn", "L0_attn_scales_gu",
                                                 "L0_attn_scales_down", "L0_ffn_absmax"))
    codes, scales = [], []
    for kind, k in CHUNKS:
        cut, blk = slice(k * P, (k + 1) * P), slice(2 * k, 2 * k + 2)
        if kind == "o":
            codes.append(ca[3].T[cut])
            scales.append(sa[3].T[blk])
        elif kind in "qkv":
            codes.append(ca["qkv".index(kind)][cut])
        elif kind in "gu":
            g = "gu".index(kind)
            codes.append(cg[g][cut].reshape(P, KT, P).transpose(2, 1, 0).reshape(P, H))
            scales.append(sg[g][cut].reshape(P, KT, 2).transpose(2, 1, 0).reshape(2, H))
        elif kind == "d":
            codes.append(cd.T[cut])
            scales.append(sd.T[blk])
        else:
            codes.append(cf.T[cut])
            scales.append(sf.T[blk])

    def tiles(m):
        return np.ascontiguousarray(m.reshape(-1, P, m.shape[1]).transpose(1, 0, 2))

    x = np.asarray(a["L0_attn_x"]).reshape(TOK, H)
    Ah, Ad = np.asarray(a["L0_attn_lora_A_h"]), np.asarray(a["L0_attn_lora_A_down"])
    Ba, Bg, Bd = (np.asarray(a[n]) for n in ("L0_attn_lora_B_attn", "L0_attn_lora_B_gu", "L0_attn_lora_B_down"))
    zero = np.zeros((RANK, FF), np.float32)
    la_d = np.zeros((P, 512), np.float32)
    lb_d = np.zeros((P, 512), np.float32)
    for g in range(4):
        part = Ad[:, g * 512:(g + 1) * 512]
        la_d[32 * g:32 * g + RANK, :part.shape[1]] = part
        lb_d[32 * g:32 * g + RANK] = Bd.T
    A4 = np.tile(np.concatenate([Ah[4], Ah[5]]), (4, 1))
    B4 = [np.tile(np.concatenate(rows), (4, 1)) for rows in ((Bg[0].T, zero), (zero, Bg[1].T))]
    eA, eB = np.asarray(a["L1_ffn_A"]), np.asarray(a["L1_ffn_B"])
    named = dict(
        codes=cat(codes), scales=cat(scales),
        scales_qkv=np.ascontiguousarray(sa[:3].reshape(3 * KT, P, H // QB).transpose(1, 0, 2)),
        eye=np.eye(P, dtype=np.float32), xT=tiles(x.T),
        loA_o=Ah[3], loB_o=Ba[3].T, loA_qkv=Ah[:3].reshape(3 * RANK, H),
        loB_qkv=Ba[:3].transpose(0, 2, 1).reshape(3 * RANK, H),
        loA_gu=tiles(A4.T), loB_gu=np.stack(B4, 1), loA_d=la_d, loB_d=lb_d,
        loA_f=np.asarray(a["L0_ffn_lora_A"]), loB_f=np.asarray(a["L0_ffn_lora_B"]).T,
        w_qkv=tiles(np.asarray(a["L1_attn_Wqkv"])),
        b_qkv=np.asarray(a["L1_attn_bqkv"]).reshape(3, HD).T,
        w_o=np.asarray(a["L1_attn_Wo"]), b_o=np.asarray(a["L1_attn_bo"]).reshape(1, H),
        ex_A=tiles(eA.reshape(ER, H).T),
        ex_B=tiles(eB.transpose(0, 2, 1).reshape(ER, H)),
        w_r=tiles(np.asarray(a["L1_ffn_Wr"]).T),
    )
    return {k: np.ascontiguousarray(v) for k, v in named.items()}


def kernel(**inputs):
    import concourse.bacc as bacc
    from concourse.bass_utils import run_bass_kernel_spmd

    arrays = laid_out(inputs)
    nc = bacc.Bacc("TRN2", target_bir_lowering=False, num_devices=1)
    args = {k: nc.dram_tensor(k, v.shape, mybir.dt.from_np(v.dtype), kind="ExternalInput").ap()
            for k, v in arrays.items()}
    out = nc.dram_tensor("out", (TOK, H), F32, kind="ExternalOutput").ap()
    build(nc, out=out, **args)
    result = run_bass_kernel_spmd(nc, [arrays], core_ids=[0])
    return result.results[0]["out"].reshape(NB, SEQ, H)
```

```python
from contextlib import ExitStack

import concourse.bass as bass
from concourse import mybir

P = 128
H = 512
KT = H // P
TOK = 1024
TT = TOK // P
SEQ = 512
NB = TOK // SEQ
TPB = SEQ // P
FF = 1792
NF = FF // P
QB = 64
RANK = 16
FFN_RANK = 64
HD = 128
EXPERTS, TOPK, ERANK = 64, 16, 16
ER = EXPERTS * ERANK
EPC = H // ERANK
LORA_SCALE = 16.0 / 64.0
EXPERT_SCALE = 32.0 / ERANK
EPS = 1e-5
ATTN_SCALE = float(HD) ** -0.5
TAKEN = -3.0e38

F32 = mybir.dt.float32
F32R = mybir.dt.float32r
I32 = mybir.dt.int32
ALU = mybir.AluOpType
ACT = mybir.ActivationFunctionType
AX_X = mybir.AxisListType.X

NF4 = [-1.0, -0.6961928009986877, -0.5250730514526367, -0.39491748809814453, -0.28444138169288635,
       -0.18477343022823334, -0.09105003625154495, 0.0, 0.07958029955625534, 0.16093020141124725,
       0.24611230194568634, 0.33791524171829224, 0.44070982933044434, 0.5626170039176941,
       0.7229568362236023, 1.0]


def line(sign, a, b):
    slope = sign * (NF4[b] - NF4[a]) / (b - a)
    return slope, sign * NF4[a] - slope * a


UPPER = [line(1, 8, 9), line(1, 10, 11), line(1, 12, 13), line(1, 14, 15)]
LOWER = [line(-1, 6, 5), line(-1, 4, 3), line(-1, 2, 1), (1.5 * (NF4[0] - NF4[1]), -NF4[0])]

GROUPS = [range(f, f + 2) for f in range(0, NF, 2)]
FFN_AT = {6: 0, 8: 1, 10: 2, 12: 3}


BEATS = {0: [0] * 8, 6: [1, 0, 1, 1, 2, 0, 1, 0], 8: [2, 0, 2, 0, 2, 0, 2, 0]}


def chunk_list():
    chunks = [(m, k) for k in range(KT) for m in "qkvo"]
    chunks += [("g", 0), ("u", 0), ("g", 1), ("u", 1), ("d", 0), ("d", 1)]
    for f in range(1, NF):
        chunks += [(m, f + 1) for m in "gud"] if f + 1 < NF else []
        chunks += [("f", FFN_AT[f])] if f in FFN_AT else []
    return chunks


CHUNKS = chunk_list()
NJ = len(CHUNKS)
MERGED = [c for c in CHUNKS if c[0] in "ovdf"]
SPLIT = [c for c in CHUNKS if c[0] not in "qk"]
SCALED = [c for c in CHUNKS if c[0] not in "qkv"]
RING_CODES = 3
RING_W = 3
RING_PLANE = 3
RING_H = 5
RING_GU = 2
RING_LN = 4


def vector_order():
    order = []

    due = []

    def half(c, part):
        order.append(("lut", c, part))
        for x in due:
            x[0] -= 1
        while due and due[0][0] <= 0:
            order.append(due.pop(0)[1])
        if part == 1:
            if c in MERGED:
                due.append([2, ("merge", c)])
            if c in SPLIT:
                due.append([3 if c in MERGED else 2, ("split", c)])
        due.sort(key=lambda x: x[0])

    def lut(c):
        half(c, 0)
        half(c, 1)

    def flush():
        order.extend(x[1] for x in due)
        due.clear()

    def unit_h(n):
        order.append(("h", n))
        due.insert(0, [1, ("hsplit", n)])

    for j in range(4 * KT):
        lut(CHUNKS[j])
    order.extend(("xsplit", i) for i in range(KT))
    flush()
    half(("g", 0), 0)
    order.extend(("xsplit", i) for i in range(KT, 2 * KT))
    order.extend(("m1", i) for i in range(KT))
    half(("g", 0), 1)
    order.append(("x1", 0))
    half(("u", 0), 0)
    order.append(("x1", 1))
    half(("u", 0), 1)
    order += [("x1", 2), ("bprep", 0), ("x1", 3), ("bprep", 1), ("x1", 4), ("x1", 5), ("bprep", 2),
              ("x1", 6), ("x1", 7)]
    lut(("g", 1))
    order.append(("p", 0))
    half(("u", 1), 0)
    order.append(("p", 1))
    order.append(("dprep", 0))
    half(("u", 1), 1)
    half(("d", 0), 0)
    order.append(("silu", 0))
    half(("d", 0), 1)
    unit_h(0)
    half(("d", 1), 0)
    order.append(("silu", 1))
    half(("d", 1), 1)
    unit_h(1)
    for f in range(1, NF):
        downs = downs_beside(f) + [None] * 4
        ahead = [(m, f + 1) for m in "gud"] if f < NF - 1 else []
        ahead += [("f", FFN_AT[f])] if f in FFN_AT else []
        halves = [(c, part) for c in ahead for part in range(2)]
        steps = (("silu", 2 * f), downs[0], ("h", 2 * f), downs[1], ("silu", 2 * f + 1), downs[2],
                 ("h", 2 * f + 1), downs[3])
        beat = iter(halves)
        for step, count in zip(steps, BEATS[len(halves)]):
            for _ in range(count):
                half(*next(beat))
            if step and step[0] == "h":
                unit_h(step[1])
            elif step:
                order.append(step)
            if f == NF - 1:
                flush()
        for rest in beat:
            half(*rest)
    order.extend(downs_beside(NF))
    return order


def downs_beside(f):
    downs = [("down", g, t) for g in range(len(GROUPS) - 1) for t in range(TT)]
    start = 4 * (f - 2) - 1
    return ([None] if f == 2 else []) + downs[max(start, 0):max(start + 4, 0)]


def tensor_order():
    order = []
    for f in range(NF):
        downs = downs_beside(f)
        for b in range(NB):
            order.append(("gate", 2 * f + b))
            if b == 0 and f < 2:
                order.append(("lora", ("d", f)))
            if b == 0 and f - 1 in FFN_AT:
                order.append(("lora", ("f", FFN_AT[f - 1])))
            order.extend(downs[2 * b:2 * b + 1])
            order.append(("up", 2 * f + b))
            order.extend(downs[2 * b + 1:2 * b + 2])
            if b == 0 and 1 <= f < NF - 1:
                order.append(("lora", ("d", f + 1)))
    return order + downs_beside(NF)


TAIL_ITEMS = """
    norm:0.0 down:6.0 stat:0.0 down:6.1 down:6.2 down:6.3 turn:0.0 stat:0.1 down:6.4 norm:0.1 stat:0.2
    norm:0.2 down:6.5 ffn:0 stat:0.3 turn:0.1 down:6.6 norm:0.3 turn:0.2 stat:1.0 down:6.7 stat:0.4 ffn:1
    norm:1.0 turn:0.3 ffn:2 stat:0.5 norm:0.4 stat:1.1 turn:1.0 stat:0.6 norm:0.5 turn:0.4 norm:1.1 ffn:3
    stat:1.2 stat:1.3 turn:1.1 turn:0.5 ffn:4 stat:0.7 norm:0.6 norm:1.2 turn:0.6 stat:1.4 turn:1.2 norm:0.7
    ffn:5 norm:1.3 stat:1.5 turn:0.7 stat:1.6 turn:1.3 ffn:6 ffn:7 norm:1.4 norm:1.5 turn:1.4 stat:1.7
    turn:1.5 qkv:0.0 norm:1.6 qkv:0.1 turn:1.6 norm:1.7 qkv:0.2 turn:1.7 s:0.0 s:0.1 vturn:0 qkv:1.0
    pturn:0.0 s:0.2 s:0.3 pturn:0.1 qkv:1.1 pturn:0.2 qkv:1.2 pturn:0.3 s:1.0 s:1.1 vturn:1 ot:0 pturn:1.0
    pturn:1.1 s:1.2 s:1.3 wo:0 wo:1 pturn:1.2 pturn:1.3 stat:2.0 stat:2.1 wo:2 wo:3 ot:1 stat:2.2 wo:4
    norm:2.0 stat:2.3 norm:2.1 wo:5 turn:2.0 norm:2.2 wo:6 wo:7 score:0 turn:2.1 h:0.0 turn:2.2 score:1
    norm:2.3 stat:2.4 h:0.1 hturn:0.0 h:1.0 hturn:0.1 turn:2.3 h:1.1 stat:2.5 stat:3.0 mix:0 hturn:1.0
    score:2 hturn:1.1 h:2.0 h:2.1 norm:2.4 score:3 norm:3.0 hturn:2.0 mix:1 hturn:2.1 turn:2.4 norm:2.5
    norm:3.1 h:3.0 mix:2 stat:3.1 stat:2.6 turn:2.5 h:3.1 stat:3.2 score:4 hturn:3.0 norm:2.6 h:4.0
    hturn:3.1 norm:3.2 stat:2.7 h:4.1 turn:2.6 stat:3.3 hturn:4.0 mix:3 score:5 hturn:4.1 norm:2.7 norm:3.3
    h:5.0 h:5.1 score:6 hturn:5.0 turn:2.7 mix:4 hturn:5.1 score:7 h:6.0 h:6.1 mix:5 norm:3.4 stat:3.4
    hturn:6.0 stat:3.5 hturn:6.1 h:7.0 h:7.1 hturn:7.0 hturn:7.1 norm:3.5 stat:3.6 mix:6 norm:3.6 mix:7
    stat:3.7 norm:3.7
"""


def tail_order():
    items = (word.split(":") for word in TAIL_ITEMS.split())
    return [(kind, *map(int, args.split("."))) for kind, args in items]


def build(nc, codes, scales, scales_qkv, eye, down_low, xT, loA_o, loB_o, loA_qkv, loB_qkv, loA_gu, loB_gu,
          loA_d, loB_d, loA_f, loB_f, w_qkv, b_qkv, w_o, b_o, ex_A, ex_B, w_r, out):
    with ExitStack() as ctx:
        bn6 = ctx.enter_context(nc.sbuf_tensor("bn6", [P, RING_LN, 6], F32))
        mv = ctx.enter_context(nc.sbuf_tensor("mv", [P, RING_LN, 2], F32))
        veps = ctx.enter_context(nc.sbuf_tensor("veps", [P, RING_LN], F32))
        rstd = ctx.enter_context(nc.sbuf_tensor("rstd", [P, RING_LN], F32))
        nbias = ctx.enter_context(nc.sbuf_tensor("nbias", [P, RING_LN], F32))
        neg_half = ctx.enter_context(nc.sbuf_tensor("neg_half", [P, 1], F32))
        low_rows = ctx.enter_context(nc.sbuf_tensor("low_rows", [P, 2], F32))
        warm = ctx.enter_context(nc.sbuf_tensor("warm", [P, 1], F32))
        base = (nc.sbuf_base + 63) // 64 * 64

        def at(name, kb, shape, dt=F32):
            return nc.alloc_sbuf_tensor_at(name, shape, dt, offset=base + int(kb * 1024))

        def sem(name):
            return ctx.enter_context(nc.semaphore(name))

        code = at("code", 0, [P, RING_CODES, 512], I32)
        scale = at("scale", 6, [P, RING_CODES, 512])
        half = at("half", 12, [P, 2, 512])
        halves = at("halves", 16, [P, 2, 2, 512])
        wf = at("wf", 24, [P, RING_W, 512])
        act_f = at("act_f", 30, [P, 2, 512])
        xs = at("xs", 34, [P, KT, TOK])
        x_hi = at("x_hi", 50, [P, KT, TOK], F32R)
        x_lo = at("x_lo", 66, [P, KT, TOK], F32R)
        m1_hi = at("m1_hi", 82, [P, KT, H], F32R)
        m1_lo = at("m1_lo", 90, [P, KT, H], F32R)
        h_hi = at("h_hi", 50, [P, RING_H, TOK], F32R)
        h_lo = at("h_lo", 70, [P, RING_H, TOK], F32R)
        rows = at("rows", 98, [P, TT, H])
        bgu_raw = at("bgu_raw", 98, [P, 2, FF])
        a4_raw = at("a4_raw", 112, [P, KT, P])
        wq_hi = at("wq_hi", 146, [P, KT, H], F32R)
        wq_lo = at("wq_lo", 154, [P, KT, H], F32R)
        wo_hi = at("wo_hi", 162, [P, KT, H], F32R)
        wo_lo = at("wo_lo", 170, [P, KT, H], F32R)
        wd_hi = at("wd_hi", 114, [P, RING_H, H], F32R)
        wd_lo = at("wd_lo", 124, [P, RING_H, H], F32R)
        bg4 = at("bg4", 134, [P, FF], F32R)
        p4 = at("p4", 141, [P, TOK], F32R)
        a4_hi = at("a4_hi", 205, [P, KT, P], F32R)
        x1_hi = at("x1_hi", 146, [P, KT, TOK], F32R)
        x1_lo = at("x1_lo", 162, [P, KT, TOK], F32R)
        gu_hi = at("gu_hi", 178, [P, RING_GU, 2, KT, P], F32R)
        gu_lo = at("gu_lo", 186, [P, RING_GU, 2, KT, P], F32R)
        la_o = at("la_o", 182, [RANK, 512])
        lb_o = at("lb_o", 184, [RANK, 512])
        la_qkv = at("la_qkv", 190, [3 * RANK, 512])
        lb_qkv = at("lb_qkv", 192, [3 * RANK, 512])
        bu4 = at("bu4", 194, [P, FF], F32R)
        la_d = at("la_d", 201, [P, 512])
        lb_d = at("lb_d", 203, [P, 512])
        la_dp = at("la_dp", 94, [P, 512], F32R)
        lb_dh = at("lb_dh", 96, [P, 512], F32R)
        lb_dl = at("lb_dl", 205, [P, 512], F32R)
        a4_lo = at("a4_lo", 132, [P, KT, P], F32R)
        ident = at("ident", 207, [P, P])
        la_f = at("la_f", 90, [FFN_RANK, 512])
        lb_f = at("lb_f", 92, [FFN_RANK, 512])
        wff_hi = at("wff_hi", 34, [P, KT, H], F32R)
        wff_lo = at("wff_lo", 42, [P, KT, H], F32R)
        xa_hi = at("xa_hi", 0, [P, KT, TOK], F32R)
        xa_lo = at("xa_lo", 16, [P, KT, TOK], F32R)
        xb_hi = at("xb_hi", 50, [P, KT, TOK], F32R)
        xb_lo = at("xb_lo", 66, [P, KT, TOK], F32R)
        ea_raw = at("ea_raw", 178, [P, KT, ER])
        eb_raw = at("eb_raw", 130, [P, ER // P, H])
        ea_hi = at("ea_hi", 162, [P, KT, ER], F32R)
        ea_lo = at("ea_lo", 178, [P, KT, ER], F32R)
        eb_hi = at("eb_hi", 114, [P, ER // P, H], F32R)
        eb_lo = at("eb_lo", 130, [P, ER // P, H], F32R)
        wqkv_raw = at("wqkv_raw", 194, [P, KT, 3 * HD])
        wout_raw = at("wout_raw", 200, [P, H])
        br_qkv = at("br_qkv", 202, [P, 3])
        wqkv_hi = at("wqkv_hi", 82, [P, KT, 3 * HD], F32R)
        wqkv_lo = at("wqkv_lo", 88, [P, KT, 3 * HD], F32R)
        wout_hi = at("wout_hi", 94, [P, H], F32R)
        wout_lo = at("wout_lo", 96, [P, H], F32R)
        bo_rows = at("bo_rows", 32, [P, H])
        wr = at("wr", 203, [P, KT, EXPERTS])
        q_hi = at("q_hi", 0, [P, NB, SEQ], F32R)
        q_lo = at("q_lo", 4, [P, NB, SEQ], F32R)
        k_hi = at("k_hi", 8, [P, NB, SEQ], F32R)
        k_lo = at("k_lo", 12, [P, NB, SEQ], F32R)
        vT = at("vT", 16, [P, SEQ])
        v_hi = at("v_hi", 24, [P, NB, TPB, HD], F32R)
        v_lo = at("v_lo", 28, [P, NB, TPB, HD], F32R)
        oT_hi = at("oT_hi", 146, [P, NB, SEQ], F32R)
        oT_lo = at("oT_lo", 150, [P, NB, SEQ], F32R)
        prob = at("prob", 18, [P, 2, SEQ])
        pT_hi = at("pT_hi", 34, [P, TPB, SEQ], F32R)
        pT_lo = at("pT_lo", 42, [P, TPB, SEQ], F32R)
        x4f = at("x4f", 154, [P, 2, KT, P])
        hg = at("hg", 0, [P, 2, ER])
        hgT_hi = at("hgT_hi", 8, [P, 2, ER // P, P], F32R)
        hgT_lo = at("hgT_lo", 16, [P, 2, ER // P, P], F32R)
        left1 = at("left1", 24, [P, 2, EXPERTS])
        left2 = at("left2", 24.5, [P, 2, EXPERTS])
        gexp = at("gexp", 25, [P, 2, EXPERTS])
        gate = at("gate", 25.5, [P, 2, EXPERTS])
        sc_qkv = at("sc_qkv", 205, [P, 12, H // QB])
        rmax = at("rmax", 22, [P, TT])
        nmax = at("nmax", 22.25, [P, TT])
        rsum = at("rsum", 22.5, [P, TT])
        rinv = at("rinv", 22.75, [P, TT])
        top8 = at("top8", 26, [P, 2, 2, 8])
        gmax = at("gmax", 26.25, [P, 2])
        gsum = at("gsum", 26.5, [P, 2])
        ginv = at("ginv", 26.75, [P, 2])

        bank = [ctx.enter_context(nc.psum_tensor(f"bank{i}", [P, 512], F32)) for i in range(8)]
        plane = bank[0:RING_PLANE]
        lora_ps = bank[3]
        mm_ps = bank[4:8]
        unit_ps = bank[4:7]
        turn_ps = bank[0:2]
        rows_ps = [bank[4], bank[5], bank[2]]
        qkv_ps = [[bank[6], bank[7], bank[3]], [bank[4], bank[5], bank[3]]]
        s_ps = bank[6:8]
        oT_ps = bank[3]
        score_ps = bank[3]
        hid_ps = bank[6:8]

        codes_in = [sem(f"codes_in{i}") for i in range(RING_CODES)]
        scale_in = [sem(f"scale_in{i}") for i in range(RING_CODES)]
        sqkv_in = sem("sqkv_in")
        x_in = sem("x_in")
        eye_in = sem("eye_in")
        lora_in = sem("lora_in")
        lorad_in = sem("lorad_in")
        loraf_in = sem("loraf_in")
        bgu_in = sem("bgu_in")
        a4_in = sem("a4_in")
        plane_ready = sem("plane_ready")
        lut_step = sem("lut_step")
        diff_done = sem("diff_done")
        mult_done = sem("mult_done")
        weight_ready = sem("weight_ready")
        lora_ready = sem("lora_ready")
        lora_added = sem("lora_added")
        eye_mid = sem("eye_mid")
        hi_done = sem("hi_done")
        lo_done = sem("lo_done")
        xhi_done = sem("xhi_done")
        xlo_done = sem("xlo_done")
        m1_ready = sem("m1_ready")
        m1hi_done = sem("m1hi_done")
        m1lo_done = sem("m1lo_done")
        x1_ready = sem("x1_ready")
        x1hi_done = sem("x1hi_done")
        x1lo_done = sem("x1lo_done")
        xs_done = sem("xs_done")
        bprep_hi = sem("bprep_hi")
        bprep_done = sem("bprep_done")
        dprep_hi = sem("dprep_hi")
        dprep_done = sem("dprep_done")
        p_ready = sem("p_ready")
        phi_done = sem("phi_done")
        plo_done = sem("plo_done")
        gate_ready = sem("gate_ready")
        unit_ready = sem("unit_ready")
        silu_done = sem("silu_done")
        h_done = sem("h_done")
        hhi_done = sem("hhi_done")
        hlo_done = sem("hlo_done")
        down_ready = sem("down_ready")
        down_added = sem("down_added")
        neg_half_set = sem("neg_half_set")
        warmed = sem("warmed")
        low_rows_set = sem("low_rows_set")
        bn_step = sem("bn_step")
        var_ready = sem("var_ready")
        rstd_ready = sem("rstd_ready")
        nbias_ready = sem("nbias_ready")
        norm_done = sem("norm_done")
        turn_ready = sem("turn_ready")
        turnhi_done = sem("turnhi_done")
        turnlo_done = sem("turnlo_done")
        ffn_ready = sem("ffn_ready")
        attn_in = sem("attn_in")
        bo_in = sem("bo_in")
        ea_in = sem("ea_in")
        eb_in = sem("eb_in")
        whi_done = sem("whi_done")
        wlo_done = sem("wlo_done")
        bo_added = sem("bo_added")
        qkv_ready = sem("qkv_ready")
        qkvhi_done = sem("qkvhi_done")
        qklo_done = sem("qklo_done")
        s_ready = sem("s_ready")
        max_done = sem("max_done")
        nmax_done = sem("nmax_done")
        exp_done = sem("exp_done")
        rinv_done = sem("rinv_done")
        oT_ready = sem("oT_ready")
        oThi_done = sem("oThi_done")
        oTlo_done = sem("oTlo_done")
        wo_ready = sem("wo_ready")
        res_done = sem("res_done")
        score_ready = sem("score_ready")
        x4f_done = sem("x4f_done")
        top_step = sem("top_step")
        gexp_done = sem("gexp_done")
        gate_done = sem("gate_done")
        gsum_done = sem("gsum_done")
        ginv_done = sem("ginv_done")
        hid_ready = sem("hid_ready")
        hg_done = sem("hg_done")
        mix_ready = sem("mix_ready")
        out_done = sem("out_done")

        V, T = vector_order(), tensor_order()
        TAIL = tail_order()

        def split_no(c):
            return SPLIT.index(c) + 1

        def group_of(f):
            return next(i for i, g in enumerate(GROUPS) if f in g)

        def down_bank(gi, t):
            return bank[7] if gi < len(GROUPS) - 1 else bank[7 - t % 2]

        def slot_free_down(f):
            return TT * (group_of(f - RING_H) + 1)

        turn_no = {x: i for i, x in enumerate(x for x in TAIL if x[0] in ("turn", "vturn", "pturn", "hturn"))}
        rows_no = {x: i for i, x in enumerate(x for x in TAIL if x[0] in ("ffn", "wo", "mix"))}
        norm_no = {x[1:]: i for i, x in enumerate(x for x in TAIL if x[0] == "norm")}
        stat_no = {x[1:]: i for i, x in enumerate(x for x in TAIL if x[0] == "stat")}

        def slot_normed(i):
            return norm_no[next(x for x, m in stat_no.items() if m == i - RING_LN)] + 1

        def rows_free(i):
            x = next(x for x, m in rows_no.items() if m == i - 3)
            if x[0] == "ffn":
                return norm_done, norm_no[(1, x[1])] + 1
            if x[0] == "wo":
                return res_done, x[1] + 1
            return res_done, TT + x[1] + 1

        def dest(c):
            kind, k = c
            if kind == "o":
                return wo_hi[:, k, :], wo_lo[:, k, :]
            if kind == "v":
                return wq_hi[:, k, :], wq_lo[:, k, :]
            if kind in "gu":
                g = "gu".index(kind)
                return gu_hi[:, k % RING_GU, g, :, :], gu_lo[:, k % RING_GU, g, :, :]
            if kind == "d":
                return wd_hi[:, k % RING_H, :], wd_lo[:, k % RING_H, :]
            return wff_hi[:, k, :], wff_lo[:, k, :]

        def shaped(c, w):
            return w.rearrange("p (k o) -> p k o", k=KT) if c[0] in "gu" else w

        def late_weights():
            pieces = []
            for k in range(KT):
                pieces.append((wqkv_raw[:, k, :], wqkv_hi[:, k, :], wqkv_lo[:, k, :], attn_in, 64))
            pieces.append((wout_raw[:, :], wout_hi[:, :], wout_lo[:, :], attn_in, 64))
            for k in range(KT):
                for h in range(ER // 512):
                    cut = slice(h * 512, (h + 1) * 512)
                    pieces.append((ea_raw[:, k, cut], ea_hi[:, k, cut], ea_lo[:, k, cut], ea_in, 16))
            for m in range(ER // P):
                pieces.append((eb_raw[:, m, :], eb_hi[:, m, :], eb_lo[:, m, :], eb_in, 16))
            return pieces

        N_EA, N_ATTN = KT * (ER // 512), KT + 1
        late_at = {x: n for n, x in enumerate(
            x for x in TAIL if x[0] in ("s", "pturn") or x[0] == "stat" and x[1] == 1) if n < len(late_weights())}

        block = ctx.enter_context(nc.Block())

        @block.sync
        def _(sp):
            for j, c in enumerate(CHUNKS):
                s = j % RING_CODES
                if c == ("o", 0):
                    sp.dma_start(xs[:, :, :], xT).then_inc(x_in, 16)
                if c == ("k", 1):
                    sp.dma_start(bgu_raw[:, :, :], loB_gu).then_inc(bgu_in, 16)
                    sp.dma_start(a4_raw[:, :, :], loA_gu).then_inc(a4_in, 16)
                if c == ("k", 2):
                    sp.dma_start(la_d[:, :], loA_d).then_inc(lorad_in, 16)
                    sp.dma_start(lb_d[:, :], loB_d).then_inc(lorad_in, 16)
                    sp.dma_start(low_rows[:, 1:2], down_low).then_inc(lorad_in, 16)
                if c == ("g", 3):
                    sp.wait_ge(x1_ready, NB * KT)
                    sp.dma_start(la_f[:, :], loA_f).then_inc(loraf_in, 16)
                    sp.dma_start(lb_f[:, :], loB_f).then_inc(loraf_in, 16)
                if j >= RING_CODES:
                    sp.wait_ge(lut_step, 6 * (j - RING_CODES + 1))
                sp.dma_start(code[:, s, :], codes[j]).then_inc(codes_in[s], 16)
                if c in SCALED:
                    i = SCALED.index(c)
                    if i >= RING_CODES:
                        before = CHUNKS.index(SCALED[i - RING_CODES])
                        sp.wait_ge(weight_ready, before + 1)
                    src = scales[i].unsqueeze(1).to_broadcast([2, QB, 512])
                    for g in range(2):
                        sp.dma_start(scale[g * QB:(g + 1) * QB, i % RING_CODES, :],
                                     src[g]).then_inc(scale_in[i % RING_CODES], 16)
            sp.wait_ge(unit_ready, 2 * NF)
            sp.wait_ge(lora_ready, len(MERGED))
            sp.dma_start(wqkv_raw[:, :, :], w_qkv).then_inc(attn_in, 16)
            sp.dma_start(wout_raw[:, :], w_o).then_inc(attn_in, 16)
            sp.dma_start(br_qkv[:, :], b_qkv).then_inc(attn_in, 16)
            sp.dma_start(wr[:, :, :], w_r).then_inc(attn_in, 16)
            sp.dma_start(ea_raw[:, :, :], ex_A).then_inc(ea_in, 16)
            sp.wait_ge(hhi_done, 2 * NF)
            sp.wait_ge(hlo_done, 2 * NF)
            sp.dma_start(bo_rows[:, :], b_o.to_broadcast([P, H])).then_inc(bo_in, 16)
            sp.wait_ge(down_ready, TT * len(GROUPS))
            sp.dma_start(eb_raw[:, :, :], ex_B).then_inc(eb_in, 16)
            for t in range(TT):
                sp.wait_ge(norm_done, norm_no[(3, t)] + 1)
                sp.dma_start(out[t * P:(t + 1) * P, :], rows[:, t, :]).then_inc(out_done, 16)
            sp.wait_ge(out_done, 16 * TT)

        @block.gpsimd
        def _(pool):
            pool.dma_start(sc_qkv[:, :, :], scales_qkv).then_inc(sqkv_in, 16)
            pool.dma_start(ident[:, :], eye).then_inc(eye_in, 16)
            pool.dma_start(la_o[:, :], loA_o).then_inc(lora_in, 16)
            pool.dma_start(lb_o[:, :], loB_o).then_inc(lora_in, 16)
            pool.dma_start(la_qkv[:, :], loA_qkv).then_inc(lora_in, 16)
            pool.dma_start(lb_qkv[:, :], loB_qkv).then_inc(lora_in, 16)
            pool.memset(neg_half[:, :], -0.5).then_inc(neg_half_set, 1)
            mults = 0
            for item in filter(None, V):
                kind = item[0]
                if kind == "lut" and item[2] == 1:
                    c = item[1]
                    j = CHUNKS.index(c)
                    w = wf[:, j % RING_W, :]
                    pool.wait_ge(lut_step, 6 * (j + 1))
                    if j >= RING_W:
                        before = [x for x in CHUNKS[:j - RING_W + 1] if x in SPLIT]
                        if before:
                            pool.wait_ge(lo_done, split_no(before[-1]))
                        pool.wait_ge(weight_ready, j)
                    pool.tensor_tensor(w, halves[:, j % 2, 0, :], halves[:, j % 2, 1, :],
                                       ALU.subtract).then_inc(diff_done, 1)
                    pool.wait_ge(diff_done, j + 1)
                    done = mult_done if c[0] in "kv" else weight_ready
                    mults += c[0] in "kv"
                    if c in SCALED:
                        i = SCALED.index(c)
                        pool.wait_ge(scale_in[i % RING_CODES], 32 * (i // RING_CODES + 1))
                        pool.tensor_tensor(w, w, scale[:, i % RING_CODES, :], ALU.mult).then_inc(done, 1)
                    else:
                        pool.wait_ge(sqkv_in, 16)
                        wv = w.rearrange("p (b e) -> p b e", e=QB)
                        sv = sc_qkv[:, "qkv".index(c[0]) * KT + c[1], :].unsqueeze(2)
                        pool.tensor_tensor(wv, wv, sv.to_broadcast([P, H // QB, QB]), ALU.mult)\
                            .then_inc(done, 1)
                    if c[0] in "kv":
                        pool.wait_ge(mult_done, mults)
                        pool.wait_ge(weight_ready, j)
                        pool.tensor_tensor(w, w, wf[:, (j - 1) % RING_W, :], ALU.add)\
                            .then_inc(weight_ready, 1)
                elif kind == "split":
                    c = item[1]
                    hi, lo = dest(c)
                    pool.wait_ge(hi_done, split_no(c))
                    w = wf[:, CHUNKS.index(c) % RING_W, :]
                    pool.tensor_tensor(lo, shaped(c, w), hi.bitcast(F32), ALU.subtract).then_inc(lo_done, 1)
                elif kind == "hsplit":
                    n = item[1]
                    f, b = n // NB, n % NB
                    hs = slice(b * SEQ, (b + 1) * SEQ)
                    pool.wait_ge(hhi_done, n + 1)
                    pool.tensor_tensor(h_lo[:, f % RING_H, hs], act_f[:, n % 2, :],
                                       h_hi[:, f % RING_H, hs].bitcast(F32), ALU.subtract).then_inc(hlo_done, 1)
            def late(item):
                if item in late_at:
                    raw, hi, lo, _, _ = late_weights()[late_at[item]]
                    pool.wait_ge(whi_done, late_at[item] + 1)
                    pool.tensor_tensor(lo, raw, hi.bitcast(F32), ALU.subtract).then_inc(wlo_done, 1)

            for item in TAIL:
                if item[0] == "stat":
                    i = stat_no[item[1:]]
                    pool.wait_ge(neg_half_set, 1)
                    pool.wait_ge(var_ready, i + 1)
                    s = i % RING_LN
                    if i >= RING_LN:
                        pool.wait_ge(norm_done, slot_normed(i))
                    pool.tensor_tensor(rstd[:, s:s + 1], veps[:, s:s + 1], neg_half[:, :], ALU.pow)\
                        .then_inc(rstd_ready, 1)
                    pool.wait_ge(rstd_ready, i + 1)
                    pool.tensor_scalar(nbias[:, s:s + 1], mv[:, s, 0:1], rstd[:, s:s + 1], -1.0, ALU.mult, ALU.mult)\
                        .then_inc(nbias_ready, 1)
                elif item[0] == "s":
                    t = TPB * item[1] + item[2]
                    pool.wait_ge(bo_in, 16)
                    pool.wait_ge(turn_ready, turn_no[("turn", 1, t)] + 1)
                    pool.tensor_tensor(rows[:, t, :], rows[:, t, :], bo_rows[:, :], ALU.add)\
                        .then_inc(bo_added, 1)
                late(item)

        @block.scalar
        def _(act):
            def copy(dst, src, done):
                nc.scalar.activation(dst, src, ACT.Copy).then_inc(done, 1)

            act.wait_ge(low_rows_set, 4)
            nc.scalar.activation(warm[:, :], low_rows[:, 0:1], ACT.Silu).then_inc(warmed, 1)
            for item in filter(None, V):
                kind = item[0]
                if kind == "lut":
                    c = item[1]
                    j = CHUNKS.index(c)
                    src = code[:, j % RING_CODES, :]
                    act.wait_ge(codes_in[j % RING_CODES], 16 * (j // RING_CODES + 1))
                    steps = [(h[2][0], h[2][1] - h[3][1], ACT.Identity) for h in (UPPER, LOWER)]
                    steps += [(h[0][0], h[0][1], ACT.Relu) for h in (UPPER, LOWER)]
                    steps += [(h[1][0], h[1][1], ACT.Identity) for h in (UPPER, LOWER)]
                    for i in range(3 * item[2], 3 * item[2] + 3):
                        slope, start, func = steps[i]
                        m = 6 * j + i
                        if m >= RING_PLANE:
                            act.wait_ge(lut_step, m - RING_PLANE + 1)
                        nc.scalar.activation(plane[m % RING_PLANE][:, :], src, func, bias=float(start),
                                             scale=float(slope)).then_inc(plane_ready, 1)
                elif kind == "split":
                    c = item[1]
                    j = CHUNKS.index(c)
                    hi, _ = dest(c)
                    act.wait_ge(weight_ready, j + 1)
                    if c in MERGED:
                        act.wait_ge(lora_added, MERGED.index(c) + 1)
                    if c[0] in "gu" and c[1] == 1:
                        act.wait_ge(lora_ready, 2 * KT)
                    if c[0] in "gu" and c[1] >= RING_GU:
                        act.wait_ge(unit_ready, 2 * (c[1] - RING_GU) + 2)
                    if c[0] == "d" and c[1] == 0:
                        act.wait_ge(m1_ready, KT)
                    if c[0] == "d" and c[1] == RING_H - 1:
                        act.wait_ge(p_ready, NB)
                    if c[0] == "d" and c[1] >= RING_H:
                        act.wait_ge(down_ready, slot_free_down(c[1]))
                    if c[0] == "f":
                        act.wait_ge(down_ready, TT)
                    copy(hi, shaped(c, wf[:, j % RING_W, :]), hi_done)
                elif kind == "xsplit":
                    k, b = item[1] // NB, item[1] % NB
                    act.wait_ge(x_in, 16)
                    copy(x_hi[:, k, b * SEQ:(b + 1) * SEQ], xs[:, k, b * SEQ:(b + 1) * SEQ], xhi_done)
                elif kind == "m1":
                    act.wait_ge(m1_ready, item[1] + 1)
                    nc.scalar.activation(m1_hi[:, item[1], :], mm_ps[item[1]][:, :], ACT.Copy, scale=1.0 / 3.0)\
                        .then_inc(m1hi_done, 1)
                elif kind == "x1":
                    n = item[1]
                    b, o = n // KT, n % KT
                    act.wait_ge(x1_ready, n + 1)
                    copy(x1_hi[:, o, b * SEQ:(b + 1) * SEQ], mm_ps[n % 4][:, :], x1hi_done)
                elif kind == "bprep":
                    i = item[1]
                    act.wait_ge(bgu_in, 16)
                    act.wait_ge(a4_in, 16)
                    act.wait_ge(weight_ready, 4 * KT)
                    copy(*((a4_hi[:, :, :], a4_raw[:, :, :]), (bg4[:, :], bgu_raw[:, 0, :]),
                           (bu4[:, :], bgu_raw[:, 1, :]))[i], bprep_hi)
                elif kind == "dprep":
                    act.wait_ge(lorad_in, 48)
                    act.wait_ge(x1_ready, NB * KT)
                    copy(la_dp[:, :], la_d[:, :], dprep_hi)
                    copy(lb_dh[:, :], lb_d[:, :], dprep_hi)
                elif kind == "p":
                    b = item[1]
                    act.wait_ge(p_ready, b + 1)
                    copy(p4[:, b * SEQ:(b + 1) * SEQ], mm_ps[2 + b][:, :], phi_done)
                elif kind == "silu":
                    n = item[1]
                    act.wait_ge(gate_ready, n + 1)
                    if n >= 2:
                        act.wait_ge(hlo_done, n - 1)
                    nc.scalar.activation(act_f[:, n % 2, :], unit_ps[2 * n % 3][:, :], ACT.Silu)\
                        .then_inc(silu_done, 1)
                elif kind == "hsplit":
                    n = item[1]
                    f, b = n // NB, n % NB
                    act.wait_ge(h_done, n + 1)
                    if f >= RING_H:
                        act.wait_ge(down_ready, slot_free_down(f))
                    copy(h_hi[:, f % RING_H, b * SEQ:(b + 1) * SEQ], act_f[:, n % 2, :], hhi_done)

            def late(item):
                if item in late_at:
                    raw, hi, lo, arrived, count = late_weights()[late_at[item]]
                    act.wait_ge(arrived, count)
                    act.wait_ge(unit_ready, 2 * NF)
                    act.wait_ge(down_ready, TT * len(GROUPS))
                    copy(hi, raw, whi_done)

            for item in TAIL:
                kind = item[0]
                if kind == "norm":
                    L, t = item[1:]
                    s = stat_no[(L, t)] % RING_LN
                    src = rows_ps[rows_no[("ffn", t)] % 3][:, :] if L == 1 else rows[:, t, :]
                    act.wait_ge(nbias_ready, stat_no[(L, t)] + 1)
                    if L == 0:
                        act.wait_ge(down_added, TT * (len(GROUPS) - 1) + t + 1)
                    if L == 1:
                        act.wait_ge(turn_ready, turn_no[("turn", 0, t)] + 1)
                    if L >= 2:
                        act.wait_ge(res_done, TT * (L - 2) + t + 1)
                    nc.scalar.activation(rows[:, t, :], src, ACT.Identity, bias=nbias[:, s:s + 1],
                                         scale=rstd[:, s:s + 1]).then_inc(norm_done, 1)
                elif kind == "turn":
                    L, t = item[1:]
                    i = turn_no[item]
                    hi = xa_hi if L == 0 else xb_hi
                    act.wait_ge(turn_ready, i + 1)
                    if L == 0:
                        act.wait_ge(lo_done, len(SPLIT))
                    if L == 1:
                        act.wait_ge(down_ready, TT * len(GROUPS))
                    if L == 2:
                        act.wait_ge(qkv_ready, 3 * NB)
                        if t >= 2:
                            act.wait_ge(score_ready, t - 1)
                        copy(x4f[:, t % 2, :, :], turn_ps[i % 2][:, :].rearrange("p (k c) -> p k c", k=KT),
                             x4f_done)
                    copy(hi[:, :, t * P:(t + 1) * P],
                         turn_ps[i % 2][:, :].rearrange("p (k c) -> p k c", k=KT), turnhi_done)
                elif kind == "qkv":
                    b, m = item[1:]
                    act.wait_ge(attn_in, 64)
                    act.wait_ge(ffn_ready, TT)
                    if b and m == 2:
                        act.wait_ge(turn_ready, turn_no[("vturn", b - 1)] + 1)
                    dst = (q_hi[:, b, :], k_hi[:, b, :], vT[:, :])[m]
                    act.wait_ge(qkv_ready, 3 * b + m + 1)
                    nc.scalar.activation(dst, qkv_ps[b][m][:, :], ACT.Identity,
                                         bias=br_qkv[:, m:m + 1]).then_inc(qkvhi_done, 1)
                elif kind == "vturn":
                    b, i = item[1], turn_no[item]
                    act.wait_ge(turn_ready, i + 1)
                    copy(v_hi[:, b, :, :], turn_ps[i % 2][:, :].rearrange("p (k c) -> p k c", k=TPB), turnhi_done)
                elif kind == "s":
                    b, q = item[1:]
                    n = TPB * b + q
                    act.wait_ge(nmax_done, n + 1)
                    if n >= 2:
                        act.wait_ge(turn_ready, turn_no[("pturn", (n - 2) // TPB, (n - 2) % TPB)] + 1)
                    nc.scalar.activation(prob[:, n % 2, :], s_ps[n % 2][:, :], ACT.Exp, scale=ATTN_SCALE,
                                         bias=nmax[:, n:n + 1], accum_out=rsum[:, n:n + 1]).then_inc(exp_done, 1)
                elif kind == "pturn":
                    b, q = item[1:]
                    i = turn_no[item]
                    act.wait_ge(turn_ready, i + 1)
                    act.wait_ge(ffn_ready, TT)
                    if b:
                        act.wait_ge(oT_ready, b)
                    copy(pT_hi[:, :, q * P:(q + 1) * P],
                         turn_ps[i % 2][:, :].rearrange("p (k c) -> p k c", k=TPB), turnhi_done)
                elif kind == "ot":
                    b = item[1]
                    act.wait_ge(oT_ready, b + 1)
                    copy(oT_hi[:, b, :], oT_ps[:, :], oThi_done)
                elif kind == "score":
                    t = item[1]
                    act.wait_ge(top_step, 5 * t + 3)
                    if t >= 2:
                        act.wait_ge(gate_done, t - 1)
                    nc.scalar.activation(gexp[:, t % 2, :], score_ps[:, 0:EXPERTS], ACT.Exp,
                                         bias=gmax[:, t % 2:t % 2 + 1]).then_inc(gexp_done, 1)
                elif kind == "hturn":
                    t, c = item[1:]
                    i = turn_no[item]
                    act.wait_ge(turn_ready, i + 1)
                    if t >= 2:
                        act.wait_ge(mix_ready, t - 1)
                    copy(hgT_hi[:, t % 2, c * 4:(c + 1) * 4, :],
                         turn_ps[i % 2][:, :].rearrange("p (k c) -> p k c", k=4), turnhi_done)
                late(item)

        @block.tensor
        def _(pe):
            def product(ps, terms, start=True, stop=True):
                last = None
                for i, (ah, al, bh, bl) in enumerate(terms):
                    for n, (a, b) in enumerate(((ah, bh), (ah, bl), (al, bh))):
                        last = nc.tensor.matmul(ps, a, b, start=start and i == 0 and n == 0,
                                                stop=stop and i == len(terms) - 1 and n == 2)
                return last

            def lora(c):
                i = MERGED.index(c)
                if i:
                    pe.wait_ge(lora_added, i)
                kind, k = c
                if kind == "o":
                    a, b = la_o[:, k * P:(k + 1) * P], lb_o[:, :]
                elif kind == "v":
                    a, b = lb_qkv[:, k * P:(k + 1) * P], la_qkv[:, :]
                elif kind == "d":
                    pe.wait_ge(dprep_done, 2)
                    r, cut = 32 * (k // 4), slice((k % 4) * P, (k % 4 + 1) * P)
                    nc.tensor.matmul(lora_ps[:, :], la_dp[r:r + 32, cut], lb_dh[r:r + 32, :], start=True, stop=False)
                    nc.tensor.matmul(lora_ps[:, :], la_dp[r:r + RANK, cut], lb_dl[r:r + RANK, :],
                                     start=False, stop=True).then_inc(lora_ready, 1)
                    return
                else:
                    pe.wait_ge(loraf_in, 32)
                    a, b = la_f[:, k * P:(k + 1) * P], lb_f[:, :]
                nc.tensor.matmul(lora_ps[:, :], a, b, start=True, stop=True).then_inc(lora_ready, 1)

            pe.wait_ge(lora_in, 64)
            lora(("v", 0))
            lora(("o", 0))
            pe.wait_ge(eye_in, 16)
            for k in range(KT):
                if k < KT - 1:
                    lora(("v", k + 1))
                pe.wait_ge(hi_done, split_no(("o", k)))
                pe.wait_ge(lo_done, split_no(("o", k)))
                for i in range(KT):
                    cut = slice(i * P, (i + 1) * P)
                    last = product(mm_ps[i][:, :], [(wq_hi[:, k, cut], wq_lo[:, k, cut],
                                                     wo_hi[:, k, :], wo_lo[:, k, :])],
                                   start=k == 0, stop=k == KT - 1)
                    if k == 0:
                        for _ in range(3):
                            nc.tensor.matmul(mm_ps[i][:, cut], ident[:, :], ident[:, :], start=False, stop=False)
                    if k == KT - 1:
                        last.then_inc(m1_ready, 1)
                if k < KT - 1:
                    lora(("o", k + 1))
            pe.wait_ge(m1hi_done, KT)
            pe.wait_ge(m1lo_done, KT)
            pe.wait_ge(xhi_done, 2 * KT)
            pe.wait_ge(xlo_done, 2 * KT)
            for n in range(NB * KT):
                b, o = n // KT, n % KT
                if n >= 4:
                    pe.wait_ge(x1hi_done, n - 3)
                    pe.wait_ge(xs_done, n - 3)
                cut, tk = slice(o * P, (o + 1) * P), slice(b * SEQ, (b + 1) * SEQ)
                product(mm_ps[n % 4][:, :], [(m1_hi[:, k, cut], m1_lo[:, k, cut], x_hi[:, k, tk], x_lo[:, k, tk])
                                             for k in range(KT)]).then_inc(x1_ready, 1)
            pe.wait_ge(bprep_done, 3)
            for b in range(NB):
                pe.wait_ge(x1hi_done, NB * KT - 1 + b)
                pe.wait_ge(x1lo_done, NB * KT - 1 + b)
                pe.wait_ge(xs_done, NB * KT - 1 + b)
                tk = slice(b * SEQ, (b + 1) * SEQ)
                product(mm_ps[2 + b][:, :], [(a4_hi[:, k, :], a4_lo[:, k, :], x1_hi[:, k, tk], x1_lo[:, k, tk])
                                             for k in range(KT)]).then_inc(p_ready, 1)

            def unit(n, g):
                f, b = n // NB, n % NB
                m = 2 * n + g
                tk = slice(b * SEQ, (b + 1) * SEQ)
                if m == 2:
                    pe.wait_ge(phi_done, NB)
                    pe.wait_ge(plo_done, NB)
                elif m > 2 and g == 0:
                    pe.wait_ge(h_done, n - 1)
                elif m > 2:
                    pe.wait_ge(silu_done, n)
                pe.wait_ge(hi_done, split_no(("gu"[g], f)))
                pe.wait_ge(lo_done, split_no(("gu"[g], f)))
                s, ps = f % RING_GU, unit_ps[m % 3][:, :]
                product(ps, [(gu_hi[:, s, g, k, :], gu_lo[:, s, g, k, :], x1_hi[:, k, tk], x1_lo[:, k, tk])
                             for k in range(KT)], stop=False)
                pe.wait_ge(phi_done, min(n + 1, NB))
                pe.wait_ge(plo_done, min(n + 1, NB))
                nc.tensor.matmul(ps, (bg4, bu4)[g][:, f * P:(f + 1) * P], p4[:, tk], start=False, stop=True)\
                    .then_inc((gate_ready, unit_ready)[g], 1)

            def down(gi, t):
                n = gi * TT + t
                last_f = GROUPS[gi][-1]
                if gi == len(GROUPS) - 1 and t == 1:
                    pe.wait_ge(h_done, 2 * NF)
                elif gi == len(GROUPS) - 1 and t > 1:
                    pe.wait_ge(down_added, n - 1)
                elif n:
                    pe.wait_ge(down_added, n)
                pe.wait_ge(hhi_done, 2 * last_f + 2)
                pe.wait_ge(hlo_done, 2 * last_f + 2)
                pe.wait_ge(hi_done, split_no(("d", last_f)))
                pe.wait_ge(lo_done, split_no(("d", last_f)))
                tk = slice(t * P, (t + 1) * P)
                ps = down_bank(gi, t)
                last = product(ps[:, :], [(h_hi[:, f % RING_H, tk], h_lo[:, f % RING_H, tk],
                                           wd_hi[:, f % RING_H, :], wd_lo[:, f % RING_H, :])
                                          for f in GROUPS[gi]], stop=gi > 0)
                if gi == 0:
                    pe.wait_ge(eye_in, 16)
                    for k in range(KT):
                        last = nc.tensor.matmul(ps[:, k * P:(k + 1) * P], xs[:, k, tk], ident[:, :],
                                                start=False, stop=k == KT - 1)
                last.then_inc(down_ready, 1)

            for item in filter(None, T):
                if item[0] == "lora":
                    lora(item[1])
                elif item[0] == "down":
                    down(item[1], item[2])
                else:
                    unit(item[1], item[0] == "up")

            def turn(ps, src):
                for k in range(4):
                    last = nc.tensor.transpose(ps[:, k * P:(k + 1) * P], src[:, k * P:(k + 1) * P], ident[:, :])
                return last

            def turn_free(i):
                if i >= 2:
                    pe.wait_ge(turnlo_done, i - 1)
                else:
                    pe.wait_ge(lut_step, 6 * NJ)

            def rows_wait(i):
                if i < 3:
                    pe.wait_ge(lut_step, 6 * NJ)
                    pe.wait_ge(h_done, 2 * NF)
                    pe.wait_ge(down_added, TT * (len(GROUPS) - 1))
                else:
                    s, v = rows_free(i)
                    pe.wait_ge(s, v)

            for item in TAIL:
                kind = item[0]
                if kind == "down":
                    down(item[1], item[2])
                elif kind == "turn":
                    L, t = item[1:]
                    i = turn_no[item]
                    turn_free(i)
                    pe.wait_ge(norm_done, norm_no[(L, t)] + 1)
                    turn(turn_ps[i % 2], rows[:, t, :]).then_inc(turn_ready, 1)
                elif kind == "ffn":
                    t = item[1]
                    rows_wait(rows_no[item])
                    pe.wait_ge(turnlo_done, turn_no[("turn", 0, t)] + 1)
                    pe.wait_ge(turnhi_done, turn_no[("turn", 0, t)] + 1)
                    pe.wait_ge(hi_done, len(SPLIT))
                    pe.wait_ge(lo_done, len(SPLIT))
                    tk = slice(t * P, (t + 1) * P)
                    product(rows_ps[rows_no[item] % 3][:, :],
                            [(xa_hi[:, k, tk], xa_lo[:, k, tk], wff_hi[:, k, :], wff_lo[:, k, :])
                             for k in range(KT)]).then_inc(ffn_ready, 1)
                elif kind == "qkv":
                    b, m = item[1:]
                    pe.wait_ge(turnlo_done, turn_no[("turn", 1, TPB * b + TPB - 1)] + 1)
                    pe.wait_ge(wlo_done, N_ATTN)
                    pe.wait_ge(lora_added, len(MERGED))
                    pe.wait_ge(down_added, TT * len(GROUPS))
                    if b:
                        pe.wait_ge(norm_done, norm_no[(1, TT - 1)] + 1)
                        pe.wait_ge(qkvhi_done, 3)
                    tk = slice(b * SEQ, (b + 1) * SEQ)
                    cut = slice(m * HD, (m + 1) * HD)
                    product(qkv_ps[b][m][:, :], [(wqkv_hi[:, k, cut], wqkv_lo[:, k, cut],
                                               xb_hi[:, k, tk], xb_lo[:, k, tk])
                                              for k in range(KT)]).then_inc(qkv_ready, 1)
                elif kind == "vturn":
                    b, i = item[1], turn_no[item]
                    turn_free(i)
                    pe.wait_ge(qkvhi_done, 3 * b + 3)
                    turn(turn_ps[i % 2], vT).then_inc(turn_ready, 1)
                elif kind == "s":
                    b, q = item[1:]
                    n = TPB * b + q
                    pe.wait_ge(qkvhi_done, 3 * b + 2)
                    pe.wait_ge(qklo_done, 2 * b + 2)
                    pe.wait_ge(down_added, TT * len(GROUPS))
                    if n >= 2:
                        pe.wait_ge(exp_done, n - 1)
                    cut = slice(q * P, (q + 1) * P)
                    product(s_ps[n % 2][:, :], [(q_hi[:, b, cut], q_lo[:, b, cut], k_hi[:, b, :], k_lo[:, b, :])])\
                        .then_inc(s_ready, 1)
                elif kind == "pturn":
                    b, q = item[1:]
                    n, i = TPB * b + q, turn_no[item]
                    turn_free(i)
                    pe.wait_ge(exp_done, n + 1)
                    turn(turn_ps[i % 2], prob[:, n % 2, :]).then_inc(turn_ready, 1)
                elif kind == "ot":
                    b = item[1]
                    i = turn_no[("pturn", b, TPB - 1)]
                    pe.wait_ge(turnhi_done, i + 1)
                    pe.wait_ge(turnlo_done, i + 1)
                    pe.wait_ge(qkvhi_done, 3 * NB)
                    pe.wait_ge(qklo_done, 2 * NB)
                    if b:
                        pe.wait_ge(oTlo_done, b)
                    product(oT_ps[:, :], [(v_hi[:, b, k, :], v_lo[:, b, k, :], pT_hi[:, k, :], pT_lo[:, k, :])
                                          for k in range(TPB)]).then_inc(oT_ready, 1)
                elif kind == "wo":
                    t = item[1]
                    b = t // TPB
                    rows_wait(rows_no[item])
                    pe.wait_ge(oThi_done, b + 1)
                    pe.wait_ge(oTlo_done, b + 1)
                    cut = slice((t % TPB) * P, (t % TPB + 1) * P)
                    product(rows_ps[rows_no[item] % 3][:, :],
                            [(oT_hi[:, b, cut], oT_lo[:, b, cut], wout_hi[:, :], wout_lo[:, :])]).then_inc(wo_ready, 1)
                elif kind == "score":
                    t = item[1]
                    pe.wait_ge(x4f_done, t + 1)
                    pe.wait_ge(attn_in, 64)
                    pe.wait_ge(oTlo_done, NB)
                    if t:
                        pe.wait_ge(gate_done, t)
                    for k in range(KT):
                        last = nc.tensor.matmul(score_ps[:, 0:EXPERTS], x4f[:, t % 2, k, :], wr[:, k, :],
                                                start=k == 0, stop=k == KT - 1)
                    last.then_inc(score_ready, 1)
                elif kind == "h":
                    t, c = item[1:]
                    tk = slice(t * P, (t + 1) * P)
                    pe.wait_ge(exp_done, TT)
                    pe.wait_ge(wlo_done, N_ATTN + N_EA)
                    pe.wait_ge(turnhi_done, turn_no[("turn", 2, t)] + 1)
                    pe.wait_ge(turnlo_done, turn_no[("turn", 2, t)] + 1)
                    if t:
                        pe.wait_ge(hg_done, 2 * (t - 1) + c + 1)
                    cut = slice(c * 512, (c + 1) * 512)
                    product(hid_ps[c][:, :], [(xb_hi[:, k, tk], xb_lo[:, k, tk], ea_hi[:, k, cut], ea_lo[:, k, cut])
                                              for k in range(KT)]).then_inc(hid_ready, 1)
                elif kind == "hturn":
                    t, c = item[1:]
                    i = turn_no[item]
                    turn_free(i)
                    pe.wait_ge(hg_done, 2 * t + c + 1)
                    turn(turn_ps[i % 2], hg[:, t % 2, c * 512:(c + 1) * 512]).then_inc(turn_ready, 1)
                elif kind == "mix":
                    t = item[1]
                    i = turn_no[("hturn", t, 1)]
                    rows_wait(rows_no[item])
                    pe.wait_ge(turnhi_done, i + 1)
                    pe.wait_ge(turnlo_done, i + 1)
                    pe.wait_ge(wlo_done, len(late_weights()))
                    product(rows_ps[rows_no[item] % 3][:, :],
                            [(hgT_hi[:, t % 2, m, :], hgT_lo[:, t % 2, m, :], eb_hi[:, m, :], eb_lo[:, m, :])
                             for m in range(ER // P)]).then_inc(mix_ready, 1)

        @block.vector
        def _(dve):
            eye_mids = 0
            for g in range(4):
                dve.memset(low_rows[32 * g:32 * g + 32, 0:1], -float(g % 2)).then_inc(low_rows_set, 1)

            def low(dst, src, hi, done):
                nc.vector.tensor_tensor(dst, src, hi.bitcast(F32), ALU.subtract).then_inc(done, 1)

            for item in filter(None, V):
                kind = item[0]
                if kind == "lut":
                    c = item[1]
                    j = CHUNKS.index(c)
                    src = code[:, j % RING_CODES, :]
                    dve.wait_ge(codes_in[j % RING_CODES], 16 * (j // RING_CODES + 1))
                    for i in range(3 * item[2], 3 * item[2] + 3):
                        m, side = 6 * j + i, i % 2
                        lines = (UPPER, LOWER)[side]
                        ps, acc = plane[m % RING_PLANE][:, :], half[:, side, :]
                        dve.wait_ge(plane_ready, m + 1)
                        if m >= 2:
                            dve.wait_ge(lut_step, m - 1)
                        if i < 2:
                            ins = nc.vector.scalar_tensor_tensor(acc, src, float(lines[3][0]), ps, ALU.mult, ALU.max)
                        elif i < 4:
                            ins = nc.vector.scalar_tensor_tensor(acc, acc, float(lines[3][1]), ps, ALU.add, ALU.max)
                        else:
                            if j >= 2:
                                dve.wait_ge(diff_done, j - 1)
                            ins = nc.vector.tensor_tensor(halves[:, j % 2, side, :], acc, ps, ALU.max)
                        ins.then_inc(lut_step, 1)
                elif kind == "merge":
                    c = item[1]
                    j, i = CHUNKS.index(c), MERGED.index(c)
                    w = wf[:, j % RING_W, :]
                    dve.wait_ge(weight_ready, j + 1)
                    dve.wait_ge(lora_ready, i + 1)
                    if c[0] != "f":
                        nc.vector.tensor_tensor(w, lora_ps[:, :], w, ALU.add).then_inc(lora_added, 1)
                    else:
                        eye_mids += 1
                        nc.vector.scalar_tensor_tensor(w, lora_ps[:, :], LORA_SCALE, w, ALU.mult, ALU.add)\
                            .then_inc(eye_mid, 1)
                        dve.wait_ge(eye_mid, eye_mids)
                        d = w[:, c[1] * P:(c[1] + 1) * P]
                        nc.vector.tensor_tensor(d, d, ident[:, :], ALU.add).then_inc(lora_added, 1)
                elif kind == "xsplit":
                    k, b = item[1] // NB, item[1] % NB
                    tk = slice(b * SEQ, (b + 1) * SEQ)
                    dve.wait_ge(xhi_done, item[1] + 1)
                    low(x_lo[:, k, tk], xs[:, k, tk], x_hi[:, k, tk], xlo_done)
                elif kind == "m1":
                    i = item[1]
                    dve.wait_ge(m1hi_done, i + 1)
                    nc.vector.scalar_tensor_tensor(m1_lo[:, i, :], mm_ps[i][:, :], 1.0 / 3.0,
                                                   m1_hi[:, i, :].bitcast(F32), ALU.mult, ALU.subtract)\
                        .then_inc(m1lo_done, 1)
                elif kind == "x1":
                    n = item[1]
                    b, o = n // KT, n % KT
                    tk = slice(b * SEQ, (b + 1) * SEQ)
                    dve.wait_ge(x1hi_done, n + 1)
                    dve.wait_ge(xlo_done, 2 * KT)
                    low(x1_lo[:, o, tk], mm_ps[n % 4][:, :], x1_hi[:, o, tk], x1lo_done)
                    nc.vector.tensor_tensor(xs[:, o, tk], mm_ps[n % 4][:, :], xs[:, o, tk], ALU.add)\
                        .then_inc(xs_done, 1)
                elif kind == "bprep":
                    i = item[1]
                    dve.wait_ge(bprep_hi, i + 1)
                    dve.wait_ge(low_rows_set, 4)
                    if i == 0:
                        low(a4_lo[:, :, :], a4_raw[:, :, :], a4_hi[:, :, :], bprep_done)
                    else:
                        b4 = (bg4, bu4)[i - 1]
                        nc.vector.scalar_tensor_tensor(b4[:, :], b4[:, :].bitcast(F32), low_rows[:, 0:1],
                                                       bgu_raw[:, i - 1, :], ALU.mult, ALU.add)\
                            .then_inc(bprep_done, 1)
                elif kind == "dprep":
                    dve.wait_ge(dprep_hi, 2)
                    nc.vector.scalar_tensor_tensor(la_dp[:, :], la_dp[:, :].bitcast(F32), low_rows[:, 1:2],
                                                   la_d[:, :], ALU.mult, ALU.add).then_inc(dprep_done, 1)
                    dve.wait_ge(p_ready, NB)
                    low(lb_dl[:, :], lb_d[:, :], lb_dh[:, :], dprep_done)
                elif kind == "p":
                    b = item[1]
                    tk = slice(b * SEQ, (b + 1) * SEQ)
                    dve.wait_ge(phi_done, b + 1)
                    low(p4[64:128, tk], mm_ps[2 + b][64:128, :], p4[64:128, tk], plo_done)
                elif kind == "h":
                    n = item[1]
                    a = act_f[:, n % 2, :]
                    dve.wait_ge(silu_done, n + 1)
                    dve.wait_ge(unit_ready, n + 1)
                    nc.vector.tensor_tensor(a, a, unit_ps[(2 * n + 1) % 3][:, :], ALU.mult).then_inc(h_done, 1)
                elif kind == "down":
                    gi, t = item[1:]
                    n = gi * TT + t
                    dve.wait_ge(down_ready, n + 1)
                    if gi == 0:
                        dve.wait_ge(bprep_done, 3)
                        nc.vector.tensor_copy(rows[:, t, :], down_bank(gi, t)[:, :]).then_inc(down_added, 1)
                    else:
                        dve.wait_ge(down_added, (gi - 1) * TT + t + 1)
                        nc.vector.tensor_tensor(rows[:, t, :], down_bank(gi, t)[:, :], rows[:, t, :], ALU.add)\
                            .then_inc(down_added, 1)

            for item in TAIL:
                kind = item[0]
                if kind == "down":
                    gi, t = item[1:]
                    n = gi * TT + t
                    dve.wait_ge(down_ready, n + 1)
                    dve.wait_ge(down_added, (gi - 1) * TT + t + 1)
                    nc.vector.tensor_tensor(rows[:, t, :], down_bank(gi, t)[:, :], rows[:, t, :], ALU.add)\
                        .then_inc(down_added, 1)
                elif kind == "stat":
                    L, t = item[1:]
                    i = stat_no[(L, t)]
                    s = i % RING_LN
                    src = rows[:, t, :]
                    if L == 0:
                        dve.wait_ge(down_added, TT * (len(GROUPS) - 1) + t + 1)
                    elif L == 1:
                        dve.wait_ge(ffn_ready, t + 1)
                        src = rows_ps[rows_no[("ffn", t)] % 3][:, :]
                    elif L == 2:
                        dve.wait_ge(res_done, t + 1)
                    else:
                        dve.wait_ge(mix_ready, t + 1)
                        nc.vector.scalar_tensor_tensor(src, rows_ps[rows_no[("mix", t)] % 3][:, :], EXPERT_SCALE,
                                                       src, ALU.mult, ALU.add).then_inc(res_done, 1)
                        dve.wait_ge(res_done, TT + t + 1)
                    nc.vector.bn_stats(bn6[:, s, :], src).then_inc(bn_step, 1)
                    dve.wait_ge(bn_step, 2 * i + 1)
                    if i >= RING_LN:
                        dve.wait_ge(norm_done, slot_normed(i))
                    nc.vector.bn_aggr(mv[:, s, :], bn6[:, s, :]).then_inc(bn_step, 1)
                    dve.wait_ge(bn_step, 2 * i + 2)
                    if i >= RING_LN:
                        dve.wait_ge(rstd_ready, i - RING_LN + 1)
                    nc.vector.tensor_scalar(veps[:, s:s + 1], mv[:, s, 1:2], EPS, None, ALU.add)\
                        .then_inc(var_ready, 1)
                elif kind == "turn":
                    L, t = item[1:]
                    i = turn_no[item]
                    hi, lo = (xa_hi, xa_lo) if L == 0 else (xb_hi, xb_lo)
                    dve.wait_ge(turnhi_done, i + 1)
                    tk = slice(t * P, (t + 1) * P)
                    low(lo[:, :, tk], turn_ps[i % 2][:, :].rearrange("p (k c) -> p k c", k=KT), hi[:, :, tk],
                        turnlo_done)
                elif kind == "qkv":
                    b, m = item[1:]
                    if m < 2:
                        hi, lo = ((q_hi, q_lo), (k_hi, k_lo))[m]
                        dve.wait_ge(qkvhi_done, 3 * b + m + 1)
                        nc.vector.scalar_tensor_tensor(lo[:, b, :], qkv_ps[b][m][:, :], br_qkv[:, m:m + 1],
                                                       hi[:, b, :].bitcast(F32), ALU.add, ALU.subtract)\
                            .then_inc(qklo_done, 1)
                elif kind == "vturn":
                    b, i = item[1], turn_no[item]
                    dve.wait_ge(turnhi_done, i + 1)
                    low(v_lo[:, b, :, :], turn_ps[i % 2][:, :].rearrange("p (k c) -> p k c", k=TPB),
                        v_hi[:, b, :, :], turnlo_done)
                elif kind == "s":
                    b, q = item[1:]
                    n = TPB * b + q
                    dve.wait_ge(s_ready, n + 1)
                    nc.vector.reduce_max(rmax[:, n:n + 1], s_ps[n % 2][:, :], AX_X).then_inc(max_done, 1)
                    dve.wait_ge(max_done, n + 1)
                    nc.vector.tensor_scalar(nmax[:, n:n + 1], rmax[:, n:n + 1], -ATTN_SCALE, None, ALU.mult)\
                        .then_inc(nmax_done, 1)
                elif kind == "pturn":
                    b, q = item[1:]
                    n, i = TPB * b + q, turn_no[item]
                    dve.wait_ge(exp_done, n + 1)
                    nc.vector.reciprocal(rinv[:, n:n + 1], rsum[:, n:n + 1]).then_inc(rinv_done, 1)
                    dve.wait_ge(turnhi_done, i + 1)
                    cut = slice(q * P, (q + 1) * P)
                    low(pT_lo[:, :, cut], turn_ps[i % 2][:, :].rearrange("p (k c) -> p k c", k=TPB),
                        pT_hi[:, :, cut], turnlo_done)
                elif kind == "ot":
                    b = item[1]
                    dve.wait_ge(oThi_done, b + 1)
                    low(oT_lo[:, b, :], oT_ps[:, :], oT_hi[:, b, :], oTlo_done)
                elif kind == "wo":
                    t = item[1]
                    dve.wait_ge(wo_ready, t + 1)
                    dve.wait_ge(rinv_done, t + 1)
                    dve.wait_ge(bo_added, t + 1)
                    nc.vector.scalar_tensor_tensor(rows[:, t, :], rows_ps[rows_no[item] % 3][:, :],
                                                   rinv[:, t:t + 1], rows[:, t, :], ALU.mult, ALU.add)\
                        .then_inc(res_done, 1)
                elif kind == "score":
                    t = item[1]
                    s, sc = t % 2, score_ps[:, 0:EXPERTS]
                    dve.wait_ge(score_ready, t + 1)
                    nc.vector.max(top8[:, s, 0, :], sc).then_inc(top_step, 1)
                    dve.wait_ge(top_step, 5 * t + 1)
                    if t >= 2:
                        dve.wait_ge(gexp_done, t - 1)
                    nc.vector.tensor_scalar(gmax[:, s:s + 1], top8[:, s, 0, 0:1], -1.0, None, ALU.mult)\
                        .then_inc(top_step, 1)
                    nc.vector.match_replace(left1[:, s, :], top8[:, s, 0, :], sc, TAKEN).then_inc(top_step, 1)
                    dve.wait_ge(top_step, 5 * t + 3)
                    nc.vector.max(top8[:, s, 1, :], left1[:, s, :]).then_inc(top_step, 1)
                    dve.wait_ge(top_step, 5 * t + 4)
                    nc.vector.match_replace(left2[:, s, :], top8[:, s, 1, :], left1[:, s, :], TAKEN)\
                        .then_inc(top_step, 1)
                    dve.wait_ge(top_step, 5 * t + 5)
                    dve.wait_ge(gexp_done, t + 1)
                    nc.vector.scalar_tensor_tensor(gate[:, s, :], left2[:, s, :], TAKEN, gexp[:, s, :],
                                                   ALU.is_equal, ALU.mult, accum_out=gsum[:, s:s + 1])\
                        .then_inc(gsum_done, 1)
                    dve.wait_ge(gsum_done, t + 1)
                    nc.vector.reciprocal(ginv[:, s:s + 1], gsum[:, s:s + 1]).then_inc(ginv_done, 1)
                    dve.wait_ge(ginv_done, t + 1)
                    nc.vector.tensor_scalar(gate[:, s, :], gate[:, s, :], ginv[:, s:s + 1], None, ALU.mult)\
                        .then_inc(gate_done, 1)
                elif kind == "h":
                    t, c = item[1:]
                    dve.wait_ge(gate_done, t + 1)
                    if t >= 2:
                        dve.wait_ge(turn_ready, turn_no[("hturn", t - 2, c)] + 1)
                    dve.wait_ge(hid_ready, 2 * t + c + 1)
                    g = gate[:, t % 2, c * EPC:(c + 1) * EPC].unsqueeze(2).to_broadcast([P, EPC, ERANK])
                    nc.vector.tensor_tensor(
                        hg[:, t % 2, c * 512:(c + 1) * 512].rearrange("p (e r) -> p e r", r=ERANK),
                        hid_ps[c][:, :].rearrange("p (e r) -> p e r", r=ERANK), g, ALU.mult).then_inc(hg_done, 1)
                elif kind == "hturn":
                    t, c = item[1:]
                    i = turn_no[item]
                    dve.wait_ge(turnhi_done, i + 1)
                    low(hgT_lo[:, t % 2, c * 4:(c + 1) * 4, :],
                        turn_ps[i % 2][:, :].rearrange("p (k c) -> p k c", k=4),
                        hgT_hi[:, t % 2, c * 4:(c + 1) * 4, :], turnlo_done)


def laid_out(a):
    import numpy as np

    def cat(parts):
        return np.ascontiguousarray(np.stack(parts))

    ca, cg, cd, cf = (np.asarray(a[n]) for n in ("L0_attn_codes_attn", "L0_attn_codes_gu", "L0_attn_codes_down",
                                                 "L0_ffn_codes"))
    sa, sg, sd, sf = (np.asarray(a[n]) for n in ("L0_attn_scales_attn", "L0_attn_scales_gu",
                                                 "L0_attn_scales_down", "L0_ffn_absmax"))
    codes, scales = [], []
    for kind, k in CHUNKS:
        cut, blk = slice(k * P, (k + 1) * P), slice(2 * k, 2 * k + 2)
        if kind == "o":
            codes.append(ca[3].T[cut])
            scales.append(sa[3].T[blk])
        elif kind in "qkv":
            codes.append(ca["qkv".index(kind)][cut])
        elif kind in "gu":
            g = "gu".index(kind)
            codes.append(cg[g][cut].reshape(P, KT, P).transpose(2, 1, 0).reshape(P, H))
            scales.append(sg[g][cut].reshape(P, KT, 2).transpose(2, 1, 0).reshape(2, H))
        elif kind == "d":
            codes.append(cd.T[cut])
            scales.append(sd.T[blk])
        else:
            codes.append(cf.T[cut])
            scales.append(sf.T[blk])

    def tiles(m):
        return np.ascontiguousarray(m.reshape(-1, P, m.shape[1]).transpose(1, 0, 2))

    x = np.asarray(a["L0_attn_x"]).reshape(TOK, H)
    Ah, Ad = np.asarray(a["L0_attn_lora_A_h"]), np.asarray(a["L0_attn_lora_A_down"])
    Ba, Bg, Bd = (np.asarray(a[n]) for n in ("L0_attn_lora_B_attn", "L0_attn_lora_B_gu", "L0_attn_lora_B_down"))
    zero = np.zeros((RANK, FF), np.float32)
    la_d = np.zeros((P, 512), np.float32)
    lb_d = np.zeros((P, 512), np.float32)
    for g in range(4):
        part = Ad[:, g * 512:(g + 1) * 512]
        for r in (32 * g, 32 * g + RANK):
            la_d[r:r + RANK, :part.shape[1]] = part
            lb_d[r:r + RANK] = Bd.T
    A4 = np.tile(np.concatenate([Ah[4], Ah[5]]), (4, 1))
    B4 = [np.tile(np.concatenate(rows), (4, 1)) for rows in ((Bg[0].T, zero), (zero, Bg[1].T))]
    eA, eB = np.asarray(a["L1_ffn_A"]), np.asarray(a["L1_ffn_B"])
    named = dict(
        codes=cat(codes), scales=cat(scales),
        scales_qkv=np.ascontiguousarray(sa[:3].reshape(3 * KT, P, H // QB).transpose(1, 0, 2)),
        eye=np.eye(P, dtype=np.float32),
        down_low=np.where(np.arange(P) % 32 < RANK, 0, -1).astype(np.float32)[:, None], xT=tiles(x.T),
        loA_o=Ah[3], loB_o=Ba[3].T, loA_qkv=Ah[:3].reshape(3 * RANK, H),
        loB_qkv=Ba[:3].transpose(0, 2, 1).reshape(3 * RANK, H),
        loA_gu=tiles(A4.T), loB_gu=np.stack(B4, 1), loA_d=la_d, loB_d=lb_d,
        loA_f=np.asarray(a["L0_ffn_lora_A"]), loB_f=np.asarray(a["L0_ffn_lora_B"]).T,
        w_qkv=tiles(np.asarray(a["L1_attn_Wqkv"])),
        b_qkv=np.asarray(a["L1_attn_bqkv"]).reshape(3, HD).T,
        w_o=np.asarray(a["L1_attn_Wo"]), b_o=np.asarray(a["L1_attn_bo"]).reshape(1, H),
        ex_A=tiles(eA.reshape(ER, H).T),
        ex_B=tiles(eB.transpose(0, 2, 1).reshape(ER, H)),
        w_r=tiles(np.asarray(a["L1_ffn_Wr"]).T),
    )
    return {k: np.ascontiguousarray(v) for k, v in named.items()}


def kernel(**inputs):
    import concourse.bacc as bacc
    from concourse.bass_utils import run_bass_kernel_spmd

    arrays = laid_out(inputs)
    nc = bacc.Bacc("TRN2", target_bir_lowering=False, num_devices=1)
    args = {k: nc.dram_tensor(k, v.shape, mybir.dt.from_np(v.dtype), kind="ExternalInput").ap()
            for k, v in arrays.items()}
    out = nc.dram_tensor("out", (TOK, H), F32, kind="ExternalOutput").ap()
    build(nc, out=out, **args)
    result = run_bass_kernel_spmd(nc, [arrays], core_ids=[0])
    return result.results[0]["out"].reshape(NB, SEQ, H)
```
